# Optimizing a Trainium2 kernel written in Bass

```python
import numpy as np
import jax
import jax.numpy as jnp

def _softmax(x, axis=-1):
    return jax.nn.softmax(x, axis=axis)

def _gelu(x):
    return jax.nn.gelu(x, approximate=True)

def _silu(x):
    return jax.nn.silu(x)

def _sigmoid(x):
    return jax.nn.sigmoid(x)

def _layernorm(x, axis=-1, eps=1e-05):
    m = jnp.mean(x, axis=axis, keepdims=True)
    v = jnp.var(x, axis=axis, keepdims=True)
    return (x - m) / jnp.sqrt(v + eps)

def _scatter_add(tgt, idx, src, axis=0):
    return tgt.at[idx].add(src)

def _segment_sum(src, seg, n):
    return jax.ops.segment_sum(src, seg, n)
kernel_name = 'mk_gnn_preln_d4_gnn_r64_c92c9f'

def setup_inputs(seed: int=0):
    np.random.seed(seed)
    _w = jnp.asarray

    def _rec_inputs():
        import jax
        import jax.numpy as jnp
        _gk = jax.random.key(seed)
        x = -8.776e-05 + 1 * jax.random.normal(jax.random.fold_in(_gk, 1), (20000, 256), jnp.float32)
        src = jax.random.randint(jax.random.fold_in(_gk, 2), (5000,), 0, 20000, jnp.int32)
        dst = jax.random.randint(jax.random.fold_in(_gk, 3), (5000,), 0, 20000, jnp.int32)
        _o = jnp.argsort(dst, stable=True)
        src = src[_o]
        dst = dst[_o]
        edge_attr_2 = jax.random.uniform(jax.random.fold_in(_gk, 12), (5000, 2), jnp.float32, 0.0, 1)
        edge_attr_256 = -8.513e-05 + 0.999844 * jax.random.normal(jax.random.fold_in(_gk, 13), (5000, 256), jnp.float32)
        edge_attr_3 = -1.09012e-05 + 0.99985 * jax.random.normal(jax.random.fold_in(_gk, 14), (5000, 3), jnp.float32)
        edge_type_11 = jax.random.randint(jax.random.fold_in(_gk, 16), (5000,), 0, 11, jnp.int32)
        return (x, src, dst, edge_attr_2, edge_attr_256, edge_attr_3, edge_type_11)
    x, src, dst, edge_attr_2, edge_attr_256, edge_attr_3, edge_type_11 = _rec_inputs()

    def _L0_gnn_setup():
        import jax, jax.numpy as jnp
        import numpy as np
        N_NODES = 20000
        N_EDGES = 5000
        IN_F = 256
        OUT_F = 256
        EDGE_F = 256

        def _mlp2(x, W1, b1, W2, b2):
            return jax.nn.relu(x @ W1 + b1) @ W2 + b2
        key = jax.random.key(seed)
        ks = jax.random.split(key, 12)

        def lin(k, fan_in, shape):
            bound = 1.0 / np.sqrt(fan_in)
            return jax.random.uniform(k, shape, jnp.float32, -bound, bound)
        node_feat = jax.random.normal(ks[0], (N_NODES, IN_F), jnp.float32)
        edge_feat = jax.random.normal(ks[1], (N_EDGES, EDGE_F), jnp.float32)
        src = jax.random.randint(ks[2], (N_EDGES,), 0, N_NODES, jnp.int32)
        dst = jax.random.randint(ks[3], (N_EDGES,), 0, N_NODES, jnp.int32)
        We1 = lin(ks[4], EDGE_F, (EDGE_F, 2 * EDGE_F))
        be1 = lin(ks[5], EDGE_F, (2 * EDGE_F,))
        We2 = lin(ks[6], 2 * EDGE_F, (2 * EDGE_F, IN_F))
        be2 = lin(ks[7], 2 * EDGE_F, (IN_F,))
        Wn1 = lin(ks[8], IN_F, (IN_F, 2 * IN_F))
        bn1 = lin(ks[9], IN_F, (2 * IN_F,))
        Wn2 = lin(ks[10], 2 * IN_F, (2 * IN_F, OUT_F))
        bn2 = lin(ks[11], 2 * IN_F, (OUT_F,))
        eps = jnp.zeros((1,), jnp.float32)
        return {'node_feat': node_feat, 'edge_feat': edge_feat, 'src': src, 'dst': dst, 'We1': We1, 'be1': be1, 'We2': We2, 'be2': be2, 'Wn1': Wn1, 'bn1': bn1, 'Wn2': Wn2, 'bn2': bn2, 'eps': eps}
    _L0_gnn_all = _L0_gnn_setup()
    _L0_gnn_in = {k: v for k, v in _L0_gnn_all.items() if k in ('We1', 'be1', 'We2', 'be2', 'Wn1', 'bn1', 'Wn2', 'bn2', 'eps')}
    del _L0_gnn_all

    def _L1_gnn_setup():
        import jax, jax.numpy as jnp
        import numpy as np
        N = 100000
        E = 50000
        D_IN = 256
        D_OUT = 256
        NUM_REL = 10
        key = jax.random.key(seed)
        k1, k2, k3, k4, k5, k6 = jax.random.split(key, 6)
        x = jax.random.normal(k1, (N, D_IN), dtype=jnp.float32)
        edge_index = jax.random.randint(k2, (2, E), 0, N, dtype=jnp.int64)
        rel = jax.random.randint(k3, (E,), 0, NUM_REL + 1, dtype=jnp.int64)
        stdv = 1.0 / np.sqrt(D_OUT)
        weight = jax.random.uniform(k4, (D_IN, D_OUT), dtype=jnp.float32, minval=-stdv, maxval=stdv)
        bias = jax.random.uniform(k5, (D_OUT,), dtype=jnp.float32, minval=-stdv, maxval=stdv)
        alpha = jax.random.normal(k6, (NUM_REL + 1, 1), dtype=jnp.float32)
        alpha = alpha.at[0].set(0.0)
        return {'x': x, 'edge_index': edge_index, 'rel': rel, 'weight': weight, 'bias': bias, 'alpha': alpha}
    _L1_gnn_all = _L1_gnn_setup()
    _L1_gnn_in = {k: v for k, v in _L1_gnn_all.items() if k in ('weight', 'bias', 'alpha')}
    del _L1_gnn_all

    def _L2_gnn_setup():
        import jax, jax.numpy as jnp
        import numpy as np
        N = 50000
        E = 6250
        IN = 256
        H = 8
        D = 32
        EF = 3
        key = jax.random.key(seed)
        ks = jax.random.split(key, 8)
        x = jax.random.normal(ks[0], (N, IN), dtype=jnp.float32)
        edge_index = jax.random.randint(ks[1], (2, E), 0, N, dtype=jnp.int64)
        edge_attr = jax.random.normal(ks[2], (E, EF), dtype=jnp.float32)
        W = jax.random.normal(ks[3], (H * D, IN), dtype=jnp.float32) * np.float32(np.sqrt(2.0 / (IN + H * D)))
        a_src = jax.random.normal(ks[4], (H, D), dtype=jnp.float32) * np.float32(np.sqrt(2.0 / (H + D)))
        a_dst = jax.random.normal(ks[5], (H, D), dtype=jnp.float32) * np.float32(np.sqrt(2.0 / (H + D)))
        edge_W = jax.random.normal(ks[6], (H * D, EF), dtype=jnp.float32) * np.float32(np.sqrt(2.0 / (EF + H * D)))
        edge_b = jnp.zeros((H * D,), dtype=jnp.float32)
        bias = jnp.zeros((H * D,), dtype=jnp.float32)
        return {'x': x, 'W': W, 'a_src': a_src, 'a_dst': a_dst, 'edge_W': edge_W, 'edge_b': edge_b, 'bias': bias, 'edge_attr': edge_attr, 'edge_index': edge_index}
    _L2_gnn_all = _L2_gnn_setup()
    _L2_gnn_in = {k: v for k, v in _L2_gnn_all.items() if k in ('W', 'a_src', 'a_dst', 'edge_W', 'edge_b', 'bias')}
    del _L2_gnn_all

    def _L3_gnn_setup():
        import jax, jax.numpy as jnp
        import numpy as np
        N_NODES = 100000
        N_EDGES = 25000
        IN_FEATS = 256
        OUT_FEATS = 64
        NUM_HEADS = 4
        key = jax.random.key(seed)
        k_h, k_adj, k_dir, k_wf, k_wr, k_af = jax.random.split(key, 6)
        h = jax.random.normal(k_h, (N_NODES, IN_FEATS), dtype=jnp.float32)
        adj = jax.random.randint(k_adj, (2, N_EDGES), 0, N_NODES, dtype=jnp.int64)
        bit = jax.random.randint(k_dir, (N_EDGES,), 0, 2).astype(jnp.float32)
        direction = jnp.stack([bit, 1.0 - bit], axis=1)
        s_w = float(np.sqrt(6.0 / (IN_FEATS + OUT_FEATS)))
        s_a = float(np.sqrt(6.0 / (NUM_HEADS + OUT_FEATS)))
        W_forward = jax.random.uniform(k_wf, (OUT_FEATS, IN_FEATS), jnp.float32, -s_w, s_w)
        W_reverse = jax.random.uniform(k_wr, (OUT_FEATS, IN_FEATS), jnp.float32, -s_w, s_w)
        attn_forward = jax.random.uniform(k_af, (1, NUM_HEADS, OUT_FEATS), jnp.float32, -s_a, s_a)
        return {'h': h, 'adj': adj, 'direction': direction, 'W_forward': W_forward, 'W_reverse': W_reverse, 'attn_forward': attn_forward}
    _L3_gnn_all = _L3_gnn_setup()
    _L3_gnn_in = {k: v for k, v in _L3_gnn_all.items() if k in ('W_forward', 'W_reverse', 'attn_forward')}
    del _L3_gnn_all
    return {'x': x, 'src': src, 'dst': dst, 'edge_attr_2': edge_attr_2, 'edge_attr_256': edge_attr_256, 'edge_attr_3': edge_attr_3, 'edge_type_11': edge_type_11, 'L0_gnn_We1': _L0_gnn_in['We1'], 'L0_gnn_be1': _L0_gnn_in['be1'], 'L0_gnn_We2': _L0_gnn_in['We2'], 'L0_gnn_be2': _L0_gnn_in['be2'], 'L0_gnn_Wn1': _L0_gnn_in['Wn1'], 'L0_gnn_bn1': _L0_gnn_in['bn1'], 'L0_gnn_Wn2': _L0_gnn_in['Wn2'], 'L0_gnn_bn2': _L0_gnn_in['bn2'], 'L0_gnn_eps': _L0_gnn_in['eps'], 'L1_gnn_weight': _L1_gnn_in['weight'], 'L1_gnn_bias': _L1_gnn_in['bias'], 'L1_gnn_alpha': _L1_gnn_in['alpha'], 'L2_gnn_W': _L2_gnn_in['W'], 'L2_gnn_a_src': _L2_gnn_in['a_src'], 'L2_gnn_a_dst': _L2_gnn_in['a_dst'], 'L2_gnn_edge_W': _L2_gnn_in['edge_W'], 'L2_gnn_edge_b': _L2_gnn_in['edge_b'], 'L2_gnn_bias': _L2_gnn_in['bias'], 'L3_gnn_W_forward': _L3_gnn_in['W_forward'], 'L3_gnn_W_reverse': _L3_gnn_in['W_reverse'], 'L3_gnn_attn_forward': _L3_gnn_in['attn_forward']}

def reference(x, src, dst, edge_attr_2, edge_attr_256, edge_attr_3, edge_type_11, L0_gnn_We1, L0_gnn_be1, L0_gnn_We2, L0_gnn_be2, L0_gnn_Wn1, L0_gnn_bn1, L0_gnn_Wn2, L0_gnn_bn2, L0_gnn_eps, L1_gnn_weight, L1_gnn_bias, L1_gnn_alpha, L2_gnn_W, L2_gnn_a_src, L2_gnn_a_dst, L2_gnn_edge_W, L2_gnn_edge_b, L2_gnn_bias, L3_gnn_W_forward, L3_gnn_W_reverse, L3_gnn_attn_forward):
    import jax
    import jax.numpy as jnp

    def _L0_gnn_ref(node_feat, edge_feat, src, dst, We1, be1, We2, be2, Wn1, bn1, Wn2, bn2, eps):
        import jax, jax.numpy as jnp
        import numpy as np
        N_NODES = 20000
        N_EDGES = 5000
        IN_F = 256
        OUT_F = 256
        EDGE_F = 256

        def _mlp2(x, W1, b1, W2, b2):
            return jax.nn.relu(x @ W1 + b1) @ W2 + b2
        e = _mlp2(edge_feat, We1, be1, We2, be2)
        msg = jax.nn.relu(node_feat[src] + e)
        out_h = jax.ops.segment_sum(msg, dst, num_segments=N_NODES)
        out = _mlp2((1.0 + eps[0]) * node_feat + out_h, Wn1, bn1, Wn2, bn2)
        return out

    def _L1_gnn_ref(x, edge_index, rel, weight, bias, alpha):
        import jax, jax.numpy as jnp
        import numpy as np
        N = 100000
        E = 50000
        D_IN = 256
        D_OUT = 256
        NUM_REL = 10
        w = alpha[rel, 0]
        support = x @ weight
        row, col = (edge_index[0], edge_index[1])
        out = jax.ops.segment_sum(w[:, None] * support[col], row, num_segments=x.shape[0])
        out = out + jax.ops.segment_sum(w[:, None] * support[row], col, num_segments=x.shape[0])
        return out + bias

    def _L2_gnn_ref(x, W, a_src, a_dst, edge_W, edge_b, bias, edge_attr, edge_index):
        import jax, jax.numpy as jnp
        import numpy as np
        N = 50000
        E = 6250
        IN = 256
        H = 8
        D = 32
        EF = 3
        n = x.shape[0]
        h = (x @ W.T).reshape(n, H, D)
        src, dst = (edge_index[0], edge_index[1])
        h_src = h[src]
        h_dst = h[dst]
        alpha = jnp.einsum('ehd,hd->eh', h_src, a_src) + jnp.einsum('ehd,hd->eh', h_dst, a_dst)
        enc = jax.nn.relu(edge_attr @ edge_W.T + edge_b).reshape(-1, H, D)
        alpha = alpha + jnp.sum(enc * h_dst, axis=-1)
        alpha = jnp.where(alpha >= 0, alpha, 0.2 * alpha)
        amax = jax.ops.segment_max(alpha, dst, num_segments=n)
        ex = jnp.exp(alpha - amax[dst])
        denom = jax.ops.segment_sum(ex, dst, num_segments=n)
        attn = ex / jnp.maximum(denom[dst], 1e-10)
        out = jax.ops.segment_sum(h_src * attn[..., None], dst, num_segments=n)
        return out.reshape(n, H * D) + bias

    def _L3_gnn_ref(h, adj, direction, W_forward, W_reverse, attn_forward):
        import jax, jax.numpy as jnp
        import numpy as np
        N_NODES = 100000
        N_EDGES = 25000
        IN_FEATS = 256
        OUT_FEATS = 64
        NUM_HEADS = 4
        N = h.shape[0]
        H = attn_forward.shape[1]
        h_fwd = h @ W_forward.T
        h_rev = h @ W_reverse.T
        src, dst = (adj[0], adj[1])
        messages = h_fwd[src] * direction[:, 0:1] + h_rev[src] * direction[:, 1:2]
        scores = jnp.einsum('ef,hf->eh', messages, attn_forward[0])
        scores = jax.nn.leaky_relu(scores, negative_slope=0.2)
        exp_scores = jnp.exp(scores - scores.max(axis=0, keepdims=True))
        sum_exp = jax.ops.segment_sum(exp_scores, dst, num_segments=N)
        norm = exp_scores / (sum_exp[dst] + 1e-10)
        outs = [jax.ops.segment_sum(messages * norm[:, hd:hd + 1], dst, num_segments=N) for hd in range(H)]
        out = jnp.stack(outs, axis=1)
        return out.reshape(N, -1)
    edge_index = jnp.stack([src, dst])
    h = jnp.maximum(_layernorm(x, axis=-1), 0.0)
    x = x + _L0_gnn_ref(h, edge_attr_256, src, dst, L0_gnn_We1, L0_gnn_be1, L0_gnn_We2, L0_gnn_be2, L0_gnn_Wn1, L0_gnn_bn1, L0_gnn_Wn2, L0_gnn_bn2, L0_gnn_eps)
    h = jnp.maximum(_layernorm(x, axis=-1), 0.0)
    x = x + _L1_gnn_ref(h, edge_index, edge_type_11, L1_gnn_weight, L1_gnn_bias, L1_gnn_alpha)
    h = jnp.maximum(_layernorm(x, axis=-1), 0.0)
    x = x + _L2_gnn_ref(h, L2_gnn_W, L2_gnn_a_src, L2_gnn_a_dst, L2_gnn_edge_W, L2_gnn_edge_b, L2_gnn_bias, edge_attr_3, edge_index)
    h = jnp.maximum(_layernorm(x, axis=-1), 0.0)
    x = x + _L3_gnn_ref(h, edge_index, edge_attr_2, L3_gnn_W_forward, L3_gnn_W_reverse, L3_gnn_attn_forward)
    return x

_drawn_inputs = setup_inputs


def setup_inputs(seed=0):
    import zlib

    import numpy as np

    out = dict(_drawn_inputs(seed))
    spreads = {'L2_gnn_edge_b': (0.0, 2.0), 'L2_gnn_bias': (0.0, 0.1)}
    factors = {'edge_attr_256': 2.951,
     'edge_attr_3': 4.8,
     'L0_gnn_We1': 2.948,
     'L0_gnn_be1': 40.451,
     'L0_gnn_be2': 22.073,
     'L0_gnn_bn1': 4.231,
     'L2_gnn_a_src': 8.807,
     'L2_gnn_a_dst': 63.614,
     'L2_gnn_edge_W': 5.101}
    for name, (base, spread) in spreads.items():
        noise = np.random.default_rng([zlib.crc32(name.encode()), seed]).standard_normal(out[name].shape)
        drawn = base * np.exp(spread * noise) if base else spread * noise
        out[name] = jnp.asarray(drawn.astype(out[name].dtype))
    for name, factor in factors.items():
        out[name] = (out[name] * factor).astype(out[name].dtype)
    return out
```

```python
from contextlib import ExitStack, contextmanager

import concourse.bass as bass
from concourse import mybir

F32 = mybir.dt.float32
BF16 = mybir.dt.bfloat16
I32 = mybir.dt.int32
ALU = mybir.AluOpType
ACT = mybir.ActivationFunctionType
AX = mybir.AxisListType
IOA = bass.IndirectOffsetOnAxis

P = 128
D = 256
DC = D // P
HID = 512
HC = HID // P
TE = 125
G = 4
GE = G * TE
LO = 256
EPS = 1e-5
SKIP = 1 << 15
NEG = -1.0e38

RD = 16
D_SRC, D_PUT, D_SLOT_S, D_SLOT_D, D_EDGE, D_SAME, D_A2, D_A3, D_ONE = 0, 1, 2, 3, 4, 5, 6, 8, 11
RC = 8
C_NODE, C_PEER, C_PUT, C_W, C_SAME = 0, 1, 2, 3, 4


@contextmanager
def signals(nc, stage):
    taken = []

    def sem(what):
        taken.append(nc.alloc_semaphore(f"{stage}_{what}"))
        return taken[-1]

    yield sem
    nc.clear_and_free_semaphores(taken)
    nc.all_engine_barrier()


def constants(nc, K):
    with ExitStack() as ctx:
        sem = ctx.enter_context(signals(nc, "const"))
        filled = sem("filled")
        done = sem("done")
        block = ctx.enter_context(nc.Block())

        @block.gpsimd
        def _(pool):
            pool.memset(K["ident"][:, :], 0.0).then_inc(filled, 1)
            pool.wait_ge(filled, 1)
            pool.affine_select(out=K["ident"][:, :], in_=K["ident"][:, :], compare_op=ALU.not_equal, fill=1.0,
                               base=0, pattern=[[-1, P]], channel_multiplier=1).then_inc(done, 1)
            pool.iota(K["iota_p"][:, :], [[0, 1]], base=0, channel_multiplier=1,
                      allow_small_or_imprecise_dtypes=True).then_inc(done, 1)
            pool.memset(K["eps"][:, :], EPS).then_inc(done, 1)
            pool.wait_ge(done, 3)


def rank_edges(nc, K, dst, src, table, zero_table):
    E = dst.shape[0]
    NT = E // TE
    NH = table.shape[0] // LO
    S = 2
    with ExitStack() as ctx:
        def sb(name, shape, dt=F32):
            return ctx.enter_context(nc.sbuf_tensor(name, shape, dt))

        def pb(name, shape, dt=F32):
            return ctx.enter_context(nc.psum_tensor(name, shape, dt))

        sem = ctx.enter_context(signals(nc, "rk"))
        key_row = [sb(f"rk_key_row{s}", [P, E], I32) for s in range(S)]
        hi_row = [sb(f"rk_hi_row{s}", [NH, E], I32) for s in range(S)]
        key40 = sb("rk_key40", [NT, S, TE], I32)
        part40 = sb("rk_part40", [NT, 2, S, TE], I32)
        key_f = sb("rk_key_f", [NT, 3, S, TE])
        key_col = sb("rk_key_col", [TE, 3, S, NT])
        iota_hi = sb("rk_iota_hi", [P, NH], BF16)
        iota_lo = sb("rk_iota_lo", [P, LO], BF16)
        before = sb("rk_before", [TE, TE])
        above = sb("rk_above", [NH, NH])
        ones = sb("rk_ones", [NH, LO])
        zero_b = sb("rk_zero_b", [P, LO], BF16)
        hot_hi = sb("rk_hot_hi", [TE, 8, NH], BF16)
        hot_lo = sb("rk_hot_lo", [TE, 8, LO], BF16)
        hot_hi_t = sb("rk_hot_hi_t", [NH, 8, TE])
        run = sb("rk_run", [NH, 4, LO])
        junk_t = sb("rk_junk_t", [TE, 8, TE])
        junk_r = sb("rk_junk_r", [TE, 8, LO])
        in_tile = sb("rk_in_tile", [TE, 8])
        in_run = sb("rk_in_run", [TE, 8])
        hist = sb("rk_hist", [NH, S, LO])
        incl = sb("rk_incl", [NH, S, LO])
        total = sb("rk_total", [NH, S])
        carry = sb("rk_carry", [NH, S])
        tab = sb("rk_tab", [NH, LO, 4])
        NZ = 25
        zeros = sb("rk_zeros", [80, NZ * D])
        p_hist = [pb(f"rk_p_hist{s}", [NH, 512]) for s in range(S)]
        p_look = [pb(f"rk_p_look{m}", [TE, 512]) for m in range(4)]
        p_misc = pb("rk_p_misc", [P, 512])

        row_in = [sem(f"row_in{s}") for s in range(S)]
        key_in = sem("key_in")
        const_a = sem("const_a")
        const_ready = sem("const_ready")
        zeros_ready = sem("zeros_ready")
        step = sem("step")
        keys_split = sem("keys_split")
        keys_turned = sem("keys_turned")
        hist_zero = sem("hist_zero")
        hots_ready = sem("hots_ready")
        run_ready = sem("run_ready")
        looked_up = sem("looked_up")
        look_read = sem("look_read")
        hist_added = sem("hist_added")
        counted = sem("counted")
        totals_ready = sem("totals_ready")
        carry_ready = sem("carry_ready")
        tab_ready = sem("tab_ready")
        stored = sem("stored")
        block = ctx.enter_context(nc.Block())
        keys = (dst, src)

        @block.sync
        def _(sp):
            for s in range(S):
                sp.dma_start(key40[:, s, :], keys[s].rearrange("(t p) -> t p", p=TE)).then_inc(key_in, 16)
            for s in range(S):
                sp.dma_start(key_row[s][:, :], keys[s].rearrange("(a e) -> a e", a=1).to_broadcast([P, E])) \
                    .then_inc(row_in[s], 16)
            sp.wait_ge(zeros_ready, 1)
            rows = zero_table.rearrange("(p r) d -> p (r d)", p=80)
            NR = zero_table.shape[0] // 80 // NZ
            for r in range(NR):
                sp.dma_start(rows[:, r * NZ * D:(r + 1) * NZ * D], zeros[:, :]).then_inc(stored, 16)
            sp.wait_ge(tab_ready, 1)
            sp.dma_start(table.rearrange("(h l) c -> h (l c)", l=LO),
                         tab[:, :, :].rearrange("h l c -> h (l c)")).then_inc(stored, 16)
            sp.wait_ge(stored, 16 * (NR + 1))

        @block.gpsimd
        def _(pool):
            pool.memset(zeros[:, :], 0.0).then_inc(zeros_ready, 1)
            pool.memset(K["src_col"][:, NT:], 0)
            pool.memset(K["dst_col"][:, NT:], 0)
            pool.iota(iota_hi[:, :], [[1, NH]], base=0, channel_multiplier=0,
                      allow_small_or_imprecise_dtypes=True).then_inc(const_ready, 1)
            pool.iota(iota_lo[:, :], [[1, LO]], base=0, channel_multiplier=0,
                      allow_small_or_imprecise_dtypes=True).then_inc(const_ready, 1)
            pool.memset(before[:, :], 1.0).then_inc(const_a, 1)
            pool.memset(above[:, :], 1.0).then_inc(const_a, 1)
            pool.memset(ones[:, :], 1.0).then_inc(const_ready, 1)
            pool.memset(zero_b[:, :], 0.0).then_inc(const_ready, 1)
            pool.wait_ge(const_a, 2)
            pool.affine_select(out=before[:, :], in_=before[:, :], compare_op=ALU.is_gt, fill=0.0,
                               base=0, pattern=[[-1, TE]], channel_multiplier=1).then_inc(const_ready, 1)
            pool.affine_select(out=above[:, :], in_=above[:, :], compare_op=ALU.is_gt, fill=0.0,
                               base=0, pattern=[[1, NH]], channel_multiplier=-1).then_inc(const_ready, 1)

        @block.vector
        def _(dve):
            dve.wait_ge(key_in, 16 * S)
            dve.tensor_scalar(part40[:, 0, :, :], key40[:, :, :], 8, None, ALU.logical_shift_right)
            dve.tensor_scalar(part40[:, 1, :, :], key40[:, :, :], LO - 1, None, ALU.bitwise_and).then_inc(step, 1)
            dve.tensor_copy(key_f[:, 0, :, :], key40[:, :, :])
            dve.wait_ge(step, 1)
            dve.tensor_copy(key_f[:, 1:3, :, :].rearrange("t a s e -> t (a s e)"),
                            part40[:, :, :, :].rearrange("t a s e -> t (a s e)")).then_inc(keys_split, 1)
            dve.wait_ge(keys_turned, 1)
            dve.tensor_copy(key_col[:, :, :, :].rearrange("p a s t -> p (a s t)"),
                            p_misc[0:TE, 0:3 * S * NT]).then_inc(step, 1)
            dve.tensor_copy(K["dst_col"][:, 0:NT], p_misc[0:TE, 0:NT])
            dve.tensor_copy(K["src_col"][:, 0:NT], p_misc[0:TE, NT:2 * NT])
            for s in range(S):
                dve.wait_ge(row_in[s], 16)
                dve.tensor_scalar(hi_row[s][:, :], key_row[s][0:NH, :], 8, None,
                                  ALU.logical_shift_right).then_inc(step, 1)
            dve.wait_ge(step, 4)
            dve.wait_ge(const_ready, 6)
            dve.sem_inc(look_read, 4)
            dve.sem_inc(hist_added, 8)
            with dve.Fori(0, NT // G) as i:
                for m in range(8):
                    j, s = m // 2, m % 2
                    t = i * G + j
                    dve.wait_ge(hist_added, i * 8 + m + 1)
                    dve.tensor_scalar(hot_hi[:, m, :], iota_hi[0:TE, :], key_col[:, 1, s, bass.ds(t, 1)], None,
                                      ALU.is_equal)
                    dve.tensor_scalar(hot_lo[:, m, :], iota_lo[0:TE, :], key_col[:, 2, s, bass.ds(t, 1)], None,
                                      ALU.is_equal)
                    dve.tensor_scalar(hot_hi_t[:, m, :], hi_row[s][:, bass.ds(t * TE, TE)], K["iota_p"][0:NH, 0:1],
                                      None, ALU.is_equal).then_inc(hots_ready, 1)
                    dve.scalar_tensor_tensor(out=junk_t[:, m, :], in0=key_row[s][0:TE, bass.ds(t * TE, TE)],
                                             scalar=key_col[:, 0, s, bass.ds(t, 1)], in1=before[:, :],
                                             op0=ALU.is_equal, op1=ALU.mult, accum_out=in_tile[:, m:m + 1])
                for m in range(8):
                    dve.wait_ge(looked_up, i * 8 + m + 1)
                    ins = dve.scalar_tensor_tensor(out=junk_r[:, m, :], in0=p_look[m % 4][:, 0:LO], scalar=1.0,
                                                   in1=hot_lo[:, m, :], op0=ALU.mult, op1=ALU.mult,
                                                   accum_out=in_run[:, m:m + 1])
                    ins.then_inc(look_read, 1)
                dve.wait_ge(look_read, i * 8 + 12)
                dve.tensor_tensor(K["ord"][:, bass.ds(i * G, G), :].rearrange("p t s -> p (t s)"), in_tile[:, :],
                                  in_run[:, :], ALU.add).then_inc(counted, 1)
                dve.wait_ge(counted, i + 1)
            dve.wait_ge(hist_added, 2 * NT + 8)
            for s in range(S):
                dve.tensor_copy(hist[:, s, :], p_hist[s][:, 0:LO]).then_inc(step, 1)
            dve.wait_ge(step, 6)
            for s in range(S):
                dve.tensor_tensor_scan(incl[:, s, :], ones[:, :], hist[:, s, :], 0.0, ALU.mult, ALU.add) \
                   .then_inc(step, 1)
            dve.wait_ge(step, 8)
            dve.tensor_copy(total[:, :], incl[:, :, LO - 1]).then_inc(totals_ready, 1)
            dve.wait_ge(carry_ready, 1)
            dve.tensor_copy(carry[:, :], p_misc[0:NH, 0:S]).then_inc(step, 1)
            dve.wait_ge(step, 9)
            for s in range(S):
                dve.tensor_scalar(tab[:, :, 2 * s + 1], incl[:, s, :], carry[:, s:s + 1], None, ALU.add) \
                   .then_inc(step, 1)
            dve.wait_ge(step, 11)
            dve.tensor_tensor(tab[:, :, 0], tab[:, :, 1], hist[:, 0, :], ALU.subtract)
            dve.tensor_tensor(tab[:, :, 2], tab[:, :, 3], hist[:, 1, :], ALU.subtract).then_inc(tab_ready, 1)

        @block.scalar
        def _(act):
            act.wait_ge(hist_zero, 1)
            with act.Fori(0, NT // G) as i:
                for m in range(8):
                    act.wait_ge(hist_added, i * 8 + m + 7)
                    act.copy(run[:, m % 4, :], p_hist[m % 2][:, 0:LO]).then_inc(run_ready, 1)

        @block.tensor
        def _(pe):
            pe.wait_ge(keys_split, 1)
            for a in range(3):
                for s in range(S):
                    c = (a * S + s) * NT
                    mm = pe.transpose(p_misc[0:TE, c:c + NT], key_f[:, a, s, :], K["ident"][0:NT, 0:NT])
            mm.then_inc(keys_turned, 1)
            pe.wait_ge(const_ready, 6)
            for s in range(S):
                mm = pe.matmul(p_hist[s][:, 0:LO], zero_b[:, 0:NH], zero_b[:, :], start=True, stop=False,
                               skip_group_check=True)
            mm.then_inc(hist_zero, 1)
            with pe.Fori(0, NT // G) as i:
                for m in range(8):
                    s = m % 2
                    pe.wait_ge(hots_ready, i * 8 + m + 1)
                    pe.wait_ge(run_ready, i * 8 + m + 1)
                    pe.wait_ge(look_read, i * 8 + m + 1)
                    pe.matmul(p_look[m % 4][:, 0:LO], hot_hi_t[:, m, :], run[:, m % 4, :], start=True, stop=True) \
                      .then_inc(looked_up, 1)
                    pe.matmul(p_hist[s][:, 0:LO], hot_hi[:, m, :], hot_lo[:, m, :], start=False, stop=False,
                              skip_group_check=True).then_inc(hist_added, 1)
            pe.wait_ge(totals_ready, 1)
            pe.matmul(p_misc[0:NH, 0:S], above[:, :], total[:, :], start=True, stop=True).then_inc(carry_ready, 1)


def rows_of(dram, g, n, p):
    return dram[bass.ds(g * (n * p), n * p), :].rearrange("(j p) d -> p j d", p=p)


def open_slot(pool, K, sem, count):
    K["token_n"] += 1
    n = K["token_n"]
    pool.dma_start(K["token"][0:1, n, :], K["ident"][0:1, 0:4]).then_inc(sem, count)


class Norm:

    def __init__(self, nc, ctx, name, sem, rows, n, eps):
        def sb(what, shape):
            return ctx.enter_context(nc.sbuf_tensor(f"{name}_{what}", shape, F32))

        self.rows, self.n, self.eps = rows, n, eps
        self.stats = sb("stats", [rows, 2, n, 6])
        self.mean_var = sb("mean_var", [rows, 2, n, 2])
        self.std = sb("std", [rows, 2, n])
        self.rstd = sb("rstd", [rows, 2, n])
        self.shift = sb("shift", [rows, 2, n])
        self.stats_done = sem("stats_done")
        self.passed = sem("stats_passed")
        self.var_ready = sem("var_ready")
        self.std_ready = sem("std_ready")
        self.rstd_done = sem("rstd_done")
        self.shift_ready = sem("shift_ready")

    def statistics(self, dve, g, b, x):
        for j in range(self.n):
            ins = dve.bn_stats(self.stats[:, b, j, :], x[:, j, :])
        ins.then_inc(self.stats_done, 1)
        dve.wait_ge(self.stats_done, g + 1)
        dve.sem_inc(self.passed, 1)
        for j in range(self.n):
            ins = dve.bn_aggr(self.mean_var[:, b, j, :], self.stats[:, b, j, :])
        ins.then_inc(self.var_ready, 1)

    def root(self, act, g, b):
        act.wait_ge(self.var_ready, g + 1)
        act.activation(self.std[:, b, :], self.mean_var[:, b, :, 1], ACT.Sqrt, bias=self.eps[0:self.rows, 0:1],
                       scale=1.0).then_inc(self.std_ready, 1)

    def scales(self, dve, g, b):
        dve.wait_ge(self.std_ready, g + 1)
        dve.reciprocal(self.rstd[:, b, :], self.std[:, b, :]).then_inc(self.rstd_done, 1)
        dve.wait_ge(self.rstd_done, g + 1)
        dve.scalar_tensor_tensor(out=self.shift[:, b, :], in0=self.mean_var[:, b, :, 0], scalar=-1.0,
                                 in1=self.rstd[:, b, :], op0=ALU.mult, op1=ALU.mult).then_inc(self.shift_ready, 1)

    def rows_out(self, act, g, b, h, x):
        act.wait_ge(self.shift_ready, g + 1)
        for j in range(self.n):
            ins = act.activation(h[:, j, :], x[:, j, :], ACT.Relu, bias=self.shift[:, b, j:j + 1],
                                 scale=self.rstd[:, b, j:j + 1])
        return ins


def build_records(nc, K, A, table, rec_d, rec_c):
    N = A["x"].shape[0]
    E = A["src"].shape[0]
    NT = E // TE
    NG = NT // G
    NREL = A["L1_gnn_alpha"].shape[0]
    W = RD + 2 * RC + 4
    RANK_D, RANK_CD, RANK_CS = RD + 2 * RC, RD + 2 * RC + 1, RD + 2 * RC + 2
    with ExitStack() as ctx:
        def sb(name, shape, dt=F32):
            return ctx.enter_context(nc.sbuf_tensor(name, shape, dt))

        sem = ctx.enter_context(signals(nc, "rc"))
        idx = sb("rc_idx", [TE, 2, 2, G], I32)
        got = sb("rc_got", [TE, 2, 2, G, 4])
        tab = sb("rc_tab", [TE, 2, NT, 4])
        node = sb("rc_node", [TE, 2, NT])
        rec = sb("rc_rec", [TE, NT, W])
        part = sb("rc_part", [TE, 12, NT])
        a2_40 = sb("rc_a2_40", [NT, TE, 2])
        a3_40 = sb("rc_a3_40", [NT, TE, 3])
        type_i = sb("rc_type_i", [NT, TE], I32)
        type_40 = sb("rc_type_40", [NT, TE])
        type_c = sb("rc_type_c", [TE, NT])
        alpha = sb("rc_alpha", [TE, NREL])
        pick = sb("rc_pick", [TE, 2, NT])
        rec_out = sb("rc_rec_out", [TE, 2, G, W])
        put_idx = sb("rc_put_idx", [TE, 2, G, 3], I32)
        p_cols = ctx.enter_context(nc.psum_tensor("rc_p_cols", [TE, 512], F32))

        small_in = sem("small_in")
        types_ready = sem("types_ready")
        cols_ready = sem("cols_ready")
        rec_cleared = sem("rec_cleared")
        idx_ready = sem("idx_ready")
        got_in = [sem(f"got_in{b}") for b in range(2)]
        got_read = sem("got_read")
        step = sem("step")
        out_ready = sem("out_ready")
        put = [sem(f"put{b}") for b in range(2)]
        passed = sem("passed")
        block = ctx.enter_context(nc.Block())

        @block.sync
        def _(sp):
            sp.dma_start(a2_40[:, :, :].rearrange("t e c -> t (e c)"),
                         A["edge_attr_2"].rearrange("(t e) c -> t (e c)", e=TE)).then_inc(small_in, 16)
            sp.dma_start(a3_40[:, :, :].rearrange("t e c -> t (e c)"),
                         A["edge_attr_3"].rearrange("(t e) c -> t (e c)", e=TE)).then_inc(small_in, 16)
            sp.dma_start(type_i[:, :], A["edge_type_11"].rearrange("(t e) -> t e", e=TE)).then_inc(small_in, 16)
            sp.dma_start(alpha[:, :], A["L1_gnn_alpha"].rearrange("r a -> a r").to_broadcast([TE, NREL])) \
                .then_inc(small_in, 16)

        @block.tensor
        def _(pe):
            pe.wait_ge(types_ready, 1)
            for c in range(2):
                pe.transpose(p_cols[:, c * NT:(c + 1) * NT], a2_40[:, :, c], K["ident"][0:NT, 0:NT])
            for c in range(3):
                pe.transpose(p_cols[:, (2 + c) * NT:(3 + c) * NT], a3_40[:, :, c], K["ident"][0:NT, 0:NT])
            pe.transpose(p_cols[:, 5 * NT:6 * NT], type_40[:, :], K["ident"][0:NT, 0:NT]).then_inc(cols_ready, 1)

        @block.gpsimd
        def _(pool):
            for b in range(2):
                open_slot(pool, K, put[b], 48 * G)
            pool.memset(rec[:, :, :], 0.0).then_inc(rec_cleared, 1)
            pool.wait_ge(rec_cleared, 1)
            pool.memset(rec[:, :, D_ONE], 1.0)
            pool.iota(rec[:, :, D_EDGE], [[TE, NT]], base=0, channel_multiplier=1,
                      allow_small_or_imprecise_dtypes=True).then_inc(rec_cleared, 1)
            pool.sem_inc(got_read, 2)
            with pool.Fori(0, NG // 2) as i:
                for b in range(2):
                    g = i * 2 + b
                    pool.wait_ge(idx_ready, g + 1)
                    pool.wait_ge(got_read, g + 1)
                    pool.sem_inc(passed, 1)
                    for s in range(2):
                        for j in range(G):
                            pool.indirect_dma_start(got[:, b, s, j, :], None, table[:, :],
                                                    IOA(idx[:, b, s, j:j + 1], 0), bounds_check=N - 1,
                                                    oob_is_err=False).then_inc(got_in[b], 16)
            with pool.Fori(0, NG // 2) as i:
                for b in range(2):
                    g = i * 2 + b
                    pool.wait_ge(out_ready, g + 1)
                    pool.sem_inc(passed, 1)
                    for j in range(G):
                        for c, lo, width, dram in ((0, 0, RD, rec_d), (1, RD, RC, rec_c), (2, RD + RC, RC, rec_c)):
                            pool.indirect_dma_start(dram[:, :], IOA(put_idx[:, b, j, c:c + 1], 0),
                                                    rec_out[:, b, j, lo:lo + width], None,
                                                    bounds_check=dram.shape[0] - 1,
                                                    oob_is_err=False).then_inc(put[b], 16)
            for b in range(2):
                pool.wait_ge(put[b], 16 * 3 * G * (NG // 2 + 1))

        @block.vector
        def _(dve):
            dve.wait_ge(small_in, 64)
            dve.tensor_copy(type_40[:, :], type_i[:, :]).then_inc(types_ready, 1)
            with dve.Fori(0, NG // 2) as i:
                for b in range(2):
                    g = i * 2 + b
                    dve.tensor_copy(idx[:, b, 0, :], K["dst_col"][:, bass.ds(g * G, G)])
                    dve.tensor_copy(idx[:, b, 1, :], K["src_col"][:, bass.ds(g * G, G)]).then_inc(idx_ready, 1)
                for b in range(2):
                    g = i * 2 + b
                    dve.wait_ge(got_in[b], (i + 1) * (32 * G))
                    for s in range(2):
                        ins = dve.tensor_copy(tab[:, s, bass.ds(g * G, G), :].rearrange("p t c -> p (t c)"),
                                              got[:, b, s, :, :].rearrange("p t c -> p (t c)"))
                    ins.then_inc(got_read, 1)
            dve.wait_ge(got_read, NG + 2)
            n = [0]

            def then(ins):
                ins.then_inc(step, 1)
                n[0] += 1
                dve.wait_ge(step, n[0])

            def rc(c):
                return rec[:, :, c]

            dve.wait_ge(cols_ready, 1)
            dve.wait_ge(rec_cleared, 2)
            dve.tensor_copy(node[:, 0, :], K["dst_col"][:, 0:NT])
            dve.tensor_copy(node[:, 1, :], K["src_col"][:, 0:NT])
            for c in range(2):
                dve.tensor_copy(rc(D_A2 + c), p_cols[:, c * NT:(c + 1) * NT])
            for c in range(3):
                dve.tensor_copy(rc(D_A3 + c), p_cols[:, (2 + c) * NT:(3 + c) * NT])
            then(dve.tensor_copy(type_c[:, :], p_cols[:, 5 * NT:6 * NT]))
            then(dve.tensor_scalar(pick[:, 0, :], type_c[:, :], 0.0, alpha[:, 0:1], ALU.is_equal, ALU.mult))
            for r in range(1, NREL):
                then(dve.tensor_scalar(pick[:, 1, :], type_c[:, :], float(r), alpha[:, r:r + 1], ALU.is_equal,
                                       ALU.mult))
                then(dve.tensor_tensor(pick[:, 0, :], pick[:, 0, :], pick[:, 1, :], ALU.add))
            dst_below, dst_upto, src_below, src_upto = (tab[:, 0, :, c] for c in range(4))
            s_dst_below, s_dst_upto, s_src_below, s_src_upto = (tab[:, 1, :, c] for c in range(4))
            CD, CS = RD, RD + RC
            then(dve.tensor_tensor(rc(RANK_D), dst_below, K["ord"][:, :, 0], ALU.add))
            dve.tensor_tensor(rc(RANK_CD), rc(RANK_D), src_below, ALU.add)
            then(dve.tensor_tensor(part[:, 0, :], s_src_below, K["ord"][:, :, 1], ALU.add))
            dve.tensor_tensor(rc(RANK_CS), part[:, 0, :], s_dst_upto, ALU.add)
            dve.tensor_tensor(part[:, 1, :], dst_upto, src_upto, ALU.add)
            dve.tensor_tensor(part[:, 2, :], s_dst_upto, s_src_upto, ALU.add)
            then(dve.tensor_tensor(part[:, 3, :], s_dst_below, s_src_below, ALU.add))
            dve.tensor_scalar(rc(D_SLOT_D), part[:, 1, :], -1.0, None, ALU.add)
            dve.tensor_scalar(rc(D_SLOT_S), part[:, 2, :], -1.0, None, ALU.add)
            dve.tensor_scalar(rc(D_SAME), K["ord"][:, :, 0], 0.0, None, ALU.is_gt)
            dve.tensor_scalar(rc(CD + C_SAME), K["ord"][:, :, 0], 0.0, None, ALU.is_gt)
            dve.tensor_tensor(rc(CS + C_SAME), rc(RANK_CS), part[:, 3, :], ALU.is_gt)
            dve.tensor_tensor(part[:, 4, :], dst_upto, rc(RANK_D), ALU.subtract)
            dve.tensor_tensor(part[:, 5, :], part[:, 1, :], rc(RANK_CD), ALU.subtract)
            then(dve.tensor_tensor(part[:, 6, :], part[:, 2, :], rc(RANK_CS), ALU.subtract))
            for c in range(3):
                ins = dve.tensor_scalar(part[:, 7 + c, :], part[:, 4 + c, :], 1.5, float(SKIP), ALU.is_gt, ALU.mult)
            then(ins)
            dve.tensor_tensor(rc(D_PUT), part[:, 7, :], node[:, 0, :], ALU.add)
            dve.tensor_tensor(rc(CD + C_PUT), part[:, 8, :], node[:, 0, :], ALU.add)
            dve.tensor_tensor(rc(CS + C_PUT), part[:, 9, :], node[:, 1, :], ALU.add)
            dve.tensor_copy(rc(D_SRC), node[:, 1, :])
            dve.tensor_copy(rc(CD + C_NODE), node[:, 0, :])
            dve.tensor_copy(rc(CD + C_PEER), node[:, 1, :])
            dve.tensor_copy(rc(CS + C_NODE), node[:, 1, :])
            dve.tensor_copy(rc(CS + C_PEER), node[:, 0, :])
            dve.tensor_copy(rc(CD + C_W), pick[:, 0, :])
            then(dve.tensor_copy(rc(CS + C_W), pick[:, 0, :]))
            with dve.Fori(0, NG // 2) as i:
                for b in range(2):
                    g = i * 2 + b
                    dve.wait_ge(put[b], (i + 1) * (48 * G))
                    dve.tensor_copy(rec_out[:, b, :, :].rearrange("p t c -> p (t c)"),
                                    rec[:, bass.ds(g * G, G), :].rearrange("p t c -> p (t c)"))
                    dve.tensor_copy(put_idx[:, b, :, :], rec[:, bass.ds(g * G, G), RANK_D:RANK_D + 3]) \
                       .then_inc(out_ready, 1)


def edge_messages(nc, K, A, msg):
    N = A["x"].shape[0]
    E = A["src"].shape[0]
    NG = E // GE
    with ExitStack() as ctx:
        def sb(name, shape, dt=F32):
            return ctx.enter_context(nc.sbuf_tensor(name, shape, dt))

        def pb(name, shape, dt=F32):
            return ctx.enter_context(nc.psum_tensor(name, shape, dt))

        sem = ctx.enter_context(signals(nc, "em"))
        w1 = sb("em_w1", [P, DC, HID])
        w2 = sb("em_w2", [P, HC, D])
        b1 = sb("em_b1", [P, HC])
        b2 = sb("em_b2", [TE, D])
        ef = sb("em_ef", [TE, 2, G, D])
        x = sb("em_x", [TE, 2, G, D])
        h = sb("em_h", [TE, 2, G, D])
        m = sb("em_m", [TE, 2, G, D])
        idx = sb("em_idx", [TE, 2, G], I32)
        ef_t = sb("em_ef_t", [P, 2, DC, GE])
        hid = sb("em_hid", [P, 2, HC, GE])
        p_t = [pb(f"em_p_t{c}", [P, 512]) for c in range(DC)]
        p_h = [pb(f"em_p_h{c}", [P, 512]) for c in range(HC)]
        p_m = [pb(f"em_p_m{c}", [TE, 2, D]) for c in range(2)]
        norm = Norm(nc, ctx, "em", sem, TE, G, K["eps"])

        w_in = sem("w_in")
        ef_in = [sem(f"ef_in{b}") for b in range(2)]
        x_in = [sem(f"x_in{b}") for b in range(2)]
        m_out = [sem(f"m_out{b}") for b in range(2)]
        idx_ready = sem("idx_ready")
        h_ready = sem("h_ready")
        ef_turned = sem("ef_turned")
        ef_t_ready = sem("ef_t_ready")
        hid_mm = sem("hid_mm")
        hid_ready = sem("hid_ready")
        m_mm = sem("m_mm")
        m_added = sem("m_added")
        m_ready = sem("m_ready")
        h_shifted = sem("h_shifted")
        passed = sem("passed")
        block = ctx.enter_context(nc.Block())

        @block.sync
        def _(sp):
            sp.dma_start(w1[:, :, :], A["L0_gnn_We1"].rearrange("(k p) n -> p k n", p=P)).then_inc(w_in, 16)
            sp.dma_start(w2[:, :, :], A["L0_gnn_We2"].rearrange("(k p) n -> p k n", p=P)).then_inc(w_in, 16)
            with nc.allow_non_contiguous_dma(reason="512 biases"):
                sp.dma_start(b1[:, :], A["L0_gnn_be1"].rearrange("(k p) -> p k", p=P)).then_inc(w_in, 16)
            sp.dma_start(b2[:, :], A["L0_gnn_be2"].rearrange("(a d) -> a d", a=1).to_broadcast([TE, D])) \
                .then_inc(w_in, 16)
            sp.sem_inc(ef_turned, 2)
            with sp.Fori(0, NG // 2) as i:
                for b in range(2):
                    g = i * 2 + b
                    sp.wait_ge(ef_turned, g + 1)
                    sp.dma_start(ef[:, b, :, :], rows_of(A["edge_attr_256"], g, G, TE)).then_inc(ef_in[b], 16)

        @block.gpsimd
        def _(pool):
            pool.sem_inc(h_ready, 2)
            with pool.Fori(0, NG // 2) as i:
                for b in range(2):
                    g = i * 2 + b
                    pool.wait_ge(idx_ready, g + 1)
                    pool.wait_ge(h_ready, g + 1)
                    pool.sem_inc(passed, 1)
                    for j in range(G):
                        pool.indirect_dma_start(x[:, b, j, :], None, A["x"], IOA(idx[:, b, j:j + 1], 0),
                                                bounds_check=N - 1, oob_is_err=False).then_inc(x_in[b], 16)

        @block.vector
        def _(dve):
            for b in range(2):
                dve.tensor_copy(idx[:, b, :], K["src_col"][:, b * G:(b + 1) * G]).then_inc(idx_ready, 1)
                dve.sem_inc(m_out[b], 16)
            dve.wait_ge(w_in, 64)
            with dve.Fori(0, NG // 2) as i:
                for b in range(2):
                    g = i * 2 + b
                    dve.wait_ge(ef_turned, g + 3)
                    dve.tensor_copy(ef_t[:, b, 0, :], p_t[0][:, 0:GE]).then_inc(ef_t_ready, 1)
                    dve.wait_ge(x_in[b], (i + 1) * (16 * G))
                    norm.statistics(dve, g, b, x[:, b, :, :])
                    dve.tensor_copy(idx[:, b, :], K["src_col"][:, bass.ds(g * G + 2 * G, G)]).then_inc(idx_ready, 1)
                    norm.scales(dve, g, b)
                    dve.wait_ge(h_ready, g + 3)
                    dve.wait_ge(m_out[b], (i + 1) * 16)
                    dve.tensor_tensor(m[:, b, :, :], h[:, b, :, :], b2[:, :].unsqueeze(1).to_broadcast([TE, G, D]),
                                      ALU.add).then_inc(h_shifted, 1)
                    dve.wait_ge(h_shifted, g + 1)
                    for c in range(2):
                        dve.wait_ge(m_mm, g * 2 + c + 1)
                        dve.tensor_tensor(m[:, b, 2 * c:2 * c + 2, :], m[:, b, 2 * c:2 * c + 2, :], p_m[c][:, :, :],
                                          ALU.add).then_inc(m_added, 1)

        @block.scalar
        def _(act):
            act.wait_ge(w_in, 64)
            with act.Fori(0, NG // 2) as i:
                for b in range(2):
                    g = i * 2 + b
                    act.wait_ge(ef_turned, g + 3)
                    act.copy(ef_t[:, b, 1, :], p_t[1][:, 0:GE]).then_inc(ef_t_ready, 1)
                    norm.root(act, g, b)
                    norm.rows_out(act, g, b, h[:, b, :, :], x[:, b, :, :]).then_inc(h_ready, 1)
                    for k in range(HC):
                        act.wait_ge(hid_mm, g * HC + k + 1)
                        act.activation(hid[:, b, k, :], p_h[k][:, 0:GE], ACT.Relu, bias=b1[:, k:k + 1]) \
                           .then_inc(hid_ready, 1)
                    act.wait_ge(m_added, g * 2 + 4)
                    act.activation(m[:, b, :, :], m[:, b, :, :], ACT.Relu).then_inc(m_ready, 1)
                    act.wait_ge(m_ready, g + 1)
                    act.dma_start(rows_of(msg, g, G, TE), m[:, b, :, :]).then_inc(m_out[b], 16)
            for b in range(2):
                act.wait_ge(m_out[b], 16 * (NG // 2 + 1))

        @block.tensor
        def _(pe):
            pe.wait_ge(w_in, 64)
            pe.sem_inc(ef_t_ready, 2)
            pe.sem_inc(hid_ready, HC)
            pe.sem_inc(m_added, 2)
            with pe.Fori(0, NG // 2) as i:
                for b in range(2):
                    g = i * 2 + b
                    pe.wait_ge(ef_in[b], (i + 1) * 16)
                    pe.wait_ge(ef_t_ready, g * 2 + 2)
                    for c in range(DC):
                        for j in range(G):
                            mm = pe.transpose(p_t[c][:, j * TE:(j + 1) * TE], ef[:, b, j, c * P:(c + 1) * P],
                                              K["ident"][0:TE, 0:TE])
                    mm.then_inc(ef_turned, 1)
                    pe.wait_ge(ef_t_ready, g * 2 + 4)
                    for k in range(HC):
                        pe.wait_ge(hid_ready, g * HC + k + 1)
                        for c in range(DC):
                            mm = pe.matmul(p_h[k][:, 0:GE], w1[:, c, k * P:(k + 1) * P], ef_t[:, b, c, :],
                                           start=(c == 0), stop=(c == DC - 1))
                        mm.then_inc(hid_mm, 1)
                    pe.wait_ge(hid_ready, g * HC + 2 * HC)
                    for c in range(2):
                        pe.wait_ge(m_added, g * 2 + c + 1)
                        for jj in range(2):
                            j = 2 * c + jj
                            for k in range(HC):
                                mm = pe.matmul(p_m[c][:, jj, :], hid[:, b, k, j * TE:(j + 1) * TE], w2[:, k, :],
                                               start=(k == 0), stop=(k == HC - 1))
                        mm.then_inc(m_mm, 1)


def aggregate_messages(nc, K, msg, rec_d, agg0):
    N = agg0.shape[0]
    E = msg.shape[0]
    NG = E // GE
    same = K["same"]
    with ExitStack() as ctx:
        def sb(name, shape, dt=F32):
            return ctx.enter_context(nc.sbuf_tensor(name, shape, dt))

        def pb(name, shape, dt=F32):
            return ctx.enter_context(nc.psum_tensor(name, shape, dt))

        sem = ctx.enter_context(signals(nc, "ag"))
        rec = sb("ag_rec", [TE, 2, G, RD])
        idx = sb("ag_idx", [TE, 2, 2, G], I32)
        m = sb("ag_m", [TE, 2, G, D])
        run = sb("ag_run", [P, 2, DC, GE])
        rows = sb("ag_rows", [TE, 2, G, D])
        p_s = pb("ag_p_s", [P, 512])
        p_t = [pb(f"ag_p_t{c}", [P, 512]) for c in range(DC)]
        p_r = [pb(f"ag_p_r{c}", [TE, 2, D]) for c in range(2)]

        rec_in = [sem(f"rec_in{b}") for b in range(2)]
        m_in = [sem(f"m_in{b}") for b in range(2)]
        put = [sem(f"put{b}") for b in range(2)]
        idx_ready = sem("idx_ready")
        same_mm = sem("same_mm")
        same_ready = sem("same_ready")
        m_turned = sem("m_turned")
        run_ready = sem("run_ready")
        run_turned = sem("run_turned")
        rows_ready = sem("rows_ready")
        passed = sem("passed")
        block = ctx.enter_context(nc.Block())

        @block.sync
        def _(sp):
            sp.sem_inc(same_mm, 2)
            with sp.Fori(0, NG // 2) as i:
                for b in range(2):
                    g = i * 2 + b
                    sp.wait_ge(same_mm, g + 1)
                    sp.dma_start(rec[:, b, :, :], rows_of(rec_d, g, G, TE)).then_inc(rec_in[b], 16)

        @block.gpsimd
        def _(pool):
            for b in range(2):
                open_slot(pool, K, put[b], 16 * G)
            pool.sem_inc(m_turned, 2)

            def put_rows(g, b):
                pool.wait_ge(rows_ready, g * 2 + 4)
                pool.sem_inc(passed, 1)
                for j in range(G):
                    pool.indirect_dma_start(agg0[:, :], IOA(idx[:, b, 1, j:j + 1], 0), rows[:, b, j, :], None,
                                            bounds_check=N - 1, oob_is_err=False).then_inc(put[b], 16)

            with pool.Fori(0, NG // 2) as i:
                for b in range(2):
                    g = i * 2 + b
                    pool.wait_ge(idx_ready, g + 1)
                    pool.wait_ge(m_turned, g + 1)
                    pool.sem_inc(passed, 1)
                    for j in range(G):
                        pool.indirect_dma_start(m[:, b, j, :], None, msg[:, :], IOA(idx[:, b, 0, j:j + 1], 0),
                                                bounds_check=E - 1, oob_is_err=False).then_inc(m_in[b], 16)
                for b in range(2):
                    put_rows(i * 2 + b, b)
            for b in range(2):
                pool.wait_ge(put[b], 16 * G * (NG // 2 + 1))

        @block.vector
        def _(dve):
            dve.memset(run[:, 1, :, GE - 1], 0.0).then_inc(run_ready, 2)
            with dve.Fori(0, NG // 2) as i:
                for b in range(2):
                    g = i * 2 + b
                    dve.wait_ge(rec_in[b], (i + 1) * 16)
                    dve.wait_ge(put[b], (i + 1) * (16 * G))
                    dve.tensor_copy(idx[:, b, 0, :], rec[:, b, :, D_EDGE])
                    dve.tensor_copy(idx[:, b, 1, :], rec[:, b, :, D_PUT]).then_inc(idx_ready, 1)
                for b in range(2):
                    g = i * 2 + b
                    dve.wait_ge(same_ready, g + 2)
                    dve.wait_ge(m_turned, g + 3)
                    dve.wait_ge(run_ready, g * 2 + 2)
                    for c in range(DC):
                        dve.tensor_tensor_scan(run[:, b, c, :], same[:, bass.ds(g * GE, GE)], p_t[c][:, 0:GE],
                                               run[:, 1 - b, c, GE - 1:GE], ALU.mult, ALU.add) \
                           .then_inc(run_ready, 1)

        @block.scalar
        def _(act):
            with act.Fori(0, NG // 2) as i:
                for b in range(2):
                    g = i * 2 + b
                    act.wait_ge(same_mm, g + 3)
                    act.copy(same[:, bass.ds(g * GE, GE)], p_s[:, 0:GE]).then_inc(same_ready, 1)
                for b in range(2):
                    g = i * 2 + b
                    act.wait_ge(put[b], (i + 1) * (16 * G))
                    for c in range(2):
                        act.wait_ge(run_turned, g * 2 + c + 1)
                        act.copy(rows[:, b, 2 * c:2 * c + 2, :], p_r[c][:, :, :]).then_inc(rows_ready, 1)

        @block.tensor
        def _(pe):
            pe.sem_inc(same_ready, 1)
            pe.sem_inc(rows_ready, 2)
            with pe.Fori(0, NG // 2) as i:
                for b in range(2):
                    g = i * 2 + b
                    pe.wait_ge(rec_in[b], (i + 1) * 16)
                    pe.wait_ge(idx_ready, g + 1)
                    pe.wait_ge(same_ready, g + 1)
                    for j in range(G):
                        mm = pe.matmul(p_s[:, j * TE:(j + 1) * TE],
                                       rec[:, b, j, D_SAME:D_SAME + 1].to_broadcast([TE, P]),
                                       K["ident"][0:TE, 0:TE], start=True, stop=True)
                    mm.then_inc(same_mm, 1)
                for b in range(2):
                    g = i * 2 + b
                    pe.wait_ge(m_in[b], (i + 1) * (16 * G))
                    pe.wait_ge(run_ready, g * 2 + 2)
                    for c in range(DC):
                        for j in range(G):
                            mm = pe.transpose(p_t[c][:, j * TE:(j + 1) * TE], m[:, b, j, c * P:(c + 1) * P],
                                              K["ident"][0:TE, 0:TE])
                    mm.then_inc(m_turned, 1)
                    pe.wait_ge(run_ready, g * 2 + 4)
                    for c in range(2):
                        pe.wait_ge(rows_ready, g * 2 + c + 1)
                        for jj in range(2):
                            j = 2 * c + jj
                            for k in range(DC):
                                mm = pe.transpose(p_r[c][:, jj, k * P:(k + 1) * P],
                                                  run[:, b, k, j * TE:(j + 1) * TE], K["ident"][:, :])
                        mm.then_inc(run_turned, 1)


def broadcast_row(vector, rows):
    return vector.rearrange("(a d) -> a d", a=1).to_broadcast([rows, vector.shape[0]])


def node_network(nc, K, A, agg0, x1_dram, out):
    N = A["x"].shape[0]
    R = G * P
    NG = -(-N // R)
    XB = 4
    UN = 4
    assert NG % UN == 0
    with ExitStack() as ctx:
        def sb(name, shape, dt=F32):
            return ctx.enter_context(nc.sbuf_tensor(name, shape, dt))

        def pb(name, shape, dt=F32):
            return ctx.enter_context(nc.psum_tensor(name, shape, dt))

        sem = ctx.enter_context(signals(nc, "nn"))
        w1 = sb("nn_w1", [P, DC, HID])
        w2 = sb("nn_w2", [P, HC, D])
        b1 = sb("nn_b1", [P, HC])
        b2 = sb("nn_b2", [P, D])
        late = sb("nn_late", [P, 2, D])
        late_sum = sb("nn_late_sum", [P, D])
        gain = sb("nn_gain", [P, 1])
        x = sb("nn_x", [P, XB, G, D])
        agg = sb("nn_agg", [P, XB, G, D])
        h = sb("nn_h", [P, 2, G, D])
        x1 = sb("nn_x1", [P, 2, G, D])
        x3 = sb("nn_x3", [P, 2, G, D])
        h_t = sb("nn_h_t", [P, 2, DC, R])
        hid = sb("nn_hid", [P, 2, HC, R])
        p_t = [pb(f"nn_p_t{c}", [P, R]) for c in range(DC)]
        p_h = [pb(f"nn_p_h{c}", [P, R]) for c in range(HC)]
        p_o = [pb(f"nn_p_o{c}", [P, 2, D]) for c in range(2)]
        norm = Norm(nc, ctx, "nn", sem, P, G, K["eps"])

        w_in = sem("w_in")
        x_in = [sem(f"x_in{r}") for r in range(XB)]
        x1_out = [sem(f"x1_out{b}") for b in range(2)]
        x3_out = [sem(f"x3_out{b}") for b in range(2)]
        late_ready = sem("late_ready")
        h_ready = sem("h_ready")
        x_shifted = sem("x_shifted")
        mixed = sem("mixed")
        turned = sem("turned")
        h_t_ready = sem("h_t_ready")
        hid_mm = sem("hid_mm")
        hid_ready = sem("hid_ready")
        o_mm = sem("o_mm")
        x1_ready = sem("x1_ready")
        x3_ready = sem("x3_ready")
        block = ctx.enter_context(nc.Block())

        def group(dram, g):
            first = min(g * R, N - R) if isinstance(g, int) else g * R
            return dram[bass.ds(first, R), :].rearrange("(p j) d -> p j d", j=G)

        def over_groups(eng, body):
            with eng.Fori(0, NG // UN - 1) as i:
                for r in range(UN):
                    body(i * UN + r, i, r)
            for r in range(UN):
                body(NG - UN + r, NG // UN - 1, r)

        @block.sync
        def _(sp):
            sp.dma_start(w1[:, :, :], A["L0_gnn_Wn1"].rearrange("(k p) n -> p k n", p=P)).then_inc(w_in, 16)
            sp.dma_start(w2[:, :, :], A["L0_gnn_Wn2"].rearrange("(k p) n -> p k n", p=P)).then_inc(w_in, 16)
            with nc.allow_non_contiguous_dma(reason="512 biases"):
                sp.dma_start(b1[:, :], A["L0_gnn_bn1"].rearrange("(k p) -> p k", p=P)).then_inc(w_in, 16)
            sp.dma_start(b2[:, :], broadcast_row(A["L0_gnn_bn2"], P)).then_inc(w_in, 16)
            sp.dma_start(late[:, 0, :], broadcast_row(A["L1_gnn_bias"], P)).then_inc(w_in, 16)
            sp.dma_start(late[:, 1, :], broadcast_row(A["L2_gnn_bias"], P)).then_inc(w_in, 16)
            sp.dma_start(gain[:, :], broadcast_row(A["L0_gnn_eps"], P)).then_inc(w_in, 16)
            sp.sem_inc(x1_ready, 2 * XB)

            def load(g, i, r):
                sp.wait_ge(x1_ready, g * 2 + 2)
                sp.dma_start(x[:, r, :, :], group(A["x"], g)).then_inc(x_in[r], 16)
                sp.dma_start(agg[:, r, :, :], group(agg0, g)).then_inc(x_in[r], 16)

            over_groups(sp, load)

        @block.gpsimd
        def _(pool):
            pool.wait_ge(late_ready, 2)
            for b in range(2):
                pool.sem_inc(x3_out[b], 16)

            def shift_rows(g, i, r):
                pool.wait_ge(h_ready, g + 1)
                pool.tensor_tensor(x[:, r, :, :], x[:, r, :, :], b2[:, :].unsqueeze(1).to_broadcast([P, G, D]),
                                   ALU.add).then_inc(x_shifted, 1)
                b = r % 2
                pool.wait_ge(x1_ready, g * 2 + 2 + 2 * XB)
                pool.wait_ge(x3_out[b], (i * (UN // 2) + r // 2 + 1) * 16)
                pool.tensor_tensor(x3[:, b, :, :], x1[:, b, :, :],
                                   late_sum[:, :].unsqueeze(1).to_broadcast([P, G, D]), ALU.add) \
                    .then_inc(x3_ready, 1)

            over_groups(pool, shift_rows)

        @block.vector
        def _(dve):
            dve.wait_ge(w_in, 16 * 7)
            for b in range(2):
                dve.sem_inc(x1_out[b], 16)
            dve.tensor_tensor(late_sum[:, :], late[:, 0, :], late[:, 1, :], ALU.add).then_inc(late_ready, 1)
            dve.tensor_scalar(gain[:, :], gain[:, :], 1.0, None, ALU.add).then_inc(late_ready, 1)
            dve.wait_ge(late_ready, 2)

            def prepare(g, i, r):
                b = r % 2
                dve.wait_ge(x_in[r], (i + 1) * 32)
                norm.statistics(dve, g, b, x[:, r, :, :])
                norm.scales(dve, g, b)
                dve.wait_ge(h_ready, g + 1)
                dve.scalar_tensor_tensor(out=agg[:, r, :, :].rearrange("p j d -> p (j d)"),
                                         in0=h[:, b, :, :].rearrange("p j d -> p (j d)"), scalar=gain[:, 0:1],
                                         in1=agg[:, r, :, :].rearrange("p j d -> p (j d)"),
                                         op0=ALU.mult, op1=ALU.add).then_inc(mixed, 1)
                dve.wait_ge(turned, g + 1)
                dve.tensor_copy(h_t[:, b, 0, :], p_t[0][:, :]).then_inc(h_t_ready, 1)

            def finish(g, i, r):
                b = r % 2
                dve.wait_ge(x_shifted, g + 1)
                dve.wait_ge(x1_out[b], (i * (UN // 2) + r // 2 + 1) * 16)
                dve.wait_ge(x3_ready, g + 1 - 2) if isinstance(g, int) and g >= 2 else None
                for c in range(2):
                    dve.wait_ge(o_mm, g * 2 + c + 1)
                    dve.tensor_tensor(x1[:, b, 2 * c:2 * c + 2, :], x[:, r, 2 * c:2 * c + 2, :], p_o[c][:, :, :],
                                      ALU.add).then_inc(x1_ready, 1)

            def body(g, i, r):
                last = isinstance(g, int) and g == NG - 1
                if not last:
                    prepare(g + 1, i + (r + 1) // UN, (r + 1) % UN)
                finish(g, i, r)

            prepare(0, 0, 0)
            over_groups(dve, body)

        @block.scalar
        def _(act):
            act.wait_ge(w_in, 16 * 7)

            def store(g, i, r):
                b = r % 2
                act.wait_ge(x1_ready, g * 2 + 2 + 2 * XB)
                act.dma_start(group(x1_dram, g), x1[:, b, :, :]).then_inc(x1_out[b], 16)
                act.wait_ge(x3_ready, g + 1)
                act.dma_start(group(out, g), x3[:, b, :, :]).then_inc(x3_out[b], 16)

            def hidden(g, b, k):
                act.wait_ge(hid_mm, g * HC + k + 1)
                act.activation(hid[:, b, k, :], p_h[k][:, :], ACT.Relu, bias=b1[:, k:k + 1]).then_inc(hid_ready, 1)

            def rows(g, r):
                norm.rows_out(act, g, r % 2, h[:, r % 2, :, :], x[:, r, :, :]).then_inc(h_ready, 1)

            def second_half(g, r):
                act.wait_ge(turned, g + 1)
                act.copy(h_t[:, r % 2, 1, :], p_t[1][:, :]).then_inc(h_t_ready, 1)

            def body(g, i, r):
                last = isinstance(g, int) and g == NG - 1
                b = r % 2
                hidden(g, b, 0)
                if not last:
                    norm.root(act, g + 1, (r + 1) % 2)
                hidden(g, b, 1)
                if not last:
                    rows(g + 1, (r + 1) % UN)
                hidden(g, b, 2)
                hidden(g, b, 3)
                if not last:
                    second_half(g + 1, (r + 1) % UN)
                if last:
                    act.wait_ge(x1_out[1 - b], 16 * (NG // 2 + 1))
                    act.wait_ge(x3_out[1 - b], 16 * (NG // 2 + 1))
                store(g, i, r)

            norm.root(act, 0, 0)
            rows(0, 0)
            second_half(0, 0)
            over_groups(act, body)
            for b in range(2):
                act.wait_ge(x1_out[b], 16 * (NG // 2 + 1))
                act.wait_ge(x3_out[b], 16 * (NG // 2 + 1))

        @block.tensor
        def _(pe):
            pe.wait_ge(w_in, 16 * 7)
            pe.sem_inc(hid_ready, HC)

            def turn(g, r):
                pe.wait_ge(mixed, g + 1)
                if not (isinstance(g, int) and g == 0):
                    pe.wait_ge(h_t_ready, g * 2)
                for c in range(DC):
                    for j in range(G):
                        mm = pe.transpose(p_t[c][:, j * P:(j + 1) * P], agg[:, r, j, c * P:(c + 1) * P],
                                          K["ident"][:, :])
                mm.then_inc(turned, 1)

            def body(g, i, r):
                last = isinstance(g, int) and g == NG - 1
                b = r % 2
                pe.wait_ge(h_t_ready, g * 2 + 2)
                for k in range(HC):
                    pe.wait_ge(hid_ready, g * HC + k + 1)
                    for c in range(DC):
                        mm = pe.matmul(p_h[k][:, :], w1[:, c, k * P:(k + 1) * P], h_t[:, b, c, :],
                                       start=(c == 0), stop=(c == DC - 1))
                    mm.then_inc(hid_mm, 1)
                if not last:
                    turn(g + 1, (r + 1) % UN)
                pe.wait_ge(hid_ready, g * HC + 2 * HC)
                for c in range(2):
                    pe.wait_ge(x1_ready, g * 2 + c + 2 * XB - 1)
                    for jj in range(2):
                        j = 2 * c + jj
                        for k in range(HC):
                            mm = pe.matmul(p_o[c][:, jj, :], hid[:, b, k, j * P:(j + 1) * P], w2[:, k, :],
                                           start=(k == 0), stop=(k == HC - 1))
                    mm.then_inc(o_mm, 1)

            turn(0, 0)
            over_groups(pe, body)


def relation_layer(nc, K, A, rec_c, x1_dram, x2_dram, out):
    N = out.shape[0]
    NG = x2_dram.shape[0] // GE
    with ExitStack() as ctx:
        def sb(name, shape, dt=F32):
            return ctx.enter_context(nc.sbuf_tensor(name, shape, dt))

        def pb(name, shape, dt=F32):
            return ctx.enter_context(nc.psum_tensor(name, shape, dt))

        sem = ctx.enter_context(signals(nc, "rl"))
        w = sb("rl_w", [P, DC, D])
        bias = sb("rl_bias", [TE, 2, D])
        rec = sb("rl_rec", [TE, 2, G, RC])
        keep = sb("rl_keep", [TE, 2, G, RC])
        idx = sb("rl_idx", [TE, 2, 2, G], I32)
        put_idx = sb("rl_put_idx", [TE, 2, G], I32)
        x = sb("rl_x", [TE, 2, G, D])
        base = sb("rl_base", [TE, 2, G, D])
        h = sb("rl_h", [TE, 2, G, D])
        same = sb("rl_same", [P, 2, GE])
        run = sb("rl_run", [P, 2, DC, GE])
        x2 = sb("rl_x2", [TE, 2, G, D])
        x3 = sb("rl_x3", [TE, 2, G, D])
        p_s = pb("rl_p_s", [P, 512])
        p_t = [pb(f"rl_p_t{c}", [P, 512]) for c in range(DC)]
        p_o = [pb(f"rl_p_o{c}", [TE, 2, D]) for c in range(2)]
        norm = Norm(nc, ctx, "rl", sem, TE, G, K["eps"])

        w_in = sem("w_in")
        rec_in = [sem(f"rec_in{b}") for b in range(2)]
        x_in = [sem(f"x_in{b}") for b in range(2)]
        x2_out = [sem(f"x2_out{b}") for b in range(2)]
        put = [sem(f"put{b}") for b in range(2)]
        idx_ready = sem("idx_ready")
        put_idx_ready = sem("put_idx_ready")
        h_ready = sem("h_ready")
        weighted = sem("weighted")
        same_mm = sem("same_mm")
        same_ready = sem("same_ready")
        turned = sem("turned")
        run_ready = sem("run_ready")
        o_mm = sem("o_mm")
        summed = sem("summed")
        x2_ready = sem("x2_ready")
        x3_ready = sem("x3_ready")
        passed = sem("passed")
        block = ctx.enter_context(nc.Block())

        def over_groups(eng, body):
            with eng.Fori(0, NG // 2 - 1) as i:
                for b in range(2):
                    body(i * 2 + b, i, b, True)
            for b in range(2):
                body(NG - 2 + b, NG // 2 - 1, b, False)

        @block.sync
        def _(sp):
            sp.dma_start(w[:, :, :], A["L1_gnn_weight"].rearrange("(k p) n -> p k n", p=P)).then_inc(w_in, 16)
            sp.dma_start(bias[:, 0, :], broadcast_row(A["L1_gnn_bias"], TE)).then_inc(w_in, 16)
            sp.dma_start(bias[:, 1, :], broadcast_row(A["L2_gnn_bias"], TE)).then_inc(w_in, 16)
            for b in range(2):
                sp.dma_start(rec[:, b, :, :], rows_of(rec_c, b, G, TE)).then_inc(rec_in[b], 16)

            def body(g, i, b, more):
                if more:
                    sp.wait_ge(idx_ready, g + 1)
                    sp.dma_start(rec[:, b, :, :], rows_of(rec_c, g + 2, G, TE)).then_inc(rec_in[b], 16)
                sp.wait_ge(x2_ready, g + 1)
                sp.dma_start(rows_of(x2_dram, g, G, TE), x2[:, b, :, :]).then_inc(x2_out[b], 16)

            over_groups(sp, body)
            for b in range(2):
                sp.wait_ge(x2_out[b], 16 * (NG // 2 + 1))

        @block.gpsimd
        def _(pool):
            for b in range(2):
                open_slot(pool, K, put[b], 16 * G)

            def fetch(g, b):
                pool.wait_ge(idx_ready, g + 1)
                pool.sem_inc(passed, 1)
                for j in range(G):
                    for s, rows in ((1, x), (0, base)):
                        pool.indirect_dma_start(rows[:, b, j, :], None, x1_dram[:, :], IOA(idx[:, b, s, j:j + 1], 0),
                                                bounds_check=N - 1, oob_is_err=False).then_inc(x_in[b], 16)

            def body(g, i, b, more):
                if more:
                    fetch(g + 2, b)
                pool.wait_ge(x3_ready, g + 1)
                pool.sem_inc(passed, 1)
                for j in range(G):
                    pool.indirect_dma_start(out[:, :], IOA(put_idx[:, b, j:j + 1], 0), x3[:, b, j, :], None,
                                            bounds_check=N - 1, oob_is_err=False).then_inc(put[b], 16)

            for b in range(2):
                fetch(b, b)
            over_groups(pool, body)
            for b in range(2):
                pool.wait_ge(put[b], 16 * G * (NG // 2 + 1))

        @block.vector
        def _(dve):
            def take(g, i, b):
                dve.wait_ge(rec_in[b], (i + 1) * 16)
                dve.tensor_copy(keep[:, b, :, :], rec[:, b, :, :])
                dve.tensor_copy(idx[:, b, 0, :], rec[:, b, :, C_NODE])
                dve.tensor_copy(idx[:, b, 1, :], rec[:, b, :, C_PEER]).then_inc(idx_ready, 1)

            dve.memset(run[:, 1, :, GE - 1], 0.0).then_inc(run_ready, 2)
            dve.wait_ge(w_in, 48)
            for b in range(2):
                dve.sem_inc(x2_out[b], 16)
                take(b, 0, b)

            def body(g, i, b, more):
                dve.wait_ge(x_in[b], (i + 1) * (32 * G))
                norm.statistics(dve, g, b, x[:, b, :, :])
                norm.scales(dve, g, b)
                dve.wait_ge(put[b], (i + 1) * (16 * G))
                dve.wait_ge(idx_ready, g + 1)
                dve.tensor_copy(put_idx[:, b, :], keep[:, b, :, C_PUT]).then_inc(put_idx_ready, 1)
                dve.wait_ge(h_ready, g + 1)
                for j in range(G):
                    ins = dve.tensor_scalar(h[:, b, j, :], h[:, b, j, :], keep[:, b, j, C_W:C_W + 1], None, ALU.mult)
                ins.then_inc(weighted, 1)
                dve.wait_ge(same_ready, g + 2)
                dve.wait_ge(turned, g + 1)
                dve.wait_ge(run_ready, g * 2 + 2)
                for c in range(DC):
                    dve.tensor_tensor_scan(run[:, b, c, :], same[:, b, :], p_t[c][:, 0:GE],
                                           run[:, 1 - b, c, GE - 1:GE], ALU.mult, ALU.add).then_inc(run_ready, 1)
                dve.wait_ge(x2_out[b], (i + 1) * 16)
                for c in range(2):
                    dve.wait_ge(o_mm, g * 2 + c + 1)
                    dve.tensor_tensor(x2[:, b, 2 * c:2 * c + 2, :], base[:, b, 2 * c:2 * c + 2, :], p_o[c][:, :, :],
                                      ALU.add).then_inc(summed, 1)
                dve.wait_ge(summed, g * 2 + 4)
                dve.tensor_tensor(x2[:, b, :, :], x2[:, b, :, :],
                                  bias[:, 0:1, :].to_broadcast([TE, G, D]), ALU.add).then_inc(x2_ready, 1)
                dve.wait_ge(x2_ready, g + 1)
                dve.tensor_tensor(x3[:, b, :, :], x2[:, b, :, :],
                                  bias[:, 1:2, :].to_broadcast([TE, G, D]), ALU.add).then_inc(x3_ready, 1)
                if more:
                    take(g + 2, i + 1, b)

            over_groups(dve, body)

        @block.scalar
        def _(act):
            def body(g, i, b, more):
                norm.root(act, g, b)
                norm.rows_out(act, g, b, h[:, b, :, :], x[:, b, :, :]).then_inc(h_ready, 1)
                act.wait_ge(same_mm, g + 1)
                act.copy(same[:, b, :], p_s[:, 0:GE]).then_inc(same_ready, 1)

            over_groups(act, body)

        @block.tensor
        def _(pe):
            pe.wait_ge(w_in, 48)
            pe.sem_inc(same_ready, 1)
            pe.sem_inc(summed, 2)

            def body(g, i, b, more):
                pe.wait_ge(idx_ready, g + 1)
                pe.wait_ge(same_ready, g + 1)
                for j in range(G):
                    mm = pe.matmul(p_s[:, j * TE:(j + 1) * TE],
                                   keep[:, b, j, C_SAME:C_SAME + 1].to_broadcast([TE, P]),
                                   K["ident"][0:TE, 0:TE], start=True, stop=True)
                mm.then_inc(same_mm, 1)
                pe.wait_ge(weighted, g + 1)
                pe.wait_ge(run_ready, g * 2 + 2)
                for c in range(DC):
                    for j in range(G):
                        mm = pe.transpose(p_t[c][:, j * TE:(j + 1) * TE], h[:, b, j, c * P:(c + 1) * P],
                                          K["ident"][0:TE, 0:TE])
                mm.then_inc(turned, 1)
                pe.wait_ge(run_ready, g * 2 + 4)
                for c in range(2):
                    pe.wait_ge(summed, g * 2 + c + 1)
                    for jj in range(2):
                        j = 2 * c + jj
                        for k in range(DC):
                            mm = pe.matmul(p_o[c][:, jj, :], run[:, b, k, j * TE:(j + 1) * TE], w[:, k, :],
                                           start=(k == 0), stop=(k == DC - 1))
                    mm.then_inc(o_mm, 1)

            over_groups(pe, body)



def attention_scores(nc, K, A, V, rec_d, x2_dram):
    NG = V["edges"] // GE
    NHEAD, DH = A["L2_gnn_a_src"].shape
    WS = D + NHEAD
    with ExitStack() as ctx:
        def sb(name, shape, dt=F32):
            return ctx.enter_context(nc.sbuf_tensor(name, shape, dt))

        def pb(name, shape, dt=F32):
            return ctx.enter_context(nc.psum_tensor(name, shape, dt))

        sem = ctx.enter_context(signals(nc, "as"))
        w = sb("as_w", [P, DC, D])
        w_t = sb("as_w_t", [P, DC, WS])
        a_col = sb("as_a_col", [P, DC])
        a_blocks = sb("as_a_blocks", [P, DC, NHEAD])
        a_dst = sb("as_a_dst", [TE, D])
        w_edge = sb("as_w_edge", [4, D])
        bias = sb("as_bias", [TE, D])
        rec = sb("as_rec", [TE, 2, G, RD])
        idx = sb("as_idx", [TE, 2, 2, G], I32)
        x = sb("as_x", [TE, 2, 2 * G, D])
        h = sb("as_h", [TE, 2 * G, D])
        h_t = sb("as_h_t", [P, 2 * DC, GE])
        attr_t = sb("as_attr_t", [4, 2, GE])
        enc = sb("as_enc", [TE, 2, D])
        score = sb("as_score", [TE, 2, G, NHEAD])
        score_l = sb("as_score_l", [TE, 2, G, NHEAD])
        p_a = pb("as_p_a", [P, 512])
        p_t = [pb(f"as_p_t{c}", [P, 512]) for c in range(DC)]
        p_src = [pb(f"as_p_src{c}", [TE, 512]) for c in range(2)]
        p_dst = [pb(f"as_p_dst{c}", [TE, 2, D]) for c in range(2)]
        norm = Norm(nc, ctx, "as", sem, TE, 2 * G, K["eps"])

        w_in = sem("w_in")
        setup = sem("setup")
        w_turned = sem("w_turned")
        w_ready = sem("w_ready")
        rec_in = [sem(f"rec_in{b}") for b in range(2)]
        x_in = [sem(f"x_in{b}") for b in range(2)]
        idx_ready = sem("idx_ready")
        h_ready = sem("h_ready")
        attr_turned = sem("attr_turned")
        small_read = sem("small_read")
        turned = sem("turned")
        h_t_ready = sem("h_t_ready")
        src_mm = sem("src_mm")
        dst_mm = sem("dst_mm")
        src_kept = sem("src_kept")
        enc_shifted = sem("enc_shifted")
        enc_scaled = sem("enc_scaled")
        enc_summed = sem("enc_summed")
        score_summed = sem("score_summed")
        score_ready = sem("score_ready")
        score_turned = sem("score_turned")
        passed = sem("passed")
        block = ctx.enter_context(nc.Block())

        def over_groups(eng, body):
            with eng.Fori(0, NG // 2 - 1) as i:
                for b in range(2):
                    body(i * 2 + b, i, b, True)
            for b in range(2):
                body(NG - 2 + b, NG // 2 - 1, b, False)

        @block.sync
        def _(sp):
            sp.dma_start(w[:, :, :], A["L2_gnn_W"].rearrange("(k p) n -> p k n", p=P)).then_inc(w_in, 16)
            with nc.allow_non_contiguous_dma(reason="a few small weights"):
                sp.dma_start(a_col[:, :], A["L2_gnn_a_src"].rearrange("h d -> (h d)").rearrange("(k p) -> p k", p=P)) \
                    .then_inc(w_in, 16)
                sp.dma_start(w_edge[0:3, :], A["L2_gnn_edge_W"].rearrange("n c -> c n")).then_inc(w_in, 16)
            sp.dma_start(w_edge[3:4, :], broadcast_row(A["L2_gnn_edge_b"], 1)).then_inc(w_in, 16)
            sp.dma_start(a_dst[:, :], broadcast_row(A["L2_gnn_a_dst"].rearrange("h d -> (h d)"), TE)).then_inc(w_in, 16)
            sp.dma_start(bias[:, :], broadcast_row(A["L2_gnn_bias"], TE)).then_inc(w_in, 16)
            for b in range(2):
                sp.dma_start(rec[:, b, :, :], rows_of(rec_d, b, G, TE)).then_inc(rec_in[b], 16)

            def body(g, i, b, more):
                if more:
                    sp.wait_ge(attr_turned, g + 1)
                    sp.dma_start(rec[:, b, :, :], rows_of(rec_d, g + 2, G, TE)).then_inc(rec_in[b], 16)

            over_groups(sp, body)

        @block.gpsimd
        def _(pool):
            pool.memset(a_blocks[:, :, :], 1.0).then_inc(setup, 1)
            pool.wait_ge(setup, 1)
            pool.affine_select(out=a_blocks[:, :, :], in_=a_blocks[:, :, :], compare_op=ALU.is_ge, fill=0.0,
                               base=0, pattern=[[P, DC], [-DH, NHEAD]], channel_multiplier=1).then_inc(setup, 1)
            pool.wait_ge(setup, 2)
            pool.affine_select(out=a_blocks[:, :, :], in_=a_blocks[:, :, :], compare_op=ALU.is_ge, fill=0.0,
                               base=DH - 1, pattern=[[-P, DC], [DH, NHEAD]], channel_multiplier=-1).then_inc(setup, 1)

            def fetch(g, b):
                pool.wait_ge(idx_ready, g + 1)
                pool.sem_inc(passed, 1)
                for j in range(G):
                    for s in range(2):
                        pool.indirect_dma_start(x[:, b, s * G + j, :], None, x2_dram[:, :],
                                                IOA(idx[:, b, s, j:j + 1], 0), bounds_check=x2_dram.shape[0] - 1,
                                                oob_is_err=False).then_inc(x_in[b], 16)

            def body(g, i, b, more):
                if more:
                    fetch(g + 2, b)

            for b in range(2):
                fetch(b, b)
            over_groups(pool, body)

        @block.vector
        def _(dve):
            def take(g, i, b):
                dve.wait_ge(rec_in[b], (i + 1) * 16)
                dve.tensor_copy(idx[:, b, 0, :], rec[:, b, :, D_SLOT_S])
                dve.tensor_copy(idx[:, b, 1, :], rec[:, b, :, D_SLOT_D]).then_inc(idx_ready, 1)

            dve.wait_ge(w_in, 96)
            for b in range(2):
                take(b, 0, b)
            dve.wait_ge(setup, 3)
            for k in range(DC):
                ins = dve.tensor_scalar(a_blocks[:, k, :], a_blocks[:, k, :], a_col[:, k:k + 1], None, ALU.mult)
            ins.then_inc(setup, 1)
            dve.wait_ge(w_turned, 1)
            for k in range(DC):
                ins = dve.tensor_copy(w_t[:, k, :], p_t[k][:, 0:WS])
            ins.then_inc(w_ready, 1)

            def body(g, i, b, more):
                dve.wait_ge(x_in[b], (i + 1) * (32 * G))
                norm.statistics(dve, g, b, x[:, b, :, :])
                norm.scales(dve, g, b)
                dve.tensor_tensor(V["base"][:, bass.ds(g * G, G), :], x[:, b, G:2 * G, :],
                                  bias[:, :].unsqueeze(1).to_broadcast([TE, G, D]), ALU.add)
                for s in range(2):
                    dve.wait_ge(turned, g * 2 + s + 1)
                    dve.tensor_copy(h_t[:, s * DC, :], p_t[0][:, 0:GE]).then_inc(h_t_ready, 1)
                for j in range(G):
                    dve.wait_ge(dst_mm, g * G + j + 1)
                    dve.scalar_tensor_tensor(out=enc[:, j % 2, :], in0=p_dst[j % 2][:, 1, :], scalar=0.0,
                                             in1=a_dst[:, :], op0=ALU.max, op1=ALU.add).then_inc(enc_shifted, 1)
                    dve.wait_ge(enc_shifted, g * G + j + 1)
                    dve.tensor_tensor(enc[:, j % 2, :], enc[:, j % 2, :], p_dst[j % 2][:, 0, :], ALU.mult) \
                       .then_inc(enc_scaled, 1)
                    dve.wait_ge(enc_scaled, g * G + j + 3)
                    dve.tensor_reduce(score[:, b, j, :], enc[:, j % 2, :].rearrange("p (h d) -> p h d", h=NHEAD),
                                      AX.X, ALU.add).then_inc(enc_summed, 1)
                dve.wait_ge(enc_summed, g * G + G)
                dve.wait_ge(src_kept, g * G + G + 2)
                dve.tensor_tensor(score[:, b, :, :], score[:, b, :, :],
                                  V["proj"][:, bass.ds(g * G, G), D:WS], ALU.add).then_inc(score_summed, 1)
                dve.wait_ge(score_summed, g + 1)
                dve.scalar_tensor_tensor(out=score_l[:, b, :, :], in0=score[:, b, :, :], scalar=0.2,
                                         in1=score[:, b, :, :], op0=ALU.mult, op1=ALU.max).then_inc(score_ready, 1)
                if more:
                    take(g + 2, i + 1, b)

            over_groups(dve, body)

        @block.scalar
        def _(act):
            def body(g, i, b, more):
                act.wait_ge(attr_turned, g + 1)
                act.copy(attr_t[:, b, :], p_a[0:4, 0:GE]).then_inc(small_read, 1)
                norm.root(act, g, b)
                norm.rows_out(act, g, b, h[:, :, :], x[:, b, :, :]).then_inc(h_ready, 1)
                for s in range(2):
                    act.wait_ge(turned, g * 2 + s + 1)
                    act.copy(h_t[:, s * DC + 1, :], p_t[1][:, 0:GE]).then_inc(h_t_ready, 1)
                for j in range(G):
                    act.wait_ge(src_mm, g * G + j + 1)
                    act.copy(V["proj"][:, bass.ds(g * G + j, 1), :].rearrange("p t n -> p (t n)"),
                             p_src[j % 2][:, 0:WS]).then_inc(src_kept, 1)
                act.wait_ge(score_turned, g + 1)
                act.copy(V["score_t"][:, bass.ds(g * GE, GE)], p_a[0:NHEAD, 0:GE]).then_inc(small_read, 1)

            over_groups(act, body)

        @block.tensor
        def _(pe):
            pe.wait_ge(w_in, 96)
            for k in range(DC):
                for n in range(DC):
                    pe.transpose(p_t[k][:, n * P:(n + 1) * P], w[:, n, k * P:(k + 1) * P], K["ident"][:, :])
            pe.wait_ge(setup, 4)
            for k in range(DC):
                for n in range(DC):
                    mm = pe.matmul(p_t[k][:, D:WS], w[:, n, k * P:(k + 1) * P], a_blocks[:, n, :],
                                   start=(n == 0), stop=(n == DC - 1))
            mm.then_inc(w_turned, 1)
            pe.sem_inc(small_read, 1)
            pe.sem_inc(src_kept, 2)
            pe.sem_inc(enc_scaled, 2)
            pe.wait_ge(w_ready, 1)
            pe.sem_inc(h_t_ready, 2)

            def body(g, i, b, more):
                pe.wait_ge(idx_ready, g + 1)
                pe.wait_ge(rec_in[b], (i + 1) * 16)
                pe.wait_ge(small_read, g * 2 + 1)
                for j in range(G):
                    mm = pe.transpose(p_a[0:4, j * TE:(j + 1) * TE], rec[:, b, j, D_A3:D_A3 + 4],
                                      K["ident"][0:TE, 0:TE])
                mm.then_inc(attr_turned, 1)
                pe.wait_ge(h_ready, g + 1)
                for s in range(2):
                    pe.wait_ge(h_t_ready, g * 4 + s * 2 + 2)
                    for c in range(DC):
                        for j in range(G):
                            mm = pe.transpose(p_t[c][:, j * TE:(j + 1) * TE], h[:, s * G + j, c * P:(c + 1) * P],
                                              K["ident"][0:TE, 0:TE])
                    mm.then_inc(turned, 1)
                pe.wait_ge(h_t_ready, g * 4 + 6)
                pe.wait_ge(small_read, g * 2 + 2)
                for j in range(G):
                    cols = slice(j * TE, (j + 1) * TE)
                    pe.wait_ge(enc_scaled, g * G + j + 1)
                    for k in range(DC):
                        pe.matmul(p_dst[j % 2][:, 0, :], h_t[:, DC + k, cols], w_t[:, k, 0:D],
                                  start=(k == 0), stop=(k == DC - 1))
                    pe.matmul(p_dst[j % 2][:, 1, :], attr_t[:, b, cols], w_edge[:, :], start=True, stop=True) \
                        .then_inc(dst_mm, 1)
                    pe.wait_ge(src_kept, g * G + j + 1)
                    for k in range(DC):
                        mm = pe.matmul(p_src[j % 2][:, 0:WS], h_t[:, k, cols], w_t[:, k, :],
                                       start=(k == 0), stop=(k == DC - 1))
                    mm.then_inc(src_mm, 1)
                pe.wait_ge(score_ready, g + 1)
                for j in range(G):
                    mm = pe.transpose(p_a[0:NHEAD, j * TE:(j + 1) * TE], score_l[:, b, j, :],
                                      K["ident"][0:TE, 0:TE])
                mm.then_inc(score_turned, 1)

            over_groups(pe, body)


def attention_weights(nc, K, V):
    E = V["edges"]
    NHEAD = V["score_t"].shape[0]
    with ExitStack() as ctx:
        def sb(name, shape, dt=F32):
            return ctx.enter_context(nc.sbuf_tensor(name, shape, dt))

        fence = sb("aw_fence", [NHEAD, E + 1])
        upto = sb("aw_upto", [NHEAD, E])
        top = sb("aw_top", [NHEAD, E])
        sem = ctx.enter_context(signals(nc, "aw"))
        step = sem("step")
        done = sem("done")
        block = ctx.enter_context(nc.Block())
        score = V["score_t"]

        @block.vector
        def _(dve):
            dve.memset(fence[:, E:E + 1], NEG)
            dve.tensor_scalar(fence[:, 0:E], K["same"][0:NHEAD, :], -1.0, -NEG, ALU.add, ALU.mult).then_inc(step, 1)
            dve.wait_ge(step, 1)
            dve.tensor_tensor_scan(upto[:, :], fence[:, 0:E], score[:, :], NEG, ALU.add, ALU.max).then_inc(step, 1)
            dve.wait_ge(step, 2)
            dve.tensor_tensor_scan(top[:, ::-1], fence[:, E:0:-1], upto[:, ::-1], NEG, ALU.add, ALU.max) \
               .then_inc(step, 1)
            dve.wait_ge(step, 3)
            dve.tensor_tensor(upto[:, :], score[:, :], top[:, :], ALU.subtract).then_inc(step, 1)

        @block.scalar
        def _(act):
            act.wait_ge(step, 4)
            act.activation(score[:, :], upto[:, :], ACT.Exp).then_inc(done, 1)
            act.wait_ge(done, 1)


def message_scores(nc, K, A, V, rec_d, x3_dram):
    NG = V["edges"] // GE
    N = x3_dram.shape[0]
    DM = A["L3_gnn_W_forward"].shape[0]
    NHEAD = A["L3_gnn_attn_forward"].shape[1]
    WS = DM + NHEAD
    with ExitStack() as ctx:
        def sb(name, shape, dt=F32):
            return ctx.enter_context(nc.sbuf_tensor(name, shape, dt))

        def pb(name, shape, dt=F32):
            return ctx.enter_context(nc.psum_tensor(name, shape, dt))

        sem = ctx.enter_context(signals(nc, "ms"))
        w = sb("ms_w", [DM, 2, D])
        attn = sb("ms_attn", [NHEAD, DM])
        attn_t = sb("ms_attn_t", [DM, NHEAD])
        w_t = sb("ms_w_t", [P, DC, 2, WS])
        rec = sb("ms_rec", [TE, 2, G, RD])
        way = sb("ms_way", [TE, 2, G, 2])
        idx = sb("ms_idx", [TE, 2, G], I32)
        x = sb("ms_x", [TE, 2, G, D])
        h = sb("ms_h", [TE, 2, G, D])
        h_t = sb("ms_h_t", [P, 2, DC, GE])
        scaled = sb("ms_scaled", [TE, 2, 2, G, WS])
        score = sb("ms_score", [TE, 2, G, NHEAD])
        score_l = sb("ms_score_l", [TE, 2, G, NHEAD])
        p_a = pb("ms_p_a", [P, 512])
        p_t = [pb(f"ms_p_t{c}", [P, 512]) for c in range(DC)]
        p_m = [pb(f"ms_p_m{c}", [TE, 2, 2, P]) for c in range(2)]
        norm = Norm(nc, ctx, "ms", sem, TE, G, K["eps"])

        w_in = sem("w_in")
        attn_turned = sem("attn_turned")
        attn_ready = sem("attn_ready")
        w_turned = sem("w_turned")
        w_ready = sem("w_ready")
        rec_in = [sem(f"rec_in{b}") for b in range(2)]
        x_in = [sem(f"x_in{b}") for b in range(2)]
        idx_ready = sem("idx_ready")
        h_ready = sem("h_ready")
        turned = sem("turned")
        h_t_ready = sem("h_t_ready")
        m_mm = sem("m_mm")
        m_scaled = sem("m_scaled")
        score_summed = sem("score_summed")
        score_ready = sem("score_ready")
        score_turned = sem("score_turned")
        score_kept = sem("score_kept")
        passed = sem("passed")
        block = ctx.enter_context(nc.Block())

        def over_groups(eng, body):
            with eng.Fori(0, NG // 2 - 1) as i:
                for b in range(2):
                    body(i * 2 + b, i, b, True)
            for b in range(2):
                body(NG - 2 + b, NG // 2 - 1, b, False)

        @block.sync
        def _(sp):
            sp.dma_start(w[:, 0, :], A["L3_gnn_W_forward"]).then_inc(w_in, 16)
            sp.dma_start(w[:, 1, :], A["L3_gnn_W_reverse"]).then_inc(w_in, 16)
            sp.dma_start(attn[:, :], A["L3_gnn_attn_forward"].rearrange("a h f -> (a h) f")).then_inc(w_in, 16)
            for b in range(2):
                sp.dma_start(rec[:, b, :, :], rows_of(rec_d, b, G, TE)).then_inc(rec_in[b], 16)

            def body(g, i, b, more):
                if more:
                    sp.wait_ge(idx_ready, g + 1)
                    sp.dma_start(rec[:, b, :, :], rows_of(rec_d, g + 2, G, TE)).then_inc(rec_in[b], 16)

            over_groups(sp, body)

        @block.gpsimd
        def _(pool):
            def fetch(g, b):
                pool.wait_ge(idx_ready, g + 1)
                pool.sem_inc(passed, 1)
                for j in range(G):
                    pool.indirect_dma_start(x[:, b, j, :], None, x3_dram[:, :], IOA(idx[:, b, j:j + 1], 0),
                                            bounds_check=N - 1, oob_is_err=False).then_inc(x_in[b], 16)

            def body(g, i, b, more):
                if more:
                    fetch(g + 2, b)

            for b in range(2):
                fetch(b, b)
            over_groups(pool, body)

        @block.vector
        def _(dve):
            def take(g, i, b):
                dve.wait_ge(rec_in[b], (i + 1) * 16)
                dve.tensor_copy(way[:, b, :, :], rec[:, b, :, D_A2:D_A2 + 2])
                dve.tensor_copy(idx[:, b, :], rec[:, b, :, D_SRC]).then_inc(idx_ready, 1)

            for b in range(2):
                take(b, 0, b)
            dve.wait_ge(attn_turned, 1)
            dve.tensor_copy(attn_t[:, :], p_a[0:DM, 0:NHEAD]).then_inc(attn_ready, 1)
            dve.wait_ge(w_turned, 1)
            for k in range(DC):
                ins = dve.tensor_copy(w_t[:, k, :, :].rearrange("p s n -> p (s n)"), p_t[k][:, 0:2 * WS])
            ins.then_inc(w_ready, 1)

            def body(g, i, b, more):
                dve.wait_ge(x_in[b], (i + 1) * (16 * G))
                norm.statistics(dve, g, b, x[:, b, :, :])
                norm.scales(dve, g, b)
                dve.wait_ge(turned, g + 1)
                dve.tensor_copy(h_t[:, b, 0, :], p_t[0][:, 0:GE]).then_inc(h_t_ready, 1)
                dve.wait_ge(m_scaled, g * 2 + 4)
                dve.tensor_tensor(V["proj"][:, bass.ds(g * G, G), 0:DM], scaled[:, b, 0, :, 0:DM],
                                  scaled[:, b, 1, :, 0:DM], ALU.add)
                dve.tensor_tensor(score[:, b, :, :], scaled[:, b, 0, :, DM:WS], scaled[:, b, 1, :, DM:WS],
                                  ALU.add).then_inc(score_summed, 1)
                dve.wait_ge(score_summed, g + 1)
                dve.scalar_tensor_tensor(out=score_l[:, b, :, :], in0=score[:, b, :, :], scalar=0.2,
                                         in1=score[:, b, :, :], op0=ALU.mult, op1=ALU.max).then_inc(score_ready, 1)
                if more:
                    take(g + 2, i + 1, b)

            over_groups(dve, body)

        @block.scalar
        def _(act):
            def body(g, i, b, more):
                norm.root(act, g, b)
                norm.rows_out(act, g, b, h[:, b, :, :], x[:, b, :, :]).then_inc(h_ready, 1)
                act.wait_ge(turned, g + 1)
                act.copy(h_t[:, b, 1, :], p_t[1][:, 0:GE]).then_inc(h_t_ready, 1)
                act.wait_ge(idx_ready, g + 1)
                for c in range(2):
                    act.wait_ge(m_mm, g * 2 + c + 1)
                    for jj in range(2):
                        for s in range(2):
                            ins = act.activation(scaled[:, b, s, 2 * c + jj, :], p_m[c][:, jj, s, 0:WS],
                                                 ACT.Identity, bias=0.0, scale=way[:, b, 2 * c + jj, s:s + 1])
                    ins.then_inc(m_scaled, 1)
                act.wait_ge(score_turned, g + 1)
                act.copy(V["score_t"][0:NHEAD, bass.ds(g * GE, GE)], p_a[0:NHEAD, 0:GE]).then_inc(score_kept, 1)

            over_groups(act, body)

        @block.tensor
        def _(pe):
            pe.wait_ge(w_in, 48)
            pe.transpose(p_a[0:DM, 0:NHEAD], attn[:, :], K["ident"][0:NHEAD, 0:NHEAD]).then_inc(attn_turned, 1)
            for k in range(DC):
                for s in range(2):
                    pe.transpose(p_t[k][:, s * WS:s * WS + DM], w[:, s, k * P:(k + 1) * P], K["ident"][0:DM, 0:DM])
            pe.wait_ge(attn_ready, 1)
            for k in range(DC):
                for s in range(2):
                    mm = pe.matmul(p_t[k][:, s * WS + DM:(s + 1) * WS], w[:, s, k * P:(k + 1) * P], attn_t[:, :],
                                   start=True, stop=True)
            mm.then_inc(w_turned, 1)
            pe.wait_ge(w_ready, 1)
            pe.sem_inc(h_t_ready, 2)
            pe.sem_inc(m_scaled, 2)
            pe.sem_inc(score_kept, 1)

            def body(g, i, b, more):
                pe.wait_ge(h_ready, g + 1)
                pe.wait_ge(h_t_ready, g * 2 + 2)
                for c in range(DC):
                    for j in range(G):
                        mm = pe.transpose(p_t[c][:, j * TE:(j + 1) * TE], h[:, b, j, c * P:(c + 1) * P],
                                          K["ident"][0:TE, 0:TE])
                mm.then_inc(turned, 1)
                pe.wait_ge(h_t_ready, g * 2 + 4)
                for c in range(2):
                    pe.wait_ge(m_scaled, g * 2 + c + 1)
                    for jj in range(2):
                        j = 2 * c + jj
                        for k in range(DC):
                            mm = pe.matmul(p_m[c][:, jj, :, 0:WS], h_t[:, b, k, j * TE:(j + 1) * TE],
                                           w_t[:, k, :, :], start=(k == 0), stop=(k == DC - 1))
                    mm.then_inc(m_mm, 1)
                pe.wait_ge(score_ready, g + 1)
                pe.wait_ge(score_kept, g + 1)
                for j in range(G):
                    mm = pe.transpose(p_a[0:NHEAD, j * TE:(j + 1) * TE], score_l[:, b, j, :],
                                      K["ident"][0:TE, 0:TE])
                mm.then_inc(score_turned, 1)

            over_groups(pe, body)


def message_weights(nc, V, NHEAD):
    with ExitStack() as ctx:
        top = ctx.enter_context(nc.sbuf_tensor("mw_top", [NHEAD, 2], F32))
        sem = ctx.enter_context(signals(nc, "mw"))
        step = sem("step")
        done = sem("done")
        block = ctx.enter_context(nc.Block())
        score = V["score_t"][0:NHEAD, :]

        @block.vector
        def _(dve):
            dve.tensor_reduce(top[:, 0:1], score, AX.X, ALU.max).then_inc(step, 1)
            dve.wait_ge(step, 1)
            dve.tensor_scalar(top[:, 1:2], top[:, 0:1], -1.0, None, ALU.mult).then_inc(step, 1)

        @block.scalar
        def _(act):
            act.wait_ge(step, 2)
            act.activation(score, score, ACT.Exp, bias=top[:, 1:2], scale=1.0).then_inc(done, 1)
            act.wait_ge(done, 1)


def attention_sums(nc, K, V, name, NHEAD, per_head, guard, keep, rec_d, out):
    N = out.shape[0]
    NG = V["edges"] // GE
    DH = D // NHEAD
    with ExitStack() as ctx:
        def sb(what, shape, dt=F32):
            return ctx.enter_context(nc.sbuf_tensor(f"{name}_{what}", shape, dt))

        def pb(what, shape, dt=F32):
            return ctx.enter_context(nc.psum_tensor(f"{name}_{what}", shape, dt))

        sem = ctx.enter_context(signals(nc, name))
        rec = sb("rec", [TE, 2, G, RD])
        idx = sb("idx", [TE, 2, G], I32)
        ex_t = sb("ex_t", [NHEAD, 2, GE])
        ex = sb("ex", [TE, 2, G, NHEAD])
        m = sb("m", [TE, 2, G, D])
        run = sb("run", [P, 2, DC, GE])
        den_t = sb("den_t", [NHEAD, 2, GE])
        den = sb("den", [TE, 2, G, NHEAD])
        rows = sb("rows", [TE, 2, G, D])
        p_e = pb("p_e", [TE, 512])
        p_d = pb("p_d", [TE, 512])
        p_t = [pb(f"p_t{c}", [P, 512]) for c in range(DC)]
        p_r = [pb(f"p_r{c}", [TE, 2, D]) for c in range(2)]

        rec_in = [sem(f"rec_in{b}") for b in range(2)]
        put = [sem(f"put{b}") for b in range(2)]
        idx_ready = sem("idx_ready")
        ex_t_ready = sem("ex_t_ready")
        pe_passed = sem("pe_passed")
        ex_turned = sem("ex_turned")
        ex_ready = sem("ex_ready")
        m_ready = sem("m_ready")
        turned = sem("turned")
        run_ready = sem("run_ready")
        den_ready = sem("den_ready")
        den_turned = sem("den_turned")
        den_read = sem("den_read")
        den_done = sem("den_done")
        rows_turned = sem("rows_turned")
        rows_scaled = sem("rows_scaled")
        rows_ready = sem("rows_ready")
        rows_kept = sem("rows_kept")
        passed = sem("passed")
        block = ctx.enter_context(nc.Block())

        def over_groups(eng, body):
            with eng.Fori(0, NG // 2) as i:
                for b in range(2):
                    body(i * 2 + b, i, b)

        @block.sync
        def _(sp):
            sp.sem_inc(idx_ready, 2)

            def body(g, i, b):
                sp.wait_ge(idx_ready, g + 1)
                sp.dma_start(rec[:, b, :, :], rows_of(rec_d, g, G, TE)).then_inc(rec_in[b], 16)

            over_groups(sp, body)

        @block.gpsimd
        def _(pool):
            for b in range(2):
                open_slot(pool, K, put[b], 16 * G)

            def body(g, i, b):
                pool.wait_ge(rows_ready, g + 1)
                pool.sem_inc(passed, 1)
                for j in range(G):
                    pool.indirect_dma_start(out[:, :], IOA(idx[:, b, j:j + 1], 0), rows[:, b, j, :], None,
                                            bounds_check=N - 1, oob_is_err=False).then_inc(put[b], 16)

            over_groups(pool, body)
            for b in range(2):
                pool.wait_ge(put[b], 16 * G * (NG // 2 + 1))

        @block.vector
        def _(dve):
            dve.memset(den_t[:, 1, GE - 1:GE], 0.0).then_inc(den_ready, 1)
            dve.memset(run[:, 1, :, GE - 1], 0.0).then_inc(run_ready, 2)

            def weigh(g, b):
                dve.wait_ge(ex_ready, g + 2)
                source = V["proj"][:, bass.ds(g * G, G), 0:D if per_head else DH]
                source = source.rearrange("p t (h d) -> p t h d", h=NHEAD) if per_head else \
                    source.unsqueeze(2).to_broadcast([TE, G, NHEAD, DH])
                dve.tensor_tensor(m[:, b, :, :].rearrange("p t (h d) -> p t h d", h=NHEAD), source,
                                  ex[:, b, :, :].unsqueeze(3).to_broadcast([TE, G, NHEAD, DH]),
                                  ALU.mult).then_inc(m_ready, 1)

            def body(g, i, b):
                weigh(g, b)
                dve.wait_ge(rec_in[b], (i + 1) * 16)
                dve.wait_ge(put[b], (i + 1) * (16 * G))
                dve.tensor_copy(idx[:, b, :], rec[:, b, :, D_PUT]).then_inc(idx_ready, 1)
                dve.wait_ge(den_ready, g + 1)
                dve.tensor_tensor_scan(den_t[:, b, :], K["same"][0:NHEAD, bass.ds(g * GE, GE)], ex_t[:, b, :],
                                       den_t[:, 1 - b, GE - 1:GE], ALU.mult, ALU.add).then_inc(den_ready, 1)
                dve.wait_ge(turned, g + 1)
                dve.wait_ge(run_ready, g * 2 + 2)
                for c in range(DC):
                    dve.tensor_tensor_scan(run[:, b, c, :], K["same"][:, bass.ds(g * GE, GE)], p_t[c][:, 0:GE],
                                           run[:, 1 - b, c, GE - 1:GE], ALU.mult, ALU.add).then_inc(run_ready, 1)
                dve.wait_ge(den_turned, g + 1)
                dve.tensor_scalar(den[:, b, :, :].rearrange("p t h -> p (t h)"), p_d[:, 0:G * NHEAD], guard[1], None,
                                  guard[0]).then_inc(den_read, 1)
                dve.wait_ge(den_read, g + 2)
                dve.reciprocal(den[:, b, :, :], den[:, b, :, :]).then_inc(den_done, 1)
                dve.wait_ge(den_done, g + 1)
                dve.wait_ge(rows_kept, g + 1)
                for c in range(2):
                    dve.wait_ge(rows_turned, g * 2 + c + 1)
                    dve.tensor_tensor(rows[:, b, 2 * c:2 * c + 2, :].rearrange("p t (h d) -> p t h d", h=NHEAD),
                                      p_r[c][:, :, :].rearrange("p t (h d) -> p t h d", h=NHEAD),
                                      den[:, b, 2 * c:2 * c + 2, :].unsqueeze(3).to_broadcast([TE, 2, NHEAD, DH]),
                                      ALU.mult).then_inc(rows_scaled, 1)
                dve.wait_ge(rows_scaled, g * 2 + 4)
                dve.tensor_tensor(rows[:, b, :, :], rows[:, b, :, :], V["base"][:, bass.ds(g * G, G), :], ALU.add) \
                   .then_inc(rows_ready, 1)

            over_groups(dve, body)

        @block.scalar
        def _(act):
            act.sem_inc(rows_kept, 2)

            def body(g, i, b):
                act.copy(ex_t[:, b, :], V["score_t"][0:NHEAD, bass.ds(g * GE, GE)]).then_inc(ex_t_ready, 1)
                act.wait_ge(ex_turned, g + 1)
                act.copy(ex[:, b, :, :].rearrange("p t h -> p (t h)"), p_e[:, 0:G * NHEAD]).then_inc(ex_ready, 1)
                act.wait_ge(rows_ready, g + 1)
                if keep:
                    act.copy(V["base"][:, bass.ds(g * G, G), :].rearrange("p t d -> p (t d)"),
                             rows[:, b, :, :].rearrange("p t d -> p (t d)")).then_inc(rows_kept, 1)
                else:
                    act.sem_inc(rows_kept, 1)

            over_groups(act, body)

        @block.tensor
        def _(pe):
            pe.sem_inc(ex_ready, 1)
            pe.sem_inc(den_read, 1)
            pe.sem_inc(rows_scaled, 2)

            def body(g, i, b):
                pe.wait_ge(ex_t_ready, g + 1)
                pe.wait_ge(ex_ready, g + 1)
                pe.sem_inc(pe_passed, 1)
                for j in range(G):
                    mm = pe.transpose(p_e[:, j * NHEAD:(j + 1) * NHEAD], ex_t[:, b, j * TE:(j + 1) * TE],
                                      K["ident"][0:NHEAD, 0:NHEAD])
                mm.then_inc(ex_turned, 1)
                pe.wait_ge(m_ready, g + 1)
                pe.wait_ge(run_ready, g * 2 + 2)
                for c in range(DC):
                    for j in range(G):
                        mm = pe.transpose(p_t[c][:, j * TE:(j + 1) * TE], m[:, b, j, c * P:(c + 1) * P],
                                          K["ident"][0:TE, 0:TE])
                mm.then_inc(turned, 1)
                pe.wait_ge(den_ready, g + 2)
                pe.wait_ge(den_read, g + 1)
                pe.sem_inc(pe_passed, 1)
                for j in range(G):
                    mm = pe.transpose(p_d[:, j * NHEAD:(j + 1) * NHEAD], den_t[:, b, j * TE:(j + 1) * TE],
                                      K["ident"][0:NHEAD, 0:NHEAD])
                mm.then_inc(den_turned, 1)
                pe.wait_ge(run_ready, g * 2 + 4)
                for c in range(2):
                    pe.wait_ge(rows_scaled, g * 2 + c + 1)
                    for jj in range(2):
                        j = 2 * c + jj
                        for k in range(DC):
                            mm = pe.transpose(p_r[c][:, jj, k * P:(k + 1) * P], run[:, b, k, j * TE:(j + 1) * TE],
                                              K["ident"][:, :])
                    mm.then_inc(rows_turned, 1)

            over_groups(pe, body)


def gnn(nc, A, out):
    N = A["x"].shape[0]
    E = A["src"].shape[0]
    NT = E // TE
    NH = -(-N // LO) + 1
    table = nc.dram_tensor("node_table", [NH * LO, 4], F32).ap()
    agg0 = nc.dram_tensor("agg0", [N, D], F32).ap()
    rec_d = nc.dram_tensor("rec_by_dst", [E, RD], F32).ap()
    rec_c = nc.dram_tensor("rec_by_node", [2 * E, RC], F32).ap()
    x1 = nc.dram_tensor("x1_by_node", [N, D], F32).ap()
    x2 = nc.dram_tensor("x2_by_place", [2 * E, D], F32).ap()
    msg = nc.dram_tensor("messages0", [E, D], F32).ap()
    with ExitStack() as ctx:
        def sb(name, shape, dt=F32):
            return ctx.enter_context(nc.sbuf_tensor(name, shape, dt))

        K = {
            "token": sb("token", [1, 32, 4]), "token_n": -1,
            "ident": sb("ident", [P, P]), "iota_p": sb("iota_p", [P, 1]), "eps": sb("eps_col", [P, 1]),
            "dst_col": sb("dst_col", [TE, NT + 2 * G], I32), "src_col": sb("src_col", [TE, NT + 2 * G], I32),
            "same": sb("same_dst", [P, E], BF16),
            "ord": sb("ord", [TE, NT, 2]),
        }
        constants(nc, K)
        rank_edges(nc, K, A["dst"], A["src"], table, agg0)
        build_records(nc, K, A, table, rec_d, rec_c)
        edge_messages(nc, K, A, msg)
        aggregate_messages(nc, K, msg, rec_d, agg0)
        node_network(nc, K, A, agg0, x1, out)
        relation_layer(nc, K, A, rec_c, x1, x2, out)
        H2, H3 = A["L2_gnn_a_src"].shape[0], A["L3_gnn_attn_forward"].shape[1]
        V = {
            "edges": E, "proj": sb("proj", [TE, NT, D + H2]), "base": sb("base", [TE, NT, D]),
            "score_t": sb("score_t", [max(H2, H3), E]),
        }
        attention_scores(nc, K, A, V, rec_d, x2)
        attention_weights(nc, K, V)
        attention_sums(nc, K, V, "a2", H2, True, (ALU.max, 1e-10), True, rec_d, out)
        message_scores(nc, K, A, V, rec_d, out)
        message_weights(nc, V, H3)
        attention_sums(nc, K, V, "a3", H3, False, (ALU.add, 1e-10), False, rec_d, out)


_INS = ['x', 'src', 'dst', 'edge_attr_2', 'edge_attr_256', 'edge_attr_3', 'edge_type_11',
        'L0_gnn_We1', 'L0_gnn_be1', 'L0_gnn_We2', 'L0_gnn_be2', 'L0_gnn_Wn1', 'L0_gnn_bn1', 'L0_gnn_Wn2',
        'L0_gnn_bn2', 'L0_gnn_eps', 'L1_gnn_weight', 'L1_gnn_bias', 'L1_gnn_alpha', 'L2_gnn_W', 'L2_gnn_a_src',
        'L2_gnn_a_dst', 'L2_gnn_edge_W', 'L2_gnn_edge_b', 'L2_gnn_bias', 'L3_gnn_W_forward', 'L3_gnn_W_reverse',
        'L3_gnn_attn_forward']


def kernel(**inputs):
    import numpy as _np
    import concourse.bacc as _bacc
    from concourse import mybir as _mybir
    from concourse.bass_utils import run_bass_kernel_spmd as _run

    nc = _bacc.Bacc("TRN2", target_bir_lowering=False, num_devices=1)
    arrays, args = {}, {}
    for name in _INS:
        a = _np.ascontiguousarray(inputs[name])
        arrays[f"in_{name}"] = a
        args[name] = nc.dram_tensor(f"in_{name}", a.shape, _mybir.dt.from_np(a.dtype), kind="ExternalInput").ap()
    out = nc.dram_tensor("out_x", inputs["x"].shape, _mybir.dt.float32, kind="ExternalOutput").ap()
    gnn(nc, args, out)
    r = _run(nc, [arrays], core_ids=[0])
    return r.results[0]["out_x"]
```

```python
from contextlib import ExitStack, contextmanager

import concourse.bass as bass
from concourse import mybir

F32 = mybir.dt.float32
BF16 = mybir.dt.bfloat16
I32 = mybir.dt.int32
ALU = mybir.AluOpType
ACT = mybir.ActivationFunctionType
AX = mybir.AxisListType
IOA = bass.IndirectOffsetOnAxis

P = 128
D = 256
DC = D // P
HID = 512
HC = HID // P
TE = 125
G = 4
GP = 2 * G
GE = G * TE
LO = 256
EPS = 1e-5
SKIP = 1 << 15
NEG = -1.0e38

RD = 16
D_SRC, D_PUT, D_SLOT_S, D_SLOT_D, D_EDGE, D_SAME, D_A2, D_A3, D_ONE = 0, 1, 2, 3, 4, 5, 6, 8, 11
RC = 8
C_NODE, C_PEER, C_PUT, C_W, C_SAME = 0, 1, 2, 3, 4


class Step:

    def __init__(self, i, r, unroll, n):
        self.i, self.r, self.unroll, self.n = i, r, unroll, n
        self.g = i * unroll + r

    def ahead(self, k):
        r = self.r + k
        return Step(self.i + r // self.unroll, r % self.unroll, self.unroll, self.n)

    def exists(self):
        return not isinstance(self.g, int) or self.g < self.n

    def slot(self, ring):
        return self.r % ring

    def round(self, ring):
        return self.i * (self.unroll // ring) + self.r // ring + 1


def over_groups(eng, n, unroll, peel, body):
    with eng.Fori(0, (n - peel) // unroll) as i:
        for r in range(unroll):
            body(Step(i, r, unroll, n))
    for g in range(n - peel, n):
        body(Step(g // unroll, g % unroll, unroll, n))


@contextmanager
def signals(nc, stage):
    taken = []

    def sem(what):
        taken.append(nc.alloc_semaphore(f"{stage}_{what}"))
        return taken[-1]

    yield sem
    nc.clear_and_free_semaphores(taken)
    nc.all_engine_barrier()


def constants(nc, K):
    with ExitStack() as ctx:
        sem = ctx.enter_context(signals(nc, "const"))
        filled = sem("filled")
        done = sem("done")
        block = ctx.enter_context(nc.Block())

        @block.gpsimd
        def _(pool):
            pool.memset(K["ident"][:, :], 0.0).then_inc(filled, 1)
            pool.wait_ge(filled, 1)
            pool.affine_select(out=K["ident"][:, :], in_=K["ident"][:, :], compare_op=ALU.not_equal, fill=1.0,
                               base=0, pattern=[[-1, P]], channel_multiplier=1).then_inc(done, 1)
            pool.iota(K["iota_p"][:, :], [[0, 1]], base=0, channel_multiplier=1,
                      allow_small_or_imprecise_dtypes=True).then_inc(done, 1)
            pool.memset(K["eps"][:, :], EPS).then_inc(done, 1)
            pool.wait_ge(done, 3)


def rank_edges(nc, K, dst, src, table, zero_table):
    E = dst.shape[0]
    NT = E // TE
    NH = table.shape[0] // LO
    S = 2
    with ExitStack() as ctx:
        def sb(name, shape, dt=F32):
            return ctx.enter_context(nc.sbuf_tensor(name, shape, dt))

        def pb(name, shape, dt=F32):
            return ctx.enter_context(nc.psum_tensor(name, shape, dt))

        sem = ctx.enter_context(signals(nc, "rk"))
        key_row = [sb(f"rk_key_row{s}", [P, E], I32) for s in range(S)]
        hi_row = [sb(f"rk_hi_row{s}", [NH, E], I32) for s in range(S)]
        key40 = sb("rk_key40", [NT, S, TE], I32)
        part40 = sb("rk_part40", [NT, 2, S, TE], I32)
        key_f = sb("rk_key_f", [NT, 3, S, TE])
        key_col = sb("rk_key_col", [TE, 3, S, NT])
        iota_hi = sb("rk_iota_hi", [P, NH], BF16)
        iota_lo = sb("rk_iota_lo", [P, LO], BF16)
        before = sb("rk_before", [TE, TE])
        above = sb("rk_above", [NH, NH])
        ones = sb("rk_ones", [NH, LO])
        zero_b = sb("rk_zero_b", [P, LO], BF16)
        hot_hi = sb("rk_hot_hi", [TE, 8, NH], BF16)
        hot_lo = sb("rk_hot_lo", [TE, 8, LO], BF16)
        hot_hi_t = sb("rk_hot_hi_t", [NH, 8, TE])
        run = sb("rk_run", [NH, 4, LO])
        junk_t = sb("rk_junk_t", [TE, 8, TE])
        junk_r = sb("rk_junk_r", [TE, 8, LO])
        in_tile = sb("rk_in_tile", [TE, 8])
        in_run = sb("rk_in_run", [TE, 8])
        hist = sb("rk_hist", [NH, S, LO])
        incl = sb("rk_incl", [NH, S, LO])
        total = sb("rk_total", [NH, S])
        carry = sb("rk_carry", [NH, S])
        tab = sb("rk_tab", [NH, LO, 4])
        NZ = 25
        zeros = sb("rk_zeros", [80, NZ * D])
        p_hist = [pb(f"rk_p_hist{s}", [NH, 512]) for s in range(S)]
        p_look = [pb(f"rk_p_look{m}", [TE, 512]) for m in range(4)]
        p_misc = pb("rk_p_misc", [P, 512])

        row_in = [sem(f"row_in{s}") for s in range(S)]
        key_in = sem("key_in")
        const_a = sem("const_a")
        const_ready = sem("const_ready")
        zeros_ready = sem("zeros_ready")
        step = sem("step")
        keys_split = sem("keys_split")
        keys_turned = sem("keys_turned")
        hist_zero = sem("hist_zero")
        hots_ready = sem("hots_ready")
        run_ready = sem("run_ready")
        looked_up = sem("looked_up")
        look_read = sem("look_read")
        hist_added = sem("hist_added")
        counted = sem("counted")
        totals_ready = sem("totals_ready")
        carry_ready = sem("carry_ready")
        tab_ready = sem("tab_ready")
        stored = sem("stored")
        block = ctx.enter_context(nc.Block())
        keys = (dst, src)

        @block.sync
        def _(sp):
            for s in range(S):
                sp.dma_start(key40[:, s, :], keys[s].rearrange("(t p) -> t p", p=TE)).then_inc(key_in, 16)
            for s in range(S):
                sp.dma_start(key_row[s][:, :], keys[s].rearrange("(a e) -> a e", a=1).to_broadcast([P, E])) \
                    .then_inc(row_in[s], 16)
            sp.wait_ge(zeros_ready, 1)
            rows = zero_table.rearrange("(p r) d -> p (r d)", p=80)
            NR = zero_table.shape[0] // 80 // NZ
            for r in range(NR):
                sp.dma_start(rows[:, r * NZ * D:(r + 1) * NZ * D], zeros[:, :]).then_inc(stored, 16)
            sp.wait_ge(tab_ready, 1)
            sp.dma_start(table.rearrange("(h l) c -> h (l c)", l=LO),
                         tab[:, :, :].rearrange("h l c -> h (l c)")).then_inc(stored, 16)
            sp.wait_ge(stored, 16 * (NR + 1))

        @block.gpsimd
        def _(pool):
            pool.memset(zeros[:, :], 0.0).then_inc(zeros_ready, 1)
            pool.memset(K["src_col"][:, NT:], 0)
            pool.memset(K["dst_col"][:, NT:], 0)
            pool.iota(iota_hi[:, :], [[1, NH]], base=0, channel_multiplier=0,
                      allow_small_or_imprecise_dtypes=True).then_inc(const_ready, 1)
            pool.iota(iota_lo[:, :], [[1, LO]], base=0, channel_multiplier=0,
                      allow_small_or_imprecise_dtypes=True).then_inc(const_ready, 1)
            pool.memset(before[:, :], 1.0).then_inc(const_a, 1)
            pool.memset(above[:, :], 1.0).then_inc(const_a, 1)
            pool.memset(ones[:, :], 1.0).then_inc(const_ready, 1)
            pool.memset(zero_b[:, :], 0.0).then_inc(const_ready, 1)
            pool.wait_ge(const_a, 2)
            pool.affine_select(out=before[:, :], in_=before[:, :], compare_op=ALU.is_gt, fill=0.0,
                               base=0, pattern=[[-1, TE]], channel_multiplier=1).then_inc(const_ready, 1)
            pool.affine_select(out=above[:, :], in_=above[:, :], compare_op=ALU.is_gt, fill=0.0,
                               base=0, pattern=[[1, NH]], channel_multiplier=-1).then_inc(const_ready, 1)

        @block.vector
        def _(dve):
            dve.wait_ge(key_in, 16 * S)
            dve.tensor_scalar(part40[:, 0, :, :], key40[:, :, :], 8, None, ALU.logical_shift_right)
            dve.tensor_scalar(part40[:, 1, :, :], key40[:, :, :], LO - 1, None, ALU.bitwise_and).then_inc(step, 1)
            dve.tensor_copy(key_f[:, 0, :, :], key40[:, :, :])
            dve.wait_ge(step, 1)
            dve.tensor_copy(key_f[:, 1:3, :, :].rearrange("t a s e -> t (a s e)"),
                            part40[:, :, :, :].rearrange("t a s e -> t (a s e)")).then_inc(keys_split, 1)
            dve.wait_ge(keys_turned, 1)
            dve.tensor_copy(key_col[:, :, :, :].rearrange("p a s t -> p (a s t)"),
                            p_misc[0:TE, 0:3 * S * NT]).then_inc(step, 1)
            dve.tensor_copy(K["dst_col"][:, 0:NT], p_misc[0:TE, 0:NT])
            dve.tensor_copy(K["src_col"][:, 0:NT], p_misc[0:TE, NT:2 * NT])
            for s in range(S):
                dve.wait_ge(row_in[s], 16)
                dve.tensor_scalar(hi_row[s][:, :], key_row[s][0:NH, :], 8, None,
                                  ALU.logical_shift_right).then_inc(step, 1)
            dve.wait_ge(step, 4)
            dve.wait_ge(const_ready, 6)
            dve.sem_inc(look_read, 4)
            dve.sem_inc(hist_added, 8)
            with dve.Fori(0, NT // G) as i:
                for m in range(8):
                    j, s = m // 2, m % 2
                    t = i * G + j
                    dve.wait_ge(hist_added, i * 8 + m + 1)
                    dve.tensor_scalar(hot_hi[:, m, :], iota_hi[0:TE, :], key_col[:, 1, s, bass.ds(t, 1)], None,
                                      ALU.is_equal)
                    dve.tensor_scalar(hot_lo[:, m, :], iota_lo[0:TE, :], key_col[:, 2, s, bass.ds(t, 1)], None,
                                      ALU.is_equal)
                    dve.tensor_scalar(hot_hi_t[:, m, :], hi_row[s][:, bass.ds(t * TE, TE)], K["iota_p"][0:NH, 0:1],
                                      None, ALU.is_equal).then_inc(hots_ready, 1)
                    dve.scalar_tensor_tensor(out=junk_t[:, m, :], in0=key_row[s][0:TE, bass.ds(t * TE, TE)],
                                             scalar=key_col[:, 0, s, bass.ds(t, 1)], in1=before[:, :],
                                             op0=ALU.is_equal, op1=ALU.mult, accum_out=in_tile[:, m:m + 1])
                for m in range(8):
                    dve.wait_ge(looked_up, i * 8 + m + 1)
                    ins = dve.scalar_tensor_tensor(out=junk_r[:, m, :], in0=p_look[m % 4][:, 0:LO], scalar=1.0,
                                                   in1=hot_lo[:, m, :], op0=ALU.mult, op1=ALU.mult,
                                                   accum_out=in_run[:, m:m + 1])
                    ins.then_inc(look_read, 1)
                dve.wait_ge(look_read, i * 8 + 12)
                dve.tensor_tensor(K["ord"][:, bass.ds(i * G, G), :].rearrange("p t s -> p (t s)"), in_tile[:, :],
                                  in_run[:, :], ALU.add).then_inc(counted, 1)
                dve.wait_ge(counted, i + 1)
            dve.wait_ge(hist_added, 2 * NT + 8)
            for s in range(S):
                dve.tensor_copy(hist[:, s, :], p_hist[s][:, 0:LO]).then_inc(step, 1)
            dve.wait_ge(step, 6)
            for s in range(S):
                dve.tensor_tensor_scan(incl[:, s, :], ones[:, :], hist[:, s, :], 0.0, ALU.mult, ALU.add) \
                   .then_inc(step, 1)
            dve.wait_ge(step, 8)
            dve.tensor_copy(total[:, :], incl[:, :, LO - 1]).then_inc(totals_ready, 1)
            dve.wait_ge(carry_ready, 1)
            dve.tensor_copy(carry[:, :], p_misc[0:NH, 0:S]).then_inc(step, 1)
            dve.wait_ge(step, 9)
            for s in range(S):
                dve.tensor_scalar(tab[:, :, 2 * s + 1], incl[:, s, :], carry[:, s:s + 1], None, ALU.add) \
                   .then_inc(step, 1)
            dve.wait_ge(step, 11)
            dve.tensor_tensor(tab[:, :, 0], tab[:, :, 1], hist[:, 0, :], ALU.subtract)
            dve.tensor_tensor(tab[:, :, 2], tab[:, :, 3], hist[:, 1, :], ALU.subtract).then_inc(tab_ready, 1)

        @block.scalar
        def _(act):
            act.wait_ge(hist_zero, 1)
            with act.Fori(0, NT // G) as i:
                for m in range(8):
                    act.wait_ge(hist_added, i * 8 + m + 7)
                    act.copy(run[:, m % 4, :], p_hist[m % 2][:, 0:LO]).then_inc(run_ready, 1)

        @block.tensor
        def _(pe):
            pe.wait_ge(keys_split, 1)
            for a in range(3):
                for s in range(S):
                    c = (a * S + s) * NT
                    mm = pe.transpose(p_misc[0:TE, c:c + NT], key_f[:, a, s, :], K["ident"][0:NT, 0:NT])
            mm.then_inc(keys_turned, 1)
            pe.wait_ge(const_ready, 6)
            for s in range(S):
                mm = pe.matmul(p_hist[s][:, 0:LO], zero_b[:, 0:NH], zero_b[:, :], start=True, stop=False,
                               skip_group_check=True)
            mm.then_inc(hist_zero, 1)
            with pe.Fori(0, NT // G) as i:
                for m in range(8):
                    s = m % 2
                    pe.wait_ge(hots_ready, i * 8 + m + 1)
                    pe.wait_ge(run_ready, i * 8 + m + 1)
                    pe.wait_ge(look_read, i * 8 + m + 1)
                    pe.matmul(p_look[m % 4][:, 0:LO], hot_hi_t[:, m, :], run[:, m % 4, :], start=True, stop=True) \
                      .then_inc(looked_up, 1)
                    pe.matmul(p_hist[s][:, 0:LO], hot_hi[:, m, :], hot_lo[:, m, :], start=False, stop=False,
                              skip_group_check=True).then_inc(hist_added, 1)
            pe.wait_ge(totals_ready, 1)
            pe.matmul(p_misc[0:NH, 0:S], above[:, :], total[:, :], start=True, stop=True).then_inc(carry_ready, 1)


def rows_of(dram, g, n, p):
    return dram[bass.ds(g * (n * p), n * p), :].rearrange("(j p) d -> p j d", p=p)


def open_slot(pool, K, sem, count):
    K["token_n"] += 1
    n = K["token_n"]
    pool.dma_start(K["token"][0:1, n, :], K["ident"][0:1, 0:4]).then_inc(sem, count)


class Norm:

    def __init__(self, nc, ctx, name, sem, rows, n, eps):
        def sb(what, shape):
            return ctx.enter_context(nc.sbuf_tensor(f"{name}_{what}", shape, F32))

        self.rows, self.n, self.eps = rows, n, eps
        self.stats = sb("stats", [rows, 2, n, 6])
        self.mean_var = sb("mean_var", [rows, 2, n, 2])
        self.std = sb("std", [rows, 2, n])
        self.rstd = sb("rstd", [rows, 2, n])
        self.shift = sb("shift", [rows, 2, n])
        self.stats_done = sem("stats_done")
        self.passed = sem("stats_passed")
        self.var_ready = sem("var_ready")
        self.std_ready = sem("std_ready")
        self.rstd_done = sem("rstd_done")
        self.shift_ready = sem("shift_ready")

    def statistics(self, dve, g, b, x):
        for j in range(self.n):
            ins = dve.bn_stats(self.stats[:, b, j, :], x[:, j, :])
        ins.then_inc(self.stats_done, 1)
        dve.wait_ge(self.stats_done, g + 1)
        dve.sem_inc(self.passed, 1)
        for j in range(self.n):
            ins = dve.bn_aggr(self.mean_var[:, b, j, :], self.stats[:, b, j, :])
        ins.then_inc(self.var_ready, 1)

    def root(self, act, g, b):
        act.wait_ge(self.var_ready, g + 1)
        act.activation(self.std[:, b, :], self.mean_var[:, b, :, 1], ACT.Sqrt, bias=self.eps[0:self.rows, 0:1],
                       scale=1.0).then_inc(self.std_ready, 1)

    def scales(self, dve, g, b):
        dve.wait_ge(self.std_ready, g + 1)
        dve.reciprocal(self.rstd[:, b, :], self.std[:, b, :]).then_inc(self.rstd_done, 1)
        dve.wait_ge(self.rstd_done, g + 1)
        dve.scalar_tensor_tensor(out=self.shift[:, b, :], in0=self.mean_var[:, b, :, 0], scalar=-1.0,
                                 in1=self.rstd[:, b, :], op0=ALU.mult, op1=ALU.mult).then_inc(self.shift_ready, 1)

    def rows_out(self, act, g, b, h, x):
        act.wait_ge(self.shift_ready, g + 1)
        for j in range(self.n):
            ins = act.activation(h[:, j, :], x[:, j, :], ACT.Relu, bias=self.shift[:, b, j:j + 1],
                                 scale=self.rstd[:, b, j:j + 1])
        return ins


class Records:

    def __init__(self, nc, ctx, sem, K, A, table, rec_d, rec_c):
        def sb(name, shape, dt=F32):
            return ctx.enter_context(nc.sbuf_tensor(f"rc_{name}", shape, dt))

        self.K, self.A, self.table, self.rec_d, self.rec_c = K, A, table, rec_d, rec_c
        self.N = A["x"].shape[0]
        self.NT = A["src"].shape[0] // TE
        self.NREL = A["L1_gnn_alpha"].shape[0]
        self.RANK_D = RD + 2 * RC
        self.W = self.RANK_D + 4
        self.NP = self.NT // GP
        NT = self.NT
        self.idx = sb("idx", [TE, 2, 2, GP], I32)
        self.got = sb("got", [TE, 2, 2, GP, 4])
        self.tab = sb("tab", [TE, 2, NT, 4])
        self.node = sb("node", [TE, 2, NT])
        self.rec = sb("rec", [TE, NT, self.W])
        self.part = sb("part", [TE, 12, NT])
        self.a2_40 = sb("a2_40", [NT, TE, 2])
        self.a3_40 = sb("a3_40", [NT, TE, 3])
        self.type_i = sb("type_i", [NT, TE], I32)
        self.type_40 = sb("type_40", [NT, TE])
        self.type_c = sb("type_c", [TE, NT])
        self.alpha = sb("alpha", [TE, self.NREL])
        self.pick = sb("pick", [TE, 2, NT])
        self.d_out = sb("d_out", [TE, 2, GP, RD])
        self.d_idx = sb("d_idx", [TE, 2, GP], I32)
        self.c_out = sb("c_out", [TE, 2, 2, RC])
        self.c_idx = sb("c_idx", [TE, 2, 2], I32)
        self.small_in = sem("small_in")
        self.types_ready = sem("types_ready")
        self.cols_ready = sem("cols_ready")
        self.rec_cleared = sem("rec_cleared")
        self.idx_ready = sem("idx_ready")
        self.got_in = [sem(f"got_in{b}") for b in range(2)]
        self.got_read = sem("got_read")
        self.step = sem("step")
        self.steps = 0
        self.d_ready = sem("d_ready")
        self.d_put = [sem(f"d_put{b}") for b in range(2)]
        self.c_ready = sem("c_ready")
        self.c_put = [sem(f"c_put{b}") for b in range(2)]
        self.passed = sem("passed")

    def rc(self, c):
        return self.rec[:, :, c]

    def then(self, dve, ins):
        ins.then_inc(self.step, 1)
        self.steps += 1
        dve.wait_ge(self.step, self.steps)

    def load(self, sp):
        A = self.A
        sp.dma_start(self.a2_40[:, :, :].rearrange("t e c -> t (e c)"),
                     A["edge_attr_2"].rearrange("(t e) c -> t (e c)", e=TE)).then_inc(self.small_in, 16)
        sp.dma_start(self.a3_40[:, :, :].rearrange("t e c -> t (e c)"),
                     A["edge_attr_3"].rearrange("(t e) c -> t (e c)", e=TE)).then_inc(self.small_in, 16)
        sp.dma_start(self.type_i[:, :], A["edge_type_11"].rearrange("(t e) -> t e", e=TE)).then_inc(self.small_in, 16)
        sp.dma_start(self.alpha[:, :], A["L1_gnn_alpha"].rearrange("r a -> a r").to_broadcast([TE, self.NREL])) \
            .then_inc(self.small_in, 16)

    def turn_columns(self, pe, bank):
        NT, ident = self.NT, self.K["ident"]
        pe.wait_ge(self.types_ready, 1)
        for c in range(2):
            pe.transpose(bank[:, c * NT:(c + 1) * NT], self.a2_40[:, :, c], ident[0:NT, 0:NT])
        for c in range(3):
            pe.transpose(bank[:, (2 + c) * NT:(3 + c) * NT], self.a3_40[:, :, c], ident[0:NT, 0:NT])
        pe.transpose(bank[:, 5 * NT:6 * NT], self.type_40[:, :], ident[0:NT, 0:NT]).then_inc(self.cols_ready, 1)

    def clear(self, pool):
        for b in range(2):
            open_slot(pool, self.K, self.d_put[b], 16 * GP)
        pool.memset(self.rec[:, :, :], 0.0).then_inc(self.rec_cleared, 1)
        pool.wait_ge(self.rec_cleared, 1)
        pool.memset(self.rec[:, :, D_ONE], 1.0)
        pool.iota(self.rec[:, :, D_EDGE], [[TE, self.NT]], base=0, channel_multiplier=1,
                  allow_small_or_imprecise_dtypes=True).then_inc(self.rec_cleared, 1)
        pool.sem_inc(self.got_read, 2)

    def columns(self, dve, bank):
        NT = self.NT
        dve.wait_ge(self.small_in, 64)
        dve.tensor_copy(self.type_40[:, :], self.type_i[:, :]).then_inc(self.types_ready, 1)
        dve.wait_ge(self.cols_ready, 1)
        dve.wait_ge(self.rec_cleared, 2)
        for c in range(2):
            dve.tensor_copy(self.rc(D_A2 + c), bank[:, c * NT:(c + 1) * NT])
        for c in range(3):
            dve.tensor_copy(self.rc(D_A3 + c), bank[:, (2 + c) * NT:(3 + c) * NT])
        self.then(dve, dve.tensor_copy(self.type_c[:, :], bank[:, 5 * NT:6 * NT]))

    def weights(self, dve):
        pick = self.pick
        self.then(dve, dve.tensor_scalar(pick[:, 0, :], self.type_c[:, :], 0.0, self.alpha[:, 0:1], ALU.is_equal,
                                         ALU.mult))
        for r in range(1, self.NREL):
            self.then(dve, dve.tensor_scalar(pick[:, 1, :], self.type_c[:, :], float(r), self.alpha[:, r:r + 1],
                                             ALU.is_equal, ALU.mult))
            self.then(dve, dve.tensor_tensor(pick[:, 0, :], pick[:, 0, :], pick[:, 1, :], ALU.add))

    def index(self, dve, q):
        b = q.slot(2)
        dve.tensor_copy(self.idx[:, b, 0, :], self.K["dst_col"][:, bass.ds(q.g * GP, GP)])
        dve.tensor_copy(self.idx[:, b, 1, :], self.K["src_col"][:, bass.ds(q.g * GP, GP)]).then_inc(self.idx_ready, 1)

    def look_up(self, pool, q):
        b = q.slot(2)
        pool.wait_ge(self.idx_ready, q.g + 1)
        pool.wait_ge(self.got_read, q.g + 1)
        pool.sem_inc(self.passed, 1)
        for s in range(2):
            for j in range(GP):
                pool.indirect_dma_start(self.got[:, b, s, j, :], None, self.table[:, :],
                                        IOA(self.idx[:, b, s, j:j + 1], 0), bounds_check=self.N - 1,
                                        oob_is_err=False).then_inc(self.got_in[b], 16)

    def keep(self, dve, q):
        b = q.slot(2)
        dve.wait_ge(self.got_in[b], q.round(2) * (32 * GP))
        for s in range(2):
            ins = dve.tensor_copy(self.tab[:, s, bass.ds(q.g * GP, GP), :].rearrange("p t c -> p (t c)"),
                                  self.got[:, b, s, :, :].rearrange("p t c -> p (t c)"))
        ins.then_inc(self.got_read, 1)

    def places(self, dve):
        tab, part, rc, node, pick, K, RANK_D = self.tab, self.part, self.rc, self.node, self.pick, self.K, self.RANK_D
        RANK_CD, RANK_CS = RANK_D + 1, RANK_D + 2

        def then(ins):
            self.then(dve, ins)

        dve.wait_ge(self.got_read, self.NP + 2)
        dve.tensor_copy(node[:, 0, :], K["dst_col"][:, 0:self.NT])
        dve.tensor_copy(node[:, 1, :], K["src_col"][:, 0:self.NT])
        dst_below, dst_upto, src_below, src_upto = (tab[:, 0, :, c] for c in range(4))
        s_dst_below, s_dst_upto, s_src_below, s_src_upto = (tab[:, 1, :, c] for c in range(4))
        CD, CS = RD, RD + RC
        then(dve.tensor_tensor(rc(RANK_D), dst_below, K["ord"][:, :, 0], ALU.add))
        dve.tensor_tensor(rc(RANK_CD), rc(RANK_D), src_below, ALU.add)
        then(dve.tensor_tensor(part[:, 0, :], s_src_below, K["ord"][:, :, 1], ALU.add))
        dve.tensor_tensor(rc(RANK_CS), part[:, 0, :], s_dst_upto, ALU.add)
        dve.tensor_tensor(part[:, 1, :], dst_upto, src_upto, ALU.add)
        dve.tensor_tensor(part[:, 2, :], s_dst_upto, s_src_upto, ALU.add)
        then(dve.tensor_tensor(part[:, 3, :], s_dst_below, s_src_below, ALU.add))
        dve.tensor_scalar(rc(D_SLOT_D), part[:, 1, :], -1.0, None, ALU.add)
        dve.tensor_scalar(rc(D_SLOT_S), part[:, 2, :], -1.0, None, ALU.add)
        dve.tensor_scalar(rc(D_SAME), K["ord"][:, :, 0], 0.0, None, ALU.is_gt)
        dve.tensor_scalar(rc(CD + C_SAME), K["ord"][:, :, 0], 0.0, None, ALU.is_gt)
        dve.tensor_tensor(rc(CS + C_SAME), rc(RANK_CS), part[:, 3, :], ALU.is_gt)
        dve.tensor_tensor(part[:, 4, :], dst_upto, rc(RANK_D), ALU.subtract)
        dve.tensor_tensor(part[:, 5, :], part[:, 1, :], rc(RANK_CD), ALU.subtract)
        then(dve.tensor_tensor(part[:, 6, :], part[:, 2, :], rc(RANK_CS), ALU.subtract))
        for c in range(3):
            ins = dve.tensor_scalar(part[:, 7 + c, :], part[:, 4 + c, :], 1.5, float(SKIP), ALU.is_gt, ALU.mult)
        then(ins)
        dve.tensor_tensor(rc(D_PUT), part[:, 7, :], node[:, 0, :], ALU.add)
        dve.tensor_tensor(rc(CD + C_PUT), part[:, 8, :], node[:, 0, :], ALU.add)
        dve.tensor_tensor(rc(CS + C_PUT), part[:, 9, :], node[:, 1, :], ALU.add)
        dve.tensor_copy(rc(D_SRC), node[:, 1, :])
        dve.tensor_copy(rc(CD + C_NODE), node[:, 0, :])
        dve.tensor_copy(rc(CD + C_PEER), node[:, 1, :])
        dve.tensor_copy(rc(CS + C_NODE), node[:, 1, :])
        dve.tensor_copy(rc(CS + C_PEER), node[:, 0, :])
        dve.tensor_copy(rc(CD + C_W), pick[:, 0, :])
        then(dve.tensor_copy(rc(CS + C_W), pick[:, 0, :]))

    def lay_out(self, dve, q):
        b = q.slot(2)
        dve.wait_ge(self.d_put[b], q.round(2) * (16 * GP))
        dve.tensor_copy(self.d_out[:, b, :, :], self.rec[:, bass.ds(q.g * GP, GP), 0:RD])
        dve.tensor_copy(self.d_idx[:, b, :], self.rec[:, bass.ds(q.g * GP, GP), self.RANK_D]) \
            .then_inc(self.d_ready, 1)

    def put_by_dst(self, pool, q):
        b = q.slot(2)
        pool.wait_ge(self.d_ready, q.g + 1)
        pool.sem_inc(self.passed, 1)
        for j in range(GP):
            pool.indirect_dma_start(self.rec_d[:, :], IOA(self.d_idx[:, b, j:j + 1], 0), self.d_out[:, b, j, :], None,
                                    bounds_check=self.rec_d.shape[0] - 1, oob_is_err=False) \
                .then_inc(self.d_put[b], 16)

    def end_by_dst(self, pool):
        for b in range(2):
            pool.wait_ge(self.d_put[b], 16 * GP * (1 + (self.NP + 1 - b) // 2))

    def start_by_node(self, pool):
        for b in range(2):
            open_slot(pool, self.K, self.c_put[b], 32)

    def put_by_node(self, pool, t):
        b = t.slot(2)
        pool.wait_ge(self.c_put[b], t.round(2) * 32)
        pool.tensor_copy(self.c_out[:, b, :, :].rearrange("p s c -> p (s c)"),
                         self.rec[:, bass.ds(t.g, 1), RD:RD + 2 * RC].rearrange("p t c -> p (t c)"))
        pool.tensor_copy(self.c_idx[:, b, :],
                         self.rec[:, bass.ds(t.g, 1), self.RANK_D + 1:self.RANK_D + 3].rearrange("p t c -> p (t c)")) \
            .then_inc(self.c_ready, 1)
        pool.wait_ge(self.c_ready, t.g + 1)
        pool.sem_inc(self.passed, 1)
        for s in range(2):
            pool.indirect_dma_start(self.rec_c[:, :], IOA(self.c_idx[:, b, s:s + 1], 0), self.c_out[:, b, s, :], None,
                                    bounds_check=self.rec_c.shape[0] - 1, oob_is_err=False) \
                .then_inc(self.c_put[b], 16)

    def end_by_node(self, pool):
        for b in range(2):
            pool.wait_ge(self.c_put[b], 32 * (1 + self.NT // 2))


def edge_messages(nc, K, A, R, msg):
    N = A["x"].shape[0]
    E = A["src"].shape[0]
    NG = E // GE
    with ExitStack() as ctx:
        def sb(name, shape, dt=F32):
            return ctx.enter_context(nc.sbuf_tensor(name, shape, dt))

        def pb(name, shape, dt=F32):
            return ctx.enter_context(nc.psum_tensor(name, shape, dt))

        sem = ctx.enter_context(signals(nc, "em"))
        w1 = sb("em_w1", [P, DC, HID])
        w2 = sb("em_w2", [P, HC, D])
        b1 = sb("em_b1", [P, HC])
        b2 = sb("em_b2", [TE, D])
        ef = sb("em_ef", [TE, 2, G, D])
        x = sb("em_x", [TE, 2, G, D])
        h = sb("em_h", [TE, 2, G, D])
        m = sb("em_m", [TE, 2, G, D])
        idx = sb("em_idx", [TE, 2, G], I32)
        ef_t = sb("em_ef_t", [P, 2, DC, GE])
        hid = sb("em_hid", [P, 2, HC, GE])
        p_t = [pb(f"em_p_t{c}", [P, 512]) for c in range(DC)]
        p_h = [pb(f"em_p_h{c}", [P, 512]) for c in range(HC)]
        p_m = [pb(f"em_p_m{c}", [TE, 2, D]) for c in range(2)]
        norm = Norm(nc, ctx, "em", sem, TE, G, K["eps"])

        w_in = sem("w_in")
        ef_in = [sem(f"ef_in{b}") for b in range(2)]
        x_in = [sem(f"x_in{b}") for b in range(2)]
        m_out = [sem(f"m_out{b}") for b in range(2)]
        idx_ready = sem("idx_ready")
        h_ready = sem("h_ready")
        ef_turned = sem("ef_turned")
        ef_t_ready = sem("ef_t_ready")
        hid_mm = sem("hid_mm")
        hid_ready = sem("hid_ready")
        m_mm = sem("m_mm")
        m_added = sem("m_added")
        m_ready = sem("m_ready")
        h_shifted = sem("h_shifted")
        passed = sem("passed")
        block = ctx.enter_context(nc.Block())
        LOOK = R.NP - 1
        assert LOOK % 2 == 0 and NG >= 2 * LOOK + 2

        def groups(eng, body, looking=None, between=None, after=None):
            with eng.Fori(0, LOOK // 2) as i:
                for r in range(2):
                    (looking or body)(Step(i, r, 2, NG))
            if between:
                between()
            with eng.Fori(0, LOOK // 2) as i:
                for r in range(2):
                    if after:
                        after(Step(i, r, 2, NG))
                    body(Step(i + LOOK // 2, r, 2, NG))
            if after:
                after(Step(LOOK // 2, 0, 2, NG))
            for g in range(2 * LOOK, NG):
                body(Step(g // 2, g % 2, 2, NG))


        @block.sync
        def _(sp):
            sp.dma_start(w1[:, :, :], A["L0_gnn_We1"].rearrange("(k p) n -> p k n", p=P)).then_inc(w_in, 16)
            sp.dma_start(w2[:, :, :], A["L0_gnn_We2"].rearrange("(k p) n -> p k n", p=P)).then_inc(w_in, 16)
            with nc.allow_non_contiguous_dma(reason="512 biases"):
                sp.dma_start(b1[:, :], A["L0_gnn_be1"].rearrange("(k p) -> p k", p=P)).then_inc(w_in, 16)
            sp.dma_start(b2[:, :], A["L0_gnn_be2"].rearrange("(a d) -> a d", a=1).to_broadcast([TE, D])) \
                .then_inc(w_in, 16)
            R.load(sp)
            sp.sem_inc(ef_turned, 2)

            def load(t):
                b = t.slot(2)
                sp.wait_ge(ef_turned, t.g + 1)
                sp.dma_start(ef[:, b, :, :], rows_of(A["edge_attr_256"], t.g, G, TE)).then_inc(ef_in[b], 16)

            over_groups(sp, NG, 2, 0, load)

        @block.gpsimd
        def _(pool):
            R.clear(pool)
            pool.sem_inc(h_ready, 2)

            def fetch(t):
                b = t.slot(2)
                pool.wait_ge(idx_ready, t.g + 1)
                pool.wait_ge(h_ready, t.g + 1)
                pool.sem_inc(passed, 1)
                for j in range(G):
                    pool.indirect_dma_start(x[:, b, j, :], None, A["x"], IOA(idx[:, b, j:j + 1], 0),
                                            bounds_check=N - 1, oob_is_err=False).then_inc(x_in[b], 16)

            def looking(t):
                R.look_up(pool, t.ahead(1))
                fetch(t.ahead(2))

            def body(t):
                if t.ahead(2).exists():
                    fetch(t.ahead(2))

            for b in range(2):
                fetch(Step(0, b, 2, NG))
            R.look_up(pool, Step(0, 0, 2, R.NP))
            groups(pool, body, looking=looking, after=lambda q: R.put_by_dst(pool, q))
            R.end_by_dst(pool)

        @block.vector
        def _(dve):
            for b in range(2):
                R.index(dve, Step(0, b, 2, R.NP))
                dve.tensor_copy(idx[:, b, :], K["src_col"][:, b * G:(b + 1) * G]).then_inc(idx_ready, 1)
                dve.sem_inc(m_out[b], 16)
            R.columns(dve, p_m[0][:, :, :].rearrange("p a d -> p (a d)"))
            dve.sem_inc(m_added, 2)
            dve.wait_ge(w_in, 64)

            def first_half(t):
                dve.wait_ge(ef_turned, t.g + 3)
                dve.tensor_copy(ef_t[:, t.slot(2), 0, :], p_t[0][:, 0:GE]).then_inc(ef_t_ready, 1)

            def looking(t):
                body(t)
                R.keep(dve, t)
                R.index(dve, t.ahead(2))

            def between():
                R.weights(dve)
                R.keep(dve, Step(LOOK // 2, 0, 2, R.NP))
                R.places(dve)

            def body(t):
                b = t.slot(2)
                dve.wait_ge(x_in[b], t.round(2) * (16 * G))
                norm.statistics(dve, t.g, b, x[:, b, :, :])
                dve.tensor_copy(idx[:, b, :], K["src_col"][:, bass.ds(t.g * G + 2 * G, G)]).then_inc(idx_ready, 1)
                norm.scales(dve, t.g, b)
                if t.ahead(1).exists():
                    first_half(t.ahead(1))
                dve.wait_ge(h_ready, t.g + 3)
                dve.wait_ge(m_out[b], t.round(2) * 16)
                dve.tensor_tensor(m[:, b, :, :], h[:, b, :, :], b2[:, :].unsqueeze(1).to_broadcast([TE, G, D]),
                                  ALU.add).then_inc(h_shifted, 1)
                dve.wait_ge(h_shifted, t.g + 1)
                for c in range(2):
                    dve.wait_ge(m_mm, t.g * 2 + c + 1)
                    dve.tensor_tensor(m[:, b, 2 * c:2 * c + 2, :], m[:, b, 2 * c:2 * c + 2, :], p_m[c][:, :, :],
                                      ALU.add).then_inc(m_added, 1)

            first_half(Step(0, 0, 2, NG))
            groups(dve, body, looking=looking, between=between, after=lambda q: R.lay_out(dve, q))

        @block.scalar
        def _(act):
            act.wait_ge(w_in, 64)

            def second_half(t):
                act.wait_ge(ef_turned, t.g + 3)
                act.copy(ef_t[:, t.slot(2), 1, :], p_t[1][:, 0:GE]).then_inc(ef_t_ready, 1)

            def hidden(t, k):
                act.wait_ge(hid_mm, t.g * HC + k + 1)
                act.activation(hid[:, t.slot(2), k, :], p_h[k][:, 0:GE], ACT.Relu, bias=b1[:, k:k + 1]) \
                   .then_inc(hid_ready, 1)

            def body(t):
                b = t.slot(2)
                norm.root(act, t.g, b)
                hidden(t, 0)
                norm.rows_out(act, t.g, b, h[:, b, :, :], x[:, b, :, :]).then_inc(h_ready, 1)
                for k in range(1, HC):
                    hidden(t, k)
                if t.ahead(1).exists():
                    second_half(t.ahead(1))
                act.wait_ge(m_added, t.g * 2 + 4)
                act.activation(m[:, b, :, :], m[:, b, :, :], ACT.Relu).then_inc(m_ready, 1)
                act.wait_ge(m_ready, t.g + 1)
                act.dma_start(rows_of(msg, t.g, G, TE), m[:, b, :, :]).then_inc(m_out[b], 16)

            second_half(Step(0, 0, 2, NG))
            groups(act, body)
            for b in range(2):
                act.wait_ge(m_out[b], 16 * (NG // 2 + 1))

        @block.tensor
        def _(pe):
            R.turn_columns(pe, p_m[0][:, :, :].rearrange("p a d -> p (a d)"))
            pe.wait_ge(w_in, 64)
            pe.sem_inc(ef_t_ready, 2)
            pe.sem_inc(hid_ready, HC)

            def turn(t):
                b = t.slot(2)
                pe.wait_ge(ef_in[b], t.round(2) * 16)
                pe.wait_ge(ef_t_ready, t.g * 2 + 2)
                for c in range(DC):
                    for j in range(G):
                        mm = pe.transpose(p_t[c][:, j * TE:(j + 1) * TE], ef[:, b, j, c * P:(c + 1) * P],
                                          K["ident"][0:TE, 0:TE])
                mm.then_inc(ef_turned, 1)

            def body(t):
                b = t.slot(2)
                pe.wait_ge(ef_t_ready, t.g * 2 + 4)
                for k in range(HC):
                    pe.wait_ge(hid_ready, t.g * HC + k + 1)
                    for c in range(DC):
                        mm = pe.matmul(p_h[k][:, 0:GE], w1[:, c, k * P:(k + 1) * P], ef_t[:, b, c, :],
                                       start=(c == 0), stop=(c == DC - 1))
                    mm.then_inc(hid_mm, 1)
                if t.ahead(1).exists():
                    turn(t.ahead(1))
                pe.wait_ge(hid_ready, t.g * HC + 2 * HC)
                for c in range(2):
                    pe.wait_ge(m_added, t.g * 2 + c + 1)
                    for jj in range(2):
                        j = 2 * c + jj
                        for k in range(HC):
                            mm = pe.matmul(p_m[c][:, jj, :], hid[:, b, k, j * TE:(j + 1) * TE], w2[:, k, :],
                                           start=(k == 0), stop=(k == HC - 1))
                    mm.then_inc(m_mm, 1)

            turn(Step(0, 0, 2, NG))
            groups(pe, body)


def aggregate_messages(nc, K, msg, rec_d, agg0):
    N = agg0.shape[0]
    E = msg.shape[0]
    NG = E // GE
    same = K["same"]
    with ExitStack() as ctx:
        def sb(name, shape, dt=F32):
            return ctx.enter_context(nc.sbuf_tensor(name, shape, dt))

        def pb(name, shape, dt=F32):
            return ctx.enter_context(nc.psum_tensor(name, shape, dt))

        sem = ctx.enter_context(signals(nc, "ag"))
        rec = sb("ag_rec", [TE, 2, G, RD])
        keep = sb("ag_keep", [TE, 2, G])
        idx = sb("ag_idx", [TE, 2, G], I32)
        put_idx = sb("ag_put_idx", [TE, 2, G], I32)
        m = sb("ag_m", [TE, 2, G, D])
        run = sb("ag_run", [P, 2, DC, GE])
        rows = sb("ag_rows", [TE, 2, G, D])
        p_s = pb("ag_p_s", [P, 512])
        p_t = [[pb(f"ag_p_t{b}{c}", [P, 512]) for c in range(DC)] for b in range(2)]
        p_r = [pb(f"ag_p_r{c}", [TE, 2, D]) for c in range(2)]

        rec_in = [sem(f"rec_in{b}") for b in range(2)]
        m_in = [sem(f"m_in{b}") for b in range(2)]
        put = [sem(f"put{b}") for b in range(2)]
        idx_ready = sem("idx_ready")
        put_idx_ready = sem("put_idx_ready")
        same_mm = sem("same_mm")
        same_ready = sem("same_ready")
        m_turned = sem("m_turned")
        run_ready = sem("run_ready")
        run_turned = sem("run_turned")
        rows_ready = sem("rows_ready")
        passed = sem("passed")
        block = ctx.enter_context(nc.Block())

        def groups(eng, body):
            over_groups(eng, NG, 2, 4, body)

        @block.sync
        def _(sp):
            sp.sem_inc(same_mm, 2)

            def load(t):
                b = t.slot(2)
                sp.wait_ge(same_mm, t.g + 1)
                sp.dma_start(rec[:, b, :, :], rows_of(rec_d, t.g, G, TE)).then_inc(rec_in[b], 16)

            groups(sp, load)

        @block.gpsimd
        def _(pool):
            for b in range(2):
                open_slot(pool, K, put[b], 16 * G)

            def fetch(t):
                b = t.slot(2)
                pool.wait_ge(idx_ready, t.g + 1)
                pool.wait_ge(m_turned, t.g + 1)
                pool.sem_inc(passed, 1)
                for j in range(G):
                    pool.indirect_dma_start(m[:, b, j, :], None, msg[:, :], IOA(idx[:, b, j:j + 1], 0),
                                            bounds_check=E - 1, oob_is_err=False).then_inc(m_in[b], 16)

            def body(t):
                if t.ahead(2).exists():
                    fetch(t.ahead(2))
                b = t.slot(2)
                pool.wait_ge(rows_ready, t.g * 2 + 4)
                pool.sem_inc(passed, 1)
                for j in range(G):
                    pool.indirect_dma_start(agg0[:, :], IOA(put_idx[:, b, j:j + 1], 0), rows[:, b, j, :], None,
                                            bounds_check=N - 1, oob_is_err=False).then_inc(put[b], 16)

            pool.sem_inc(m_turned, 2)
            fetch(Step(0, 0, 2, NG))
            fetch(Step(0, 1, 2, NG))
            groups(pool, body)
            for b in range(2):
                pool.wait_ge(put[b], 16 * G * (NG // 2 + 1))

        @block.vector
        def _(dve):
            dve.memset(run[:, 1, :, GE - 1], 0.0).then_inc(run_ready, 4)

            def take(t):
                b = t.slot(2)
                dve.wait_ge(rec_in[b], t.round(2) * 16)
                dve.wait_ge(put_idx_ready, t.g + 1)
                dve.tensor_copy(keep[:, b, :], rec[:, b, :, D_PUT])
                dve.tensor_copy(idx[:, b, :], rec[:, b, :, D_EDGE]).then_inc(idx_ready, 1)

            def body(t):
                b = t.slot(2)
                dve.wait_ge(put[b], t.round(2) * (16 * G))
                dve.wait_ge(idx_ready, t.g + 1)
                dve.tensor_copy(put_idx[:, b, :], keep[:, b, :]).then_inc(put_idx_ready, 1)
                dve.wait_ge(m_turned, t.g + 3)
                if t.ahead(2).exists():
                    take(t.ahead(2))
                dve.wait_ge(same_ready, t.g + 2)
                dve.wait_ge(run_ready, t.g * 2 + 4)
                for c in range(DC):
                    dve.tensor_tensor_scan(run[:, b, c, :], same[:, bass.ds(t.g * GE, GE)], p_t[b][c][:, 0:GE],
                                           run[:, 1 - b, c, GE - 1:GE], ALU.mult, ALU.add) \
                       .then_inc(run_ready, 1)

            dve.sem_inc(put_idx_ready, 2)
            take(Step(0, 0, 2, NG))
            take(Step(0, 1, 2, NG))
            groups(dve, body)

        @block.scalar
        def _(act):
            def mask(t):
                act.wait_ge(same_mm, t.g + 3)
                act.copy(same[:, bass.ds(t.g * GE, GE)], p_s[:, 0:GE]).then_inc(same_ready, 1)

            def body(t):
                b = t.slot(2)
                if t.ahead(1).exists():
                    mask(t.ahead(1))
                act.wait_ge(put[b], t.round(2) * (16 * G))
                for c in range(2):
                    act.wait_ge(run_turned, t.g * 2 + c + 1)
                    act.copy(rows[:, b, 2 * c:2 * c + 2, :], p_r[c][:, :, :]).then_inc(rows_ready, 1)

            mask(Step(0, 0, 2, NG))
            groups(act, body)

        @block.tensor
        def _(pe):
            def turn(t):
                b = t.slot(2)
                pe.wait_ge(rec_in[b], t.round(2) * 16)
                pe.wait_ge(idx_ready, t.g + 1)
                pe.wait_ge(same_ready, t.g + 1)
                for j in range(G):
                    mm = pe.matmul(p_s[:, j * TE:(j + 1) * TE],
                                   rec[:, b, j, D_SAME:D_SAME + 1].to_broadcast([TE, P]),
                                   K["ident"][0:TE, 0:TE], start=True, stop=True)
                mm.then_inc(same_mm, 1)
                pe.wait_ge(m_in[b], t.round(2) * (16 * G))
                pe.wait_ge(run_ready, t.g * 2 + 2)
                for c in range(DC):
                    for j in range(G):
                        mm = pe.transpose(p_t[b][c][:, j * TE:(j + 1) * TE], m[:, b, j, c * P:(c + 1) * P],
                                          K["ident"][0:TE, 0:TE])
                mm.then_inc(m_turned, 1)

            def body(t):
                b = t.slot(2)
                if t.ahead(1).exists():
                    turn(t.ahead(1))
                pe.wait_ge(run_ready, t.g * 2 + 6)
                for c in range(2):
                    pe.wait_ge(rows_ready, t.g * 2 + c + 1)
                    for jj in range(2):
                        j = 2 * c + jj
                        for k in range(DC):
                            mm = pe.transpose(p_r[c][:, jj, k * P:(k + 1) * P],
                                              run[:, b, k, j * TE:(j + 1) * TE], K["ident"][:, :])
                    mm.then_inc(run_turned, 1)

            pe.sem_inc(same_ready, 1)
            pe.sem_inc(rows_ready, 2)
            turn(Step(0, 0, 2, NG))
            groups(pe, body)


def broadcast_row(vector, rows):
    return vector.rearrange("(a d) -> a d", a=1).to_broadcast([rows, vector.shape[0]])


def node_network(nc, K, A, R, agg0, x1_dram, out):
    N = A["x"].shape[0]
    ROWS = G * P
    NG = -(-N // ROWS)
    XB = 4
    UN = 4
    assert NG % UN == 0 and XB == UN and NG == R.NT
    with ExitStack() as ctx:
        def sb(name, shape, dt=F32):
            return ctx.enter_context(nc.sbuf_tensor(name, shape, dt))

        def pb(name, shape, dt=F32):
            return ctx.enter_context(nc.psum_tensor(name, shape, dt))

        sem = ctx.enter_context(signals(nc, "nn"))
        w1 = sb("nn_w1", [P, DC, HID])
        w2 = sb("nn_w2", [P, HC, D])
        b1 = sb("nn_b1", [P, HC])
        b2 = sb("nn_b2", [P, D])
        late = sb("nn_late", [P, 2, D])
        late_sum = sb("nn_late_sum", [P, D])
        gain = sb("nn_gain", [P, 1])
        x = sb("nn_x", [P, XB, G, D])
        agg = sb("nn_agg", [P, XB, G, D])
        h = sb("nn_h", [P, 2, G, D])
        x1 = sb("nn_x1", [P, 2, G, D])
        x3 = sb("nn_x3", [P, 2, G, D])
        h_t = sb("nn_h_t", [P, 2, DC, ROWS])
        hid = sb("nn_hid", [P, 2, HC, ROWS])
        p_t = [pb(f"nn_p_t{c}", [P, ROWS]) for c in range(DC)]
        p_h = [pb(f"nn_p_h{c}", [P, ROWS]) for c in range(HC)]
        p_o = [pb(f"nn_p_o{c}", [P, 2, D]) for c in range(2)]
        norm = Norm(nc, ctx, "nn", sem, P, G, K["eps"])

        w_in = sem("w_in")
        x_in = [sem(f"x_in{r}") for r in range(XB)]
        x1_out = [sem(f"x1_out{b}") for b in range(2)]
        x3_out = [sem(f"x3_out{b}") for b in range(2)]
        late_ready = sem("late_ready")
        h_ready = sem("h_ready")
        x_shifted = sem("x_shifted")
        mixed = sem("mixed")
        turned = sem("turned")
        h_t_ready = sem("h_t_ready")
        hid_mm = sem("hid_mm")
        hid_ready = sem("hid_ready")
        o_mm = sem("o_mm")
        x1_ready = sem("x1_ready")
        x3_ready = sem("x3_ready")
        block = ctx.enter_context(nc.Block())

        def group(dram, g):
            first = min(g * ROWS, N - ROWS) if isinstance(g, int) else g * ROWS
            return dram[bass.ds(first, ROWS), :].rearrange("(p j) d -> p j d", j=G)

        def groups(eng, body):
            over_groups(eng, NG, UN, UN, body)

        start = [Step(0, k, UN, NG) for k in range(XB)]

        @block.sync
        def _(sp):
            sp.dma_start(w1[:, :, :], A["L0_gnn_Wn1"].rearrange("(k p) n -> p k n", p=P)).then_inc(w_in, 16)
            sp.dma_start(w2[:, :, :], A["L0_gnn_Wn2"].rearrange("(k p) n -> p k n", p=P)).then_inc(w_in, 16)
            with nc.allow_non_contiguous_dma(reason="512 biases"):
                sp.dma_start(b1[:, :], A["L0_gnn_bn1"].rearrange("(k p) -> p k", p=P)).then_inc(w_in, 16)
            sp.dma_start(b2[:, :], broadcast_row(A["L0_gnn_bn2"], P)).then_inc(w_in, 16)
            sp.dma_start(late[:, 0, :], broadcast_row(A["L1_gnn_bias"], P)).then_inc(w_in, 16)
            sp.dma_start(late[:, 1, :], broadcast_row(A["L2_gnn_bias"], P)).then_inc(w_in, 16)
            sp.dma_start(gain[:, :], broadcast_row(A["L0_gnn_eps"], P)).then_inc(w_in, 16)
            for b in range(2):
                sp.sem_inc(x1_out[b], 16)
                sp.sem_inc(x3_out[b], 16)

            def load(t):
                sp.dma_start(x[:, t.r, :, :], group(A["x"], t.g)).then_inc(x_in[t.r], 16)
                sp.dma_start(agg[:, t.r, :, :], group(agg0, t.g)).then_inc(x_in[t.r], 16)

            def body(t):
                b = t.slot(2)
                if isinstance(t.g, int) and t.g == NG - 1:
                    sp.wait_ge(x1_out[1 - b], 16 * (NG // 2 + 1))
                    sp.wait_ge(x3_out[1 - b], 16 * (NG // 2 + 1))
                sp.wait_ge(x1_ready, t.g * 2 + 4)
                sp.dma_start(group(x1_dram, t.g), x1[:, b, :, :]).then_inc(x1_out[b], 16)
                if t.ahead(XB).exists():
                    load(t.ahead(XB))
                sp.wait_ge(x3_ready, t.g + 3)
                sp.dma_start(group(out, t.g), x3[:, b, :, :]).then_inc(x3_out[b], 16)

            for t in start:
                load(t)
            over_groups(sp, NG, UN, 2 * UN, body)
            for b in range(2):
                sp.wait_ge(x1_out[b], 16 * (NG // 2 + 1))
                sp.wait_ge(x3_out[b], 16 * (NG // 2 + 1))

        @block.gpsimd
        def _(pool):
            pool.sem_inc(x3_ready, 2)
            R.start_by_node(pool)
            pool.wait_ge(late_ready, 2)

            def body(t):
                b = t.slot(2)
                pool.wait_ge(h_ready, t.g + 1)
                pool.tensor_tensor(x[:, t.r, :, :], x[:, t.r, :, :],
                                   b2[:, :].unsqueeze(1).to_broadcast([P, G, D]), ALU.add).then_inc(x_shifted, 1)
                R.put_by_node(pool, t)
                pool.wait_ge(x1_ready, t.g * 2 + 4)
                pool.wait_ge(x3_out[b], t.round(2) * 16)
                pool.tensor_tensor(x3[:, b, :, :], x1[:, b, :, :],
                                   late_sum[:, :].unsqueeze(1).to_broadcast([P, G, D]), ALU.add) \
                    .then_inc(x3_ready, 1)

            groups(pool, body)
            R.end_by_node(pool)

        @block.vector
        def _(dve):
            dve.wait_ge(w_in, 16 * 7)
            dve.tensor_tensor(late_sum[:, :], late[:, 0, :], late[:, 1, :], ALU.add).then_inc(late_ready, 1)
            dve.tensor_scalar(gain[:, :], gain[:, :], 1.0, None, ALU.add).then_inc(late_ready, 1)
            dve.wait_ge(late_ready, 2)

            def statistics(t):
                dve.wait_ge(x_in[t.r], t.round(UN) * 32)
                norm.statistics(dve, t.g, t.slot(2), x[:, t.r, :, :])

            def mix(t):
                dve.wait_ge(h_ready, t.g + 1)
                dve.scalar_tensor_tensor(out=agg[:, t.r, :, :].rearrange("p j d -> p (j d)"),
                                         in0=h[:, t.slot(2), :, :].rearrange("p j d -> p (j d)"),
                                         scalar=gain[:, 0:1],
                                         in1=agg[:, t.r, :, :].rearrange("p j d -> p (j d)"),
                                         op0=ALU.mult, op1=ALU.add).then_inc(mixed, 1)

            def first_half(t):
                dve.wait_ge(turned, t.g + 1)
                dve.tensor_copy(h_t[:, t.slot(2), 0, :], p_t[0][:, :]).then_inc(h_t_ready, 1)

            def body(t):
                b = t.slot(2)
                if t.ahead(2).exists():
                    statistics(t.ahead(2))
                    norm.scales(dve, t.ahead(2).g, b)
                if t.ahead(1).exists():
                    first_half(t.ahead(1))
                if t.ahead(2).exists():
                    mix(t.ahead(2))
                dve.wait_ge(x_shifted, t.g + 1)
                dve.wait_ge(x1_out[b], t.round(2) * 16)
                dve.wait_ge(x3_ready, t.g + 1)
                for c in range(2):
                    dve.wait_ge(o_mm, t.g * 2 + c + 1)
                    dve.tensor_tensor(x1[:, b, 2 * c:2 * c + 2, :], x[:, t.r, 2 * c:2 * c + 2, :], p_o[c][:, :, :],
                                      ALU.add).then_inc(x1_ready, 1)

            for t in start[0:2]:
                statistics(t)
                norm.scales(dve, t.g, t.slot(2))
                mix(t)
            first_half(start[0])
            groups(dve, body)

        @block.scalar
        def _(act):
            act.wait_ge(w_in, 16 * 7)

            def hidden(t, k):
                act.wait_ge(hid_mm, t.g * HC + k + 1)
                act.activation(hid[:, t.slot(2), k, :], p_h[k][:, :], ACT.Relu, bias=b1[:, k:k + 1]) \
                   .then_inc(hid_ready, 1)

            def rows(t):
                norm.rows_out(act, t.g, t.slot(2), h[:, t.slot(2), :, :], x[:, t.r, :, :]).then_inc(h_ready, 1)

            def second_half(t):
                act.wait_ge(turned, t.g + 1)
                act.copy(h_t[:, t.slot(2), 1, :], p_t[1][:, :]).then_inc(h_t_ready, 1)

            def body(t):
                if t.ahead(2).exists():
                    act.wait_ge(mixed, t.g + 1)
                    norm.root(act, t.ahead(2).g, t.slot(2))
                hidden(t, 0)
                if t.ahead(2).exists():
                    rows(t.ahead(2))
                for k in range(1, HC):
                    hidden(t, k)
                if t.ahead(1).exists():
                    second_half(t.ahead(1))

            for t in start[0:2]:
                norm.root(act, t.g, t.slot(2))
                rows(t)
            second_half(start[0])
            groups(act, body)

        @block.tensor
        def _(pe):
            pe.wait_ge(w_in, 16 * 7)
            pe.sem_inc(hid_ready, HC)
            pe.sem_inc(h_t_ready, 2)
            pe.sem_inc(x1_ready, 2)

            def turn(t):
                pe.wait_ge(mixed, t.g + 1)
                pe.wait_ge(h_t_ready, t.g * 2 + 2)
                for c in range(DC):
                    for j in range(G):
                        mm = pe.transpose(p_t[c][:, j * P:(j + 1) * P], agg[:, t.r, j, c * P:(c + 1) * P],
                                          K["ident"][:, :])
                mm.then_inc(turned, 1)

            def body(t):
                b = t.slot(2)
                pe.wait_ge(h_t_ready, t.g * 2 + 4)
                for k in range(HC):
                    pe.wait_ge(hid_ready, t.g * HC + k + 1)
                    for c in range(DC):
                        mm = pe.matmul(p_h[k][:, :], w1[:, c, k * P:(k + 1) * P], h_t[:, b, c, :],
                                       start=(c == 0), stop=(c == DC - 1))
                    mm.then_inc(hid_mm, 1)
                if t.ahead(1).exists():
                    turn(t.ahead(1))
                pe.wait_ge(hid_ready, t.g * HC + 2 * HC)
                for c in range(2):
                    pe.wait_ge(x1_ready, t.g * 2 + c + 1)
                    for jj in range(2):
                        j = 2 * c + jj
                        for k in range(HC):
                            mm = pe.matmul(p_o[c][:, jj, :], hid[:, b, k, j * P:(j + 1) * P], w2[:, k, :],
                                           start=(k == 0), stop=(k == HC - 1))
                    mm.then_inc(o_mm, 1)

            turn(start[0])
            groups(pe, body)


def relation_layer(nc, K, A, rec_c, x1_dram, x2_dram, out):
    N = out.shape[0]
    NG = x2_dram.shape[0] // GE
    with ExitStack() as ctx:
        def sb(name, shape, dt=F32):
            return ctx.enter_context(nc.sbuf_tensor(name, shape, dt))

        def pb(name, shape, dt=F32):
            return ctx.enter_context(nc.psum_tensor(name, shape, dt))

        sem = ctx.enter_context(signals(nc, "rl"))
        w = sb("rl_w", [P, DC, D])
        bias = sb("rl_bias", [TE, 2, D])
        rec = sb("rl_rec", [TE, 2, G, RC])
        keep = sb("rl_keep", [TE, 4, G, RC])
        idx = sb("rl_idx", [TE, 2, 2, G], I32)
        put_idx = sb("rl_put_idx", [TE, 4, G], I32)
        x = sb("rl_x", [TE, 2, G, D])
        base = sb("rl_base", [TE, 2, G, D])
        h = sb("rl_h", [TE, 2, G, D])
        same = sb("rl_same", [P, 2, GE])
        run = sb("rl_run", [P, 2, DC, GE])
        x2 = sb("rl_x2", [TE, 4, G, D])
        x3 = sb("rl_x3", [TE, 2, G, D])
        p_s = pb("rl_p_s", [P, 512])
        p_t = [[pb(f"rl_p_t{b}{c}", [P, 512]) for c in range(DC)] for b in range(2)]
        p_o = [pb(f"rl_p_o{c}", [TE, 2, D]) for c in range(2)]
        norm = Norm(nc, ctx, "rl", sem, TE, G, K["eps"])

        w_in = sem("w_in")
        rec_in = [sem(f"rec_in{b}") for b in range(2)]
        x_in = [sem(f"x_in{b}") for b in range(2)]
        x2_out = [sem(f"x2_out{b}") for b in range(4)]
        put = [sem(f"put{b}") for b in range(4)]
        idx_ready = sem("idx_ready")
        h_ready = sem("h_ready")
        weighted = sem("weighted")
        same_mm = sem("same_mm")
        same_ready = sem("same_ready")
        turned = sem("turned")
        run_ready = sem("run_ready")
        o_mm = sem("o_mm")
        summed = sem("summed")
        x2_based = sem("x2_based")
        x3_ready = sem("x3_ready")
        passed = sem("passed")
        block = ctx.enter_context(nc.Block())

        def groups(eng, body):
            over_groups(eng, NG, 4, 4, body)

        first = [Step(0, r, 4, NG) for r in range(4)]

        @block.sync
        def _(sp):
            sp.dma_start(w[:, :, :], A["L1_gnn_weight"].rearrange("(k p) n -> p k n", p=P)).then_inc(w_in, 16)
            sp.dma_start(bias[:, 0, :], broadcast_row(A["L1_gnn_bias"], TE)).then_inc(w_in, 16)
            sp.dma_start(bias[:, 1, :], broadcast_row(A["L2_gnn_bias"], TE)).then_inc(w_in, 16)
            sp.sem_inc(idx_ready, 2)

            def load(t):
                b = t.slot(2)
                sp.wait_ge(idx_ready, t.g + 1)
                sp.dma_start(rec[:, b, :, :], rows_of(rec_c, t.g, G, TE)).then_inc(rec_in[b], 16)

            groups(sp, load)

        @block.gpsimd
        def _(pool):
            for k in range(4):
                open_slot(pool, K, put[k], 16 * G)

            def fetch(t):
                b = t.slot(2)
                pool.wait_ge(idx_ready, t.g + 3)
                pool.sem_inc(passed, 1)
                for j in range(G):
                    for s, rows in ((1, x), (0, base)):
                        pool.indirect_dma_start(rows[:, b, j, :], None, x1_dram[:, :], IOA(idx[:, b, s, j:j + 1], 0),
                                                bounds_check=N - 1, oob_is_err=False).then_inc(x_in[b], 16)

            def body(t):
                if t.ahead(4).exists():
                    fetch(t.ahead(4))
                pool.wait_ge(x3_ready, t.g + 1)
                pool.sem_inc(passed, 1)
                for j in range(G):
                    pool.indirect_dma_start(out[:, :], IOA(put_idx[:, t.slot(4), j:j + 1], 0),
                                            x3[:, t.slot(2), j, :], None, bounds_check=N - 1,
                                            oob_is_err=False).then_inc(put[t.slot(4)], 16)

            for t in first:
                fetch(t)
            groups(pool, body)
            for k in range(4):
                pool.wait_ge(put[k], 16 * G * (NG // 4 + 1))

        @block.vector
        def _(dve):
            def take(t):
                b = t.slot(2)
                dve.wait_ge(rec_in[b], t.round(2) * 16)
                dve.wait_ge(same_mm, t.g + 1)
                dve.tensor_copy(keep[:, t.slot(4), :, :], rec[:, b, :, :])
                dve.tensor_copy(idx[:, b, 0, :], rec[:, b, :, C_NODE])
                dve.tensor_copy(idx[:, b, 1, :], rec[:, b, :, C_PEER]).then_inc(idx_ready, 1)

            def prepare(t):
                b, k = t.slot(2), t.slot(4)
                dve.wait_ge(x_in[b], t.round(2) * (32 * G))
                norm.statistics(dve, t.g, b, x[:, b, :, :])
                dve.wait_ge(x2_out[k], t.round(4) * 16)
                dve.tensor_tensor(x2[:, k, :, :], base[:, b, :, :], bias[:, 0:1, :].to_broadcast([TE, G, D]),
                                  ALU.add).then_inc(x2_based, 1)
                norm.scales(dve, t.g, b)
                dve.wait_ge(idx_ready, t.g + 3)
                dve.wait_ge(put[k], t.round(4) * (16 * G))
                dve.tensor_copy(put_idx[:, k, :], keep[:, k, :, C_PUT])
                dve.wait_ge(h_ready, t.g + 1)
                for j in range(G):
                    ins = dve.tensor_scalar(h[:, b, j, :], h[:, b, j, :], keep[:, k, j, C_W:C_W + 1], None, ALU.mult)
                ins.then_inc(weighted, 1)
                if t.ahead(2).exists():
                    take(t.ahead(2))

            def body(t):
                if t.ahead(2).exists():
                    prepare(t.ahead(2))
                b, k = t.slot(2), t.slot(4)
                dve.wait_ge(same_ready, t.g + 2)
                dve.wait_ge(turned, t.g + 1)
                dve.wait_ge(run_ready, t.g * 2 + 4)
                for c in range(DC):
                    dve.tensor_tensor_scan(run[:, b, c, :], same[:, b, :], p_t[b][c][:, 0:GE],
                                           run[:, 1 - b, c, GE - 1:GE], ALU.mult, ALU.add).then_inc(run_ready, 1)
                dve.wait_ge(x2_based, t.g + 1)
                for c in range(2):
                    dve.wait_ge(o_mm, t.g * 2 + c + 1)
                    ins = dve.tensor_tensor(x2[:, k, 2 * c:2 * c + 2, :], x2[:, k, 2 * c:2 * c + 2, :],
                                            p_o[c][:, :, :], ALU.add)
                    ins.then_inc(summed, 1)
                dve.wait_ge(summed, t.g * 2 + 4)
                before = t.ahead(-2)
                dve.wait_ge(put[before.slot(4)], (before.round(4) + 1) * (16 * G))
                dve.tensor_tensor(x3[:, b, :, :], x2[:, k, :, :],
                                  bias[:, 1:2, :].to_broadcast([TE, G, D]), ALU.add).then_inc(x3_ready, 1)

            dve.memset(run[:, 1, :, GE - 1], 0.0).then_inc(run_ready, 4)
            dve.wait_ge(w_in, 48)
            dve.sem_inc(same_mm, 4)
            for k in range(4):
                dve.sem_inc(x2_out[k], 16)
            take(first[0])
            take(first[1])
            prepare(first[0])
            prepare(first[1])
            groups(dve, body)

        @block.scalar
        def _(act):
            def prepare(t):
                b = t.slot(2)
                norm.root(act, t.g, b)
                norm.rows_out(act, t.g, b, h[:, b, :, :], x[:, b, :, :]).then_inc(h_ready, 1)

            def mask(t):
                act.wait_ge(same_mm, t.g + 5)
                act.copy(same[:, t.slot(2), :], p_s[:, 0:GE]).then_inc(same_ready, 1)

            def body(t):
                if t.ahead(1).exists():
                    mask(t.ahead(1))
                if t.ahead(2).exists():
                    prepare(t.ahead(2))
                k = t.slot(4)
                act.wait_ge(summed, t.g * 2 + 4)
                act.dma_start(rows_of(x2_dram, t.g, G, TE), x2[:, k, :, :]).then_inc(x2_out[k], 16)

            prepare(first[0])
            mask(first[0])
            prepare(first[1])
            groups(act, body)
            for k in range(4):
                act.wait_ge(x2_out[k], 16 * (NG // 4 + 1))

        @block.tensor
        def _(pe):
            def turn(t):
                b, k = t.slot(2), t.slot(4)
                pe.wait_ge(idx_ready, t.g + 3)
                pe.wait_ge(same_ready, t.g + 1)
                for j in range(G):
                    mm = pe.matmul(p_s[:, j * TE:(j + 1) * TE],
                                   keep[:, k, j, C_SAME:C_SAME + 1].to_broadcast([TE, P]),
                                   K["ident"][0:TE, 0:TE], start=True, stop=True)
                mm.then_inc(same_mm, 1)
                pe.wait_ge(weighted, t.g + 1)
                pe.wait_ge(run_ready, t.g * 2 + 2)
                for c in range(DC):
                    for j in range(G):
                        mm = pe.transpose(p_t[b][c][:, j * TE:(j + 1) * TE], h[:, b, j, c * P:(c + 1) * P],
                                          K["ident"][0:TE, 0:TE])
                mm.then_inc(turned, 1)

            def body(t):
                b = t.slot(2)
                if t.ahead(1).exists():
                    turn(t.ahead(1))
                pe.wait_ge(run_ready, t.g * 2 + 6)
                for c in range(2):
                    pe.wait_ge(summed, t.g * 2 + c + 1)
                    for jj in range(2):
                        j = 2 * c + jj
                        for k in range(DC):
                            mm = pe.matmul(p_o[c][:, jj, :], run[:, b, k, j * TE:(j + 1) * TE], w[:, k, :],
                                           start=(k == 0), stop=(k == DC - 1))
                    mm.then_inc(o_mm, 1)

            pe.wait_ge(w_in, 48)
            pe.sem_inc(same_ready, 1)
            pe.sem_inc(summed, 2)
            turn(first[0])
            groups(pe, body)


def attention_scores(nc, K, A, V, rec_d, x2_dram):
    NG = V["edges"] // GE
    NHEAD, DH = A["L2_gnn_a_src"].shape
    WS = D + NHEAD
    with ExitStack() as ctx:
        def sb(name, shape, dt=F32):
            return ctx.enter_context(nc.sbuf_tensor(name, shape, dt))

        def pb(name, shape, dt=F32):
            return ctx.enter_context(nc.psum_tensor(name, shape, dt))

        sem = ctx.enter_context(signals(nc, "as"))
        w = sb("as_w", [P, DC, D])
        w_t = sb("as_w_t", [P, DC, WS])
        a_col = sb("as_a_col", [P, DC])
        a_blocks = sb("as_a_blocks", [P, DC, NHEAD])
        a_dst = sb("as_a_dst", [TE, D])
        w_edge = sb("as_w_edge", [4, D])
        bias = sb("as_bias", [TE, D])
        rec = sb("as_rec", [TE, 2, G, RD])
        idx = sb("as_idx", [TE, 2, 2, G], I32)
        x = sb("as_x", [TE, 2, 2 * G, D])
        h = sb("as_h", [TE, 2 * G, D])
        h_t = sb("as_h_t", [P, 2 * DC, GE])
        attr_t = sb("as_attr_t", [4, 2, GE])
        enc = sb("as_enc", [TE, 2, D])
        score = sb("as_score", [TE, 2, G, NHEAD])
        score_l = sb("as_score_l", [TE, 2, G, NHEAD])
        p_a = pb("as_p_a", [P, 512])
        p_t = [pb(f"as_p_t{c}", [P, 512]) for c in range(DC)]
        p_src = [pb(f"as_p_src{c}", [TE, 512]) for c in range(2)]
        p_dst = [pb(f"as_p_dst{c}", [TE, 2, D]) for c in range(2)]
        norm = Norm(nc, ctx, "as", sem, TE, 2 * G, K["eps"])

        w_in = sem("w_in")
        setup = sem("setup")
        w_turned = sem("w_turned")
        w_ready = sem("w_ready")
        rec_in = [sem(f"rec_in{b}") for b in range(2)]
        x_in = [sem(f"x_in{b}") for b in range(2)]
        idx_ready = sem("idx_ready")
        h_ready = sem("h_ready")
        attr_turned = sem("attr_turned")
        small_read = sem("small_read")
        turned = sem("turned")
        h_t_ready = sem("h_t_ready")
        src_mm = sem("src_mm")
        dst_mm = sem("dst_mm")
        src_kept = sem("src_kept")
        enc_shifted = sem("enc_shifted")
        enc_scaled = sem("enc_scaled")
        enc_summed = sem("enc_summed")
        score_summed = sem("score_summed")
        score_ready = sem("score_ready")
        score_turned = sem("score_turned")
        passed = sem("passed")
        block = ctx.enter_context(nc.Block())

        def over_groups(eng, body):
            with eng.Fori(0, NG // 2 - 1) as i:
                for b in range(2):
                    body(i * 2 + b, i, b, True)
            for b in range(2):
                body(NG - 2 + b, NG // 2 - 1, b, False)

        @block.sync
        def _(sp):
            sp.dma_start(w[:, :, :], A["L2_gnn_W"].rearrange("(k p) n -> p k n", p=P)).then_inc(w_in, 16)
            with nc.allow_non_contiguous_dma(reason="a few small weights"):
                sp.dma_start(a_col[:, :], A["L2_gnn_a_src"].rearrange("h d -> (h d)").rearrange("(k p) -> p k", p=P)) \
                    .then_inc(w_in, 16)
                sp.dma_start(w_edge[0:3, :], A["L2_gnn_edge_W"].rearrange("n c -> c n")).then_inc(w_in, 16)
            sp.dma_start(w_edge[3:4, :], broadcast_row(A["L2_gnn_edge_b"], 1)).then_inc(w_in, 16)
            sp.dma_start(a_dst[:, :], broadcast_row(A["L2_gnn_a_dst"].rearrange("h d -> (h d)"), TE)).then_inc(w_in, 16)
            sp.dma_start(bias[:, :], broadcast_row(A["L2_gnn_bias"], TE)).then_inc(w_in, 16)
            for b in range(2):
                sp.dma_start(rec[:, b, :, :], rows_of(rec_d, b, G, TE)).then_inc(rec_in[b], 16)

            def body(g, i, b, more):
                if more:
                    sp.wait_ge(attr_turned, g + 1)
                    sp.dma_start(rec[:, b, :, :], rows_of(rec_d, g + 2, G, TE)).then_inc(rec_in[b], 16)

            over_groups(sp, body)

        @block.gpsimd
        def _(pool):
            pool.memset(a_blocks[:, :, :], 1.0).then_inc(setup, 1)
            pool.wait_ge(setup, 1)
            pool.affine_select(out=a_blocks[:, :, :], in_=a_blocks[:, :, :], compare_op=ALU.is_ge, fill=0.0,
                               base=0, pattern=[[P, DC], [-DH, NHEAD]], channel_multiplier=1).then_inc(setup, 1)
            pool.wait_ge(setup, 2)
            pool.affine_select(out=a_blocks[:, :, :], in_=a_blocks[:, :, :], compare_op=ALU.is_ge, fill=0.0,
                               base=DH - 1, pattern=[[-P, DC], [DH, NHEAD]], channel_multiplier=-1).then_inc(setup, 1)

            def fetch(g, b):
                pool.wait_ge(idx_ready, g + 1)
                pool.sem_inc(passed, 1)
                for j in range(G):
                    for s in range(2):
                        pool.indirect_dma_start(x[:, b, s * G + j, :], None, x2_dram[:, :],
                                                IOA(idx[:, b, s, j:j + 1], 0), bounds_check=x2_dram.shape[0] - 1,
                                                oob_is_err=False).then_inc(x_in[b], 16)

            def body(g, i, b, more):
                if more:
                    fetch(g + 2, b)

            for b in range(2):
                fetch(b, b)
            over_groups(pool, body)

        @block.vector
        def _(dve):
            def take(g, i, b):
                dve.wait_ge(rec_in[b], (i + 1) * 16)
                dve.tensor_copy(idx[:, b, 0, :], rec[:, b, :, D_SLOT_S])
                dve.tensor_copy(idx[:, b, 1, :], rec[:, b, :, D_SLOT_D]).then_inc(idx_ready, 1)

            dve.wait_ge(w_in, 96)
            for b in range(2):
                take(b, 0, b)
            dve.wait_ge(setup, 3)
            for k in range(DC):
                ins = dve.tensor_scalar(a_blocks[:, k, :], a_blocks[:, k, :], a_col[:, k:k + 1], None, ALU.mult)
            ins.then_inc(setup, 1)
            dve.wait_ge(w_turned, 1)
            for k in range(DC):
                ins = dve.tensor_copy(w_t[:, k, :], p_t[k][:, 0:WS])
            ins.then_inc(w_ready, 1)

            def body(g, i, b, more):
                dve.wait_ge(x_in[b], (i + 1) * (32 * G))
                norm.statistics(dve, g, b, x[:, b, :, :])
                norm.scales(dve, g, b)
                dve.tensor_tensor(V["base"][:, bass.ds(g * G, G), :], x[:, b, G:2 * G, :],
                                  bias[:, :].unsqueeze(1).to_broadcast([TE, G, D]), ALU.add)
                for s in range(2):
                    dve.wait_ge(turned, g * 2 + s + 1)
                    dve.tensor_copy(h_t[:, s * DC, :], p_t[0][:, 0:GE]).then_inc(h_t_ready, 1)
                for j in range(G):
                    dve.wait_ge(dst_mm, g * G + j + 1)
                    dve.scalar_tensor_tensor(out=enc[:, j % 2, :], in0=p_dst[j % 2][:, 1, :], scalar=0.0,
                                             in1=a_dst[:, :], op0=ALU.max, op1=ALU.add).then_inc(enc_shifted, 1)
                    dve.wait_ge(enc_shifted, g * G + j + 1)
                    dve.tensor_tensor(enc[:, j % 2, :], enc[:, j % 2, :], p_dst[j % 2][:, 0, :], ALU.mult) \
                       .then_inc(enc_scaled, 1)
                    dve.wait_ge(enc_scaled, g * G + j + 3)
                    dve.tensor_reduce(score[:, b, j, :], enc[:, j % 2, :].rearrange("p (h d) -> p h d", h=NHEAD),
                                      AX.X, ALU.add).then_inc(enc_summed, 1)
                dve.wait_ge(enc_summed, g * G + G)
                dve.wait_ge(src_kept, g * G + G + 2)
                dve.tensor_tensor(score[:, b, :, :], score[:, b, :, :],
                                  V["proj"][:, bass.ds(g * G, G), D:WS], ALU.add).then_inc(score_summed, 1)
                dve.wait_ge(score_summed, g + 1)
                dve.scalar_tensor_tensor(out=score_l[:, b, :, :], in0=score[:, b, :, :], scalar=0.2,
                                         in1=score[:, b, :, :], op0=ALU.mult, op1=ALU.max).then_inc(score_ready, 1)
                if more:
                    take(g + 2, i + 1, b)

            over_groups(dve, body)

        @block.scalar
        def _(act):
            def body(g, i, b, more):
                act.wait_ge(attr_turned, g + 1)
                act.copy(attr_t[:, b, :], p_a[0:4, 0:GE]).then_inc(small_read, 1)
                norm.root(act, g, b)
                norm.rows_out(act, g, b, h[:, :, :], x[:, b, :, :]).then_inc(h_ready, 1)
                for s in range(2):
                    act.wait_ge(turned, g * 2 + s + 1)
                    act.copy(h_t[:, s * DC + 1, :], p_t[1][:, 0:GE]).then_inc(h_t_ready, 1)
                for j in range(G):
                    act.wait_ge(src_mm, g * G + j + 1)
                    act.copy(V["proj"][:, bass.ds(g * G + j, 1), :].rearrange("p t n -> p (t n)"),
                             p_src[j % 2][:, 0:WS]).then_inc(src_kept, 1)
                act.wait_ge(score_turned, g + 1)
                act.copy(V["score_t"][:, bass.ds(g * GE, GE)], p_a[0:NHEAD, 0:GE]).then_inc(small_read, 1)

            over_groups(act, body)

        @block.tensor
        def _(pe):
            pe.wait_ge(w_in, 96)
            for k in range(DC):
                for n in range(DC):
                    pe.transpose(p_t[k][:, n * P:(n + 1) * P], w[:, n, k * P:(k + 1) * P], K["ident"][:, :])
            pe.wait_ge(setup, 4)
            for k in range(DC):
                for n in range(DC):
                    mm = pe.matmul(p_t[k][:, D:WS], w[:, n, k * P:(k + 1) * P], a_blocks[:, n, :],
                                   start=(n == 0), stop=(n == DC - 1))
            mm.then_inc(w_turned, 1)
            pe.sem_inc(small_read, 1)
            pe.sem_inc(src_kept, 2)
            pe.sem_inc(enc_scaled, 2)
            pe.wait_ge(w_ready, 1)
            pe.sem_inc(h_t_ready, 2)

            def body(g, i, b, more):
                pe.wait_ge(idx_ready, g + 1)
                pe.wait_ge(rec_in[b], (i + 1) * 16)
                pe.wait_ge(small_read, g * 2 + 1)
                for j in range(G):
                    mm = pe.transpose(p_a[0:4, j * TE:(j + 1) * TE], rec[:, b, j, D_A3:D_A3 + 4],
                                      K["ident"][0:TE, 0:TE])
                mm.then_inc(attr_turned, 1)
                pe.wait_ge(h_ready, g + 1)
                for s in range(2):
                    pe.wait_ge(h_t_ready, g * 4 + s * 2 + 2)
                    for c in range(DC):
                        for j in range(G):
                            mm = pe.transpose(p_t[c][:, j * TE:(j + 1) * TE], h[:, s * G + j, c * P:(c + 1) * P],
                                              K["ident"][0:TE, 0:TE])
                    mm.then_inc(turned, 1)
                pe.wait_ge(h_t_ready, g * 4 + 6)
                pe.wait_ge(small_read, g * 2 + 2)
                for j in range(G):
                    cols = slice(j * TE, (j + 1) * TE)
                    pe.wait_ge(enc_scaled, g * G + j + 1)
                    for k in range(DC):
                        pe.matmul(p_dst[j % 2][:, 0, :], h_t[:, DC + k, cols], w_t[:, k, 0:D],
                                  start=(k == 0), stop=(k == DC - 1))
                    pe.matmul(p_dst[j % 2][:, 1, :], attr_t[:, b, cols], w_edge[:, :], start=True, stop=True) \
                        .then_inc(dst_mm, 1)
                    pe.wait_ge(src_kept, g * G + j + 1)
                    for k in range(DC):
                        mm = pe.matmul(p_src[j % 2][:, 0:WS], h_t[:, k, cols], w_t[:, k, :],
                                       start=(k == 0), stop=(k == DC - 1))
                    mm.then_inc(src_mm, 1)
                pe.wait_ge(score_ready, g + 1)
                for j in range(G):
                    mm = pe.transpose(p_a[0:NHEAD, j * TE:(j + 1) * TE], score_l[:, b, j, :],
                                      K["ident"][0:TE, 0:TE])
                mm.then_inc(score_turned, 1)

            over_groups(pe, body)


def attention_weights(nc, K, V):
    E = V["edges"]
    NHEAD = V["score_t"].shape[0]
    with ExitStack() as ctx:
        def sb(name, shape, dt=F32):
            return ctx.enter_context(nc.sbuf_tensor(name, shape, dt))

        fence = sb("aw_fence", [NHEAD, E + 1])
        upto = sb("aw_upto", [NHEAD, E])
        top = sb("aw_top", [NHEAD, E])
        sem = ctx.enter_context(signals(nc, "aw"))
        step = sem("step")
        done = sem("done")
        block = ctx.enter_context(nc.Block())
        score = V["score_t"]

        @block.vector
        def _(dve):
            dve.memset(fence[:, E:E + 1], NEG)
            dve.tensor_scalar(fence[:, 0:E], K["same"][0:NHEAD, :], -1.0, -NEG, ALU.add, ALU.mult).then_inc(step, 1)
            dve.wait_ge(step, 1)
            dve.tensor_tensor_scan(upto[:, :], fence[:, 0:E], score[:, :], NEG, ALU.add, ALU.max).then_inc(step, 1)
            dve.wait_ge(step, 2)
            dve.tensor_tensor_scan(top[:, ::-1], fence[:, E:0:-1], upto[:, ::-1], NEG, ALU.add, ALU.max) \
               .then_inc(step, 1)
            dve.wait_ge(step, 3)
            dve.tensor_tensor(upto[:, :], score[:, :], top[:, :], ALU.subtract).then_inc(step, 1)

        @block.scalar
        def _(act):
            act.wait_ge(step, 4)
            act.activation(score[:, :], upto[:, :], ACT.Exp).then_inc(done, 1)
            act.wait_ge(done, 1)


def message_scores(nc, K, A, V, rec_d, x3_dram):
    NG = V["edges"] // GE
    N = x3_dram.shape[0]
    DM = A["L3_gnn_W_forward"].shape[0]
    NHEAD = A["L3_gnn_attn_forward"].shape[1]
    WS = DM + NHEAD
    with ExitStack() as ctx:
        def sb(name, shape, dt=F32):
            return ctx.enter_context(nc.sbuf_tensor(name, shape, dt))

        def pb(name, shape, dt=F32):
            return ctx.enter_context(nc.psum_tensor(name, shape, dt))

        sem = ctx.enter_context(signals(nc, "ms"))
        w = sb("ms_w", [DM, 2, D])
        attn = sb("ms_attn", [NHEAD, DM])
        attn_t = sb("ms_attn_t", [DM, NHEAD])
        w_t = sb("ms_w_t", [P, DC, 2, WS])
        rec = sb("ms_rec", [TE, 2, G, RD])
        way = sb("ms_way", [TE, 2, G, 2])
        idx = sb("ms_idx", [TE, 2, G], I32)
        x = sb("ms_x", [TE, 2, G, D])
        h = sb("ms_h", [TE, 2, G, D])
        h_t = sb("ms_h_t", [P, 2, DC, GE])
        scaled = sb("ms_scaled", [TE, 2, 2, G, WS])
        score = sb("ms_score", [TE, 2, G, NHEAD])
        score_l = sb("ms_score_l", [TE, 2, G, NHEAD])
        p_a = pb("ms_p_a", [P, 512])
        p_t = [pb(f"ms_p_t{c}", [P, 512]) for c in range(DC)]
        p_m = [pb(f"ms_p_m{c}", [TE, 2, 2, P]) for c in range(2)]
        norm = Norm(nc, ctx, "ms", sem, TE, G, K["eps"])

        w_in = sem("w_in")
        attn_turned = sem("attn_turned")
        attn_ready = sem("attn_ready")
        w_turned = sem("w_turned")
        w_ready = sem("w_ready")
        rec_in = [sem(f"rec_in{b}") for b in range(2)]
        x_in = [sem(f"x_in{b}") for b in range(2)]
        idx_ready = sem("idx_ready")
        h_ready = sem("h_ready")
        turned = sem("turned")
        h_t_ready = sem("h_t_ready")
        m_mm = sem("m_mm")
        m_scaled = sem("m_scaled")
        score_summed = sem("score_summed")
        score_ready = sem("score_ready")
        score_turned = sem("score_turned")
        score_kept = sem("score_kept")
        passed = sem("passed")
        block = ctx.enter_context(nc.Block())

        def over_groups(eng, body):
            with eng.Fori(0, NG // 2 - 1) as i:
                for b in range(2):
                    body(i * 2 + b, i, b, True)
            for b in range(2):
                body(NG - 2 + b, NG // 2 - 1, b, False)

        @block.sync
        def _(sp):
            sp.dma_start(w[:, 0, :], A["L3_gnn_W_forward"]).then_inc(w_in, 16)
            sp.dma_start(w[:, 1, :], A["L3_gnn_W_reverse"]).then_inc(w_in, 16)
            sp.dma_start(attn[:, :], A["L3_gnn_attn_forward"].rearrange("a h f -> (a h) f")).then_inc(w_in, 16)
            for b in range(2):
                sp.dma_start(rec[:, b, :, :], rows_of(rec_d, b, G, TE)).then_inc(rec_in[b], 16)

            def body(g, i, b, more):
                if more:
                    sp.wait_ge(idx_ready, g + 1)
                    sp.dma_start(rec[:, b, :, :], rows_of(rec_d, g + 2, G, TE)).then_inc(rec_in[b], 16)

            over_groups(sp, body)

        @block.gpsimd
        def _(pool):
            def fetch(g, b):
                pool.wait_ge(idx_ready, g + 1)
                pool.sem_inc(passed, 1)
                for j in range(G):
                    pool.indirect_dma_start(x[:, b, j, :], None, x3_dram[:, :], IOA(idx[:, b, j:j + 1], 0),
                                            bounds_check=N - 1, oob_is_err=False).then_inc(x_in[b], 16)

            def body(g, i, b, more):
                if more:
                    fetch(g + 2, b)

            for b in range(2):
                fetch(b, b)
            over_groups(pool, body)

        @block.vector
        def _(dve):
            def take(g, i, b):
                dve.wait_ge(rec_in[b], (i + 1) * 16)
                dve.tensor_copy(way[:, b, :, :], rec[:, b, :, D_A2:D_A2 + 2])
                dve.tensor_copy(idx[:, b, :], rec[:, b, :, D_SRC]).then_inc(idx_ready, 1)

            for b in range(2):
                take(b, 0, b)
            dve.wait_ge(attn_turned, 1)
            dve.tensor_copy(attn_t[:, :], p_a[0:DM, 0:NHEAD]).then_inc(attn_ready, 1)
            dve.wait_ge(w_turned, 1)
            for k in range(DC):
                ins = dve.tensor_copy(w_t[:, k, :, :].rearrange("p s n -> p (s n)"), p_t[k][:, 0:2 * WS])
            ins.then_inc(w_ready, 1)

            def body(g, i, b, more):
                dve.wait_ge(x_in[b], (i + 1) * (16 * G))
                norm.statistics(dve, g, b, x[:, b, :, :])
                norm.scales(dve, g, b)
                dve.wait_ge(turned, g + 1)
                dve.tensor_copy(h_t[:, b, 0, :], p_t[0][:, 0:GE]).then_inc(h_t_ready, 1)
                dve.wait_ge(m_scaled, g * 2 + 4)
                dve.tensor_tensor(V["proj"][:, bass.ds(g * G, G), 0:DM], scaled[:, b, 0, :, 0:DM],
                                  scaled[:, b, 1, :, 0:DM], ALU.add)
                dve.tensor_tensor(score[:, b, :, :], scaled[:, b, 0, :, DM:WS], scaled[:, b, 1, :, DM:WS],
                                  ALU.add).then_inc(score_summed, 1)
                dve.wait_ge(score_summed, g + 1)
                dve.scalar_tensor_tensor(out=score_l[:, b, :, :], in0=score[:, b, :, :], scalar=0.2,
                                         in1=score[:, b, :, :], op0=ALU.mult, op1=ALU.max).then_inc(score_ready, 1)
                if more:
                    take(g + 2, i + 1, b)

            over_groups(dve, body)

        @block.scalar
        def _(act):
            def body(g, i, b, more):
                norm.root(act, g, b)
                norm.rows_out(act, g, b, h[:, b, :, :], x[:, b, :, :]).then_inc(h_ready, 1)
                act.wait_ge(turned, g + 1)
                act.copy(h_t[:, b, 1, :], p_t[1][:, 0:GE]).then_inc(h_t_ready, 1)
                act.wait_ge(idx_ready, g + 1)
                for c in range(2):
                    act.wait_ge(m_mm, g * 2 + c + 1)
                    for jj in range(2):
                        for s in range(2):
                            ins = act.activation(scaled[:, b, s, 2 * c + jj, :], p_m[c][:, jj, s, 0:WS],
                                                 ACT.Identity, bias=0.0, scale=way[:, b, 2 * c + jj, s:s + 1])
                    ins.then_inc(m_scaled, 1)
                act.wait_ge(score_turned, g + 1)
                act.copy(V["score_t"][0:NHEAD, bass.ds(g * GE, GE)], p_a[0:NHEAD, 0:GE]).then_inc(score_kept, 1)

            over_groups(act, body)

        @block.tensor
        def _(pe):
            pe.wait_ge(w_in, 48)
            pe.transpose(p_a[0:DM, 0:NHEAD], attn[:, :], K["ident"][0:NHEAD, 0:NHEAD]).then_inc(attn_turned, 1)
            for k in range(DC):
                for s in range(2):
                    pe.transpose(p_t[k][:, s * WS:s * WS + DM], w[:, s, k * P:(k + 1) * P], K["ident"][0:DM, 0:DM])
            pe.wait_ge(attn_ready, 1)
            for k in range(DC):
                for s in range(2):
                    mm = pe.matmul(p_t[k][:, s * WS + DM:(s + 1) * WS], w[:, s, k * P:(k + 1) * P], attn_t[:, :],
                                   start=True, stop=True)
            mm.then_inc(w_turned, 1)
            pe.wait_ge(w_ready, 1)
            pe.sem_inc(h_t_ready, 2)
            pe.sem_inc(m_scaled, 2)
            pe.sem_inc(score_kept, 1)

            def body(g, i, b, more):
                pe.wait_ge(h_ready, g + 1)
                pe.wait_ge(h_t_ready, g * 2 + 2)
                for c in range(DC):
                    for j in range(G):
                        mm = pe.transpose(p_t[c][:, j * TE:(j + 1) * TE], h[:, b, j, c * P:(c + 1) * P],
                                          K["ident"][0:TE, 0:TE])
                mm.then_inc(turned, 1)
                pe.wait_ge(h_t_ready, g * 2 + 4)
                for c in range(2):
                    pe.wait_ge(m_scaled, g * 2 + c + 1)
                    for jj in range(2):
                        j = 2 * c + jj
                        for k in range(DC):
                            mm = pe.matmul(p_m[c][:, jj, :, 0:WS], h_t[:, b, k, j * TE:(j + 1) * TE],
                                           w_t[:, k, :, :], start=(k == 0), stop=(k == DC - 1))
                    mm.then_inc(m_mm, 1)
                pe.wait_ge(score_ready, g + 1)
                pe.wait_ge(score_kept, g + 1)
                for j in range(G):
                    mm = pe.transpose(p_a[0:NHEAD, j * TE:(j + 1) * TE], score_l[:, b, j, :],
                                      K["ident"][0:TE, 0:TE])
                mm.then_inc(score_turned, 1)

            over_groups(pe, body)


def message_weights(nc, V, NHEAD):
    with ExitStack() as ctx:
        top = ctx.enter_context(nc.sbuf_tensor("mw_top", [NHEAD, 2], F32))
        sem = ctx.enter_context(signals(nc, "mw"))
        step = sem("step")
        done = sem("done")
        block = ctx.enter_context(nc.Block())
        score = V["score_t"][0:NHEAD, :]

        @block.vector
        def _(dve):
            dve.tensor_reduce(top[:, 0:1], score, AX.X, ALU.max).then_inc(step, 1)
            dve.wait_ge(step, 1)
            dve.tensor_scalar(top[:, 1:2], top[:, 0:1], -1.0, None, ALU.mult).then_inc(step, 1)

        @block.scalar
        def _(act):
            act.wait_ge(step, 2)
            act.activation(score, score, ACT.Exp, bias=top[:, 1:2], scale=1.0).then_inc(done, 1)
            act.wait_ge(done, 1)


def attention_sums(nc, K, V, name, NHEAD, per_head, guard, keep, rec_d, out):
    N = out.shape[0]
    NG = V["edges"] // GE
    DH = D // NHEAD
    with ExitStack() as ctx:
        def sb(what, shape, dt=F32):
            return ctx.enter_context(nc.sbuf_tensor(f"{name}_{what}", shape, dt))

        def pb(what, shape, dt=F32):
            return ctx.enter_context(nc.psum_tensor(f"{name}_{what}", shape, dt))

        sem = ctx.enter_context(signals(nc, name))
        rec = sb("rec", [TE, 2, G, RD])
        idx = sb("idx", [TE, 2, G], I32)
        ex_t = sb("ex_t", [NHEAD, 2, GE])
        ex = sb("ex", [TE, 2, G, NHEAD])
        m = sb("m", [TE, 2, G, D])
        run = sb("run", [P, 2, DC, GE])
        den_t = sb("den_t", [NHEAD, 2, GE])
        den = sb("den", [TE, 2, G, NHEAD])
        rows = sb("rows", [TE, 2, G, D])
        p_e = pb("p_e", [TE, 512])
        p_d = pb("p_d", [TE, 512])
        p_t = [pb(f"p_t{c}", [P, 512]) for c in range(DC)]
        p_r = [pb(f"p_r{c}", [TE, 2, D]) for c in range(2)]

        rec_in = [sem(f"rec_in{b}") for b in range(2)]
        put = [sem(f"put{b}") for b in range(2)]
        idx_ready = sem("idx_ready")
        ex_t_ready = sem("ex_t_ready")
        pe_passed = sem("pe_passed")
        ex_turned = sem("ex_turned")
        ex_ready = sem("ex_ready")
        m_ready = sem("m_ready")
        turned = sem("turned")
        run_ready = sem("run_ready")
        den_ready = sem("den_ready")
        den_turned = sem("den_turned")
        den_read = sem("den_read")
        den_done = sem("den_done")
        rows_turned = sem("rows_turned")
        rows_scaled = sem("rows_scaled")
        rows_ready = sem("rows_ready")
        rows_kept = sem("rows_kept")
        passed = sem("passed")
        block = ctx.enter_context(nc.Block())

        def over_groups(eng, body):
            with eng.Fori(0, NG // 2) as i:
                for b in range(2):
                    body(i * 2 + b, i, b)

        @block.sync
        def _(sp):
            sp.sem_inc(idx_ready, 2)

            def body(g, i, b):
                sp.wait_ge(idx_ready, g + 1)
                sp.dma_start(rec[:, b, :, :], rows_of(rec_d, g, G, TE)).then_inc(rec_in[b], 16)

            over_groups(sp, body)

        @block.gpsimd
        def _(pool):
            for b in range(2):
                open_slot(pool, K, put[b], 16 * G)

            def body(g, i, b):
                pool.wait_ge(rows_ready, g + 1)
                pool.sem_inc(passed, 1)
                for j in range(G):
                    pool.indirect_dma_start(out[:, :], IOA(idx[:, b, j:j + 1], 0), rows[:, b, j, :], None,
                                            bounds_check=N - 1, oob_is_err=False).then_inc(put[b], 16)

            over_groups(pool, body)
            for b in range(2):
                pool.wait_ge(put[b], 16 * G * (NG // 2 + 1))

        @block.vector
        def _(dve):
            dve.memset(den_t[:, 1, GE - 1:GE], 0.0).then_inc(den_ready, 1)
            dve.memset(run[:, 1, :, GE - 1], 0.0).then_inc(run_ready, 2)

            def weigh(g, b):
                dve.wait_ge(ex_ready, g + 2)
                source = V["proj"][:, bass.ds(g * G, G), 0:D if per_head else DH]
                source = source.rearrange("p t (h d) -> p t h d", h=NHEAD) if per_head else \
                    source.unsqueeze(2).to_broadcast([TE, G, NHEAD, DH])
                dve.tensor_tensor(m[:, b, :, :].rearrange("p t (h d) -> p t h d", h=NHEAD), source,
                                  ex[:, b, :, :].unsqueeze(3).to_broadcast([TE, G, NHEAD, DH]),
                                  ALU.mult).then_inc(m_ready, 1)

            def body(g, i, b):
                weigh(g, b)
                dve.wait_ge(rec_in[b], (i + 1) * 16)
                dve.wait_ge(put[b], (i + 1) * (16 * G))
                dve.tensor_copy(idx[:, b, :], rec[:, b, :, D_PUT]).then_inc(idx_ready, 1)
                dve.wait_ge(den_ready, g + 1)
                dve.tensor_tensor_scan(den_t[:, b, :], K["same"][0:NHEAD, bass.ds(g * GE, GE)], ex_t[:, b, :],
                                       den_t[:, 1 - b, GE - 1:GE], ALU.mult, ALU.add).then_inc(den_ready, 1)
                dve.wait_ge(turned, g + 1)
                dve.wait_ge(run_ready, g * 2 + 2)
                for c in range(DC):
                    dve.tensor_tensor_scan(run[:, b, c, :], K["same"][:, bass.ds(g * GE, GE)], p_t[c][:, 0:GE],
                                           run[:, 1 - b, c, GE - 1:GE], ALU.mult, ALU.add).then_inc(run_ready, 1)
                dve.wait_ge(den_turned, g + 1)
                dve.tensor_scalar(den[:, b, :, :].rearrange("p t h -> p (t h)"), p_d[:, 0:G * NHEAD], guard[1], None,
                                  guard[0]).then_inc(den_read, 1)
                dve.wait_ge(den_read, g + 2)
                dve.reciprocal(den[:, b, :, :], den[:, b, :, :]).then_inc(den_done, 1)
                dve.wait_ge(den_done, g + 1)
                dve.wait_ge(rows_kept, g + 1)
                for c in range(2):
                    dve.wait_ge(rows_turned, g * 2 + c + 1)
                    dve.tensor_tensor(rows[:, b, 2 * c:2 * c + 2, :].rearrange("p t (h d) -> p t h d", h=NHEAD),
                                      p_r[c][:, :, :].rearrange("p t (h d) -> p t h d", h=NHEAD),
                                      den[:, b, 2 * c:2 * c + 2, :].unsqueeze(3).to_broadcast([TE, 2, NHEAD, DH]),
                                      ALU.mult).then_inc(rows_scaled, 1)
                dve.wait_ge(rows_scaled, g * 2 + 4)
                dve.tensor_tensor(rows[:, b, :, :], rows[:, b, :, :], V["base"][:, bass.ds(g * G, G), :], ALU.add) \
                   .then_inc(rows_ready, 1)

            over_groups(dve, body)

        @block.scalar
        def _(act):
            act.sem_inc(rows_kept, 2)

            def body(g, i, b):
                act.copy(ex_t[:, b, :], V["score_t"][0:NHEAD, bass.ds(g * GE, GE)]).then_inc(ex_t_ready, 1)
                act.wait_ge(ex_turned, g + 1)
                act.copy(ex[:, b, :, :].rearrange("p t h -> p (t h)"), p_e[:, 0:G * NHEAD]).then_inc(ex_ready, 1)
                act.wait_ge(rows_ready, g + 1)
                if keep:
                    act.copy(V["base"][:, bass.ds(g * G, G), :].rearrange("p t d -> p (t d)"),
                             rows[:, b, :, :].rearrange("p t d -> p (t d)")).then_inc(rows_kept, 1)
                else:
                    act.sem_inc(rows_kept, 1)

            over_groups(act, body)

        @block.tensor
        def _(pe):
            pe.sem_inc(ex_ready, 1)
            pe.sem_inc(den_read, 1)
            pe.sem_inc(rows_scaled, 2)

            def body(g, i, b):
                pe.wait_ge(ex_t_ready, g + 1)
                pe.wait_ge(ex_ready, g + 1)
                pe.sem_inc(pe_passed, 1)
                for j in range(G):
                    mm = pe.transpose(p_e[:, j * NHEAD:(j + 1) * NHEAD], ex_t[:, b, j * TE:(j + 1) * TE],
                                      K["ident"][0:NHEAD, 0:NHEAD])
                mm.then_inc(ex_turned, 1)
                pe.wait_ge(m_ready, g + 1)
                pe.wait_ge(run_ready, g * 2 + 2)
                for c in range(DC):
                    for j in range(G):
                        mm = pe.transpose(p_t[c][:, j * TE:(j + 1) * TE], m[:, b, j, c * P:(c + 1) * P],
                                          K["ident"][0:TE, 0:TE])
                mm.then_inc(turned, 1)
                pe.wait_ge(den_ready, g + 2)
                pe.wait_ge(den_read, g + 1)
                pe.sem_inc(pe_passed, 1)
                for j in range(G):
                    mm = pe.transpose(p_d[:, j * NHEAD:(j + 1) * NHEAD], den_t[:, b, j * TE:(j + 1) * TE],
                                      K["ident"][0:NHEAD, 0:NHEAD])
                mm.then_inc(den_turned, 1)
                pe.wait_ge(run_ready, g * 2 + 4)
                for c in range(2):
                    pe.wait_ge(rows_scaled, g * 2 + c + 1)
                    for jj in range(2):
                        j = 2 * c + jj
                        for k in range(DC):
                            mm = pe.transpose(p_r[c][:, jj, k * P:(k + 1) * P], run[:, b, k, j * TE:(j + 1) * TE],
                                              K["ident"][:, :])
                    mm.then_inc(rows_turned, 1)

            over_groups(pe, body)


def gnn(nc, A, out):
    N = A["x"].shape[0]
    E = A["src"].shape[0]
    NT = E // TE
    NH = -(-N // LO) + 1
    table = nc.dram_tensor("node_table", [NH * LO, 4], F32).ap()
    agg0 = nc.dram_tensor("agg0", [N, D], F32).ap()
    rec_d = nc.dram_tensor("rec_by_dst", [E, RD], F32).ap()
    rec_c = nc.dram_tensor("rec_by_node", [2 * E, RC], F32).ap()
    x1 = nc.dram_tensor("x1_by_node", [N, D], F32).ap()
    x2 = nc.dram_tensor("x2_by_place", [2 * E, D], F32).ap()
    msg = nc.dram_tensor("messages0", [E, D], F32).ap()
    with ExitStack() as ctx:
        def sb(name, shape, dt=F32):
            return ctx.enter_context(nc.sbuf_tensor(name, shape, dt))

        K = {
            "token": sb("token", [1, 32, 4]), "token_n": -1,
            "ident": sb("ident", [P, P]), "iota_p": sb("iota_p", [P, 1]), "eps": sb("eps_col", [P, 1]),
            "dst_col": sb("dst_col", [TE, NT + 2 * G], I32), "src_col": sb("src_col", [TE, NT + 2 * G], I32),
            "same": sb("same_dst", [P, E], BF16),
            "ord": sb("ord", [TE, NT, 2]),
        }
        constants(nc, K)
        rank_edges(nc, K, A["dst"], A["src"], table, agg0)
        with ExitStack() as ctx_r:
            R = Records(nc, ctx_r, ctx_r.enter_context(signals(nc, "rc")), K, A, table, rec_d, rec_c)
            edge_messages(nc, K, A, R, msg)
            aggregate_messages(nc, K, msg, rec_d, agg0)
            node_network(nc, K, A, R, agg0, x1, out)
        relation_layer(nc, K, A, rec_c, x1, x2, out)
        H2, H3 = A["L2_gnn_a_src"].shape[0], A["L3_gnn_attn_forward"].shape[1]
        V = {
            "edges": E, "proj": sb("proj", [TE, NT, D + H2]), "base": sb("base", [TE, NT, D]),
            "score_t": sb("score_t", [max(H2, H3), E]),
        }
        attention_scores(nc, K, A, V, rec_d, x2)
        attention_weights(nc, K, V)
        attention_sums(nc, K, V, "a2", H2, True, (ALU.max, 1e-10), True, rec_d, out)
        message_scores(nc, K, A, V, rec_d, out)
        message_weights(nc, V, H3)
        attention_sums(nc, K, V, "a3", H3, False, (ALU.add, 1e-10), False, rec_d, out)


_INS = ['x', 'src', 'dst', 'edge_attr_2', 'edge_attr_256', 'edge_attr_3', 'edge_type_11',
        'L0_gnn_We1', 'L0_gnn_be1', 'L0_gnn_We2', 'L0_gnn_be2', 'L0_gnn_Wn1', 'L0_gnn_bn1', 'L0_gnn_Wn2',
        'L0_gnn_bn2', 'L0_gnn_eps', 'L1_gnn_weight', 'L1_gnn_bias', 'L1_gnn_alpha', 'L2_gnn_W', 'L2_gnn_a_src',
        'L2_gnn_a_dst', 'L2_gnn_edge_W', 'L2_gnn_edge_b', 'L2_gnn_bias', 'L3_gnn_W_forward', 'L3_gnn_W_reverse',
        'L3_gnn_attn_forward']


def kernel(**inputs):
    import numpy as _np
    import concourse.bacc as _bacc
    from concourse import mybir as _mybir
    from concourse.bass_utils import run_bass_kernel_spmd as _run

    nc = _bacc.Bacc("TRN2", target_bir_lowering=False, num_devices=1)
    arrays, args = {}, {}
    for name in _INS:
        a = _np.ascontiguousarray(inputs[name])
        arrays[f"in_{name}"] = a
        args[name] = nc.dram_tensor(f"in_{name}", a.shape, _mybir.dt.from_np(a.dtype), kind="ExternalInput").ap()
    out = nc.dram_tensor("out_x", inputs["x"].shape, _mybir.dt.float32, kind="ExternalOutput").ap()
    gnn(nc, args, out)
    r = _run(nc, [arrays], core_ids=[0])
    return r.results[0]["out_x"]
```

```python
from contextlib import ExitStack

import concourse.bass as bass
from concourse import mybir

F32 = mybir.dt.float32
BF16 = mybir.dt.bfloat16
I32 = mybir.dt.int32
ALU = mybir.AluOpType
ACT = mybir.ActivationFunctionType
AX = mybir.AxisListType
IOA = bass.IndirectOffsetOnAxis

P = 128
D = 256
DC = D // P
HID = 512
HC = HID // P
TE = 125
G = 4
GP = 2 * G
GE = G * TE
LO = 256
EPS = 1e-5
SKIP = 1 << 15
NEG = -1.0e38

RD = 16
D_SRC, D_DST, D_PUT, D_EDGE, D_SAME, D_A2, D_A3, D_ONE = 0, 1, 2, 4, 5, 6, 8, 11
RC = 8
C_PEER, C_PUT, C_W, C_SAME = 0, 1, 2, 3


class Step:

    def __init__(self, i, r, unroll, n):
        self.i, self.r, self.unroll, self.n = i, r, unroll, n
        self.g = i * unroll + r

    def ahead(self, k):
        r = self.r + k
        return Step(self.i + r // self.unroll, r % self.unroll, self.unroll, self.n)

    def exists(self):
        return not isinstance(self.g, int) or self.g < self.n

    def slot(self, ring):
        return self.r % ring

    def round(self, ring):
        return self.i * (self.unroll // ring) + self.r // ring + 1


def over_groups(eng, n, unroll, peel, body):
    assert (n - peel) % unroll == 0
    with eng.Fori(0, (n - peel) // unroll) as i:
        for r in range(unroll):
            body(Step(i, r, unroll, n))
    for g in range(n - peel, n):
        body(Step(g // unroll, g % unroll, unroll, n))


def signals(nc, K, stage):
    def sem(what):
        K["signals"].append(nc.alloc_semaphore(f"{stage}_{what}"))
        return K["signals"][-1]

    return sem


def reuse_signals(nc, K):
    nc.clear_and_free_semaphores(K["signals"])
    nc.all_engine_barrier()
    K["signals"] = []


def constants(nc, K):
    with ExitStack() as ctx:
        sem = signals(nc, K, "const")
        filled = sem("filled")
        done = sem("done")
        block = ctx.enter_context(nc.Block())

        @block.gpsimd
        def _(pool):
            pool.memset(K["ident"][:, :], 0.0).then_inc(filled, 1)
            pool.wait_ge(filled, 1)
            pool.affine_select(out=K["ident"][:, :], in_=K["ident"][:, :], compare_op=ALU.not_equal, fill=1.0,
                               base=0, pattern=[[-1, P]], channel_multiplier=1).then_inc(done, 1)
            pool.iota(K["iota_p"][:, :], [[0, 1]], base=0, channel_multiplier=1,
                      allow_small_or_imprecise_dtypes=True).then_inc(done, 1)
            pool.memset(K["eps"][:, :], EPS).then_inc(done, 1)
            pool.wait_ge(done, 3)


def rank_edges(nc, K, dst, src, table, zero_table):
    E = dst.shape[0]
    NT = E // TE
    NH = table.shape[0] // LO
    S = 2
    M = G * S
    with ExitStack() as ctx:
        def sb(name, shape, dt=F32):
            return ctx.enter_context(nc.sbuf_tensor(name, shape, dt))

        def pb(name, shape, dt=F32):
            return ctx.enter_context(nc.psum_tensor(name, shape, dt))

        sem = signals(nc, K, "rk")
        key_row = [sb(f"rk_key_row{s}", [P, E], I32) for s in range(S)]
        hi_row = [sb(f"rk_hi_row{s}", [NH, E], I32) for s in range(S)]
        key40 = sb("rk_key40", [NT, S, TE], I32)
        part40 = sb("rk_part40", [NT, 2, S, TE], I32)
        key_f = sb("rk_key_f", [NT, 3, S, TE])
        key_col = sb("rk_key_col", [TE, 3, S, NT])
        iota_hi = sb("rk_iota_hi", [P, NH], BF16)
        iota_lo = sb("rk_iota_lo", [P, LO], BF16)
        before = sb("rk_before", [TE, TE])
        above = sb("rk_above", [NH, NH])
        ones = sb("rk_ones", [NH, LO])
        zero_b = sb("rk_zero_b", [P, LO], BF16)
        hot_hi = sb("rk_hot_hi", [TE, 2, M, NH], BF16)
        hot_lo = sb("rk_hot_lo", [TE, 2, M, LO], BF16)
        hot_hi_t = sb("rk_hot_hi_t", [NH, 2, M, TE])
        run = sb("rk_run", [NH, 4, LO])
        junk_t = sb("rk_junk_t", [TE, 2, M, TE])
        junk_r = sb("rk_junk_r", [TE, 2, M, LO])
        in_tile = sb("rk_in_tile", [TE, 2, M])
        in_run = sb("rk_in_run", [TE, 2, M])
        hist = sb("rk_hist", [NH, S, LO])
        incl = sb("rk_incl", [NH, S, LO])
        total = sb("rk_total", [NH, S])
        carry = sb("rk_carry", [NH, S])
        tab = sb("rk_tab", [NH, LO, 4])
        NZ = 25
        zeros = sb("rk_zeros", [80, NZ * D])
        p_hist = [pb(f"rk_p_hist{s}", [NH, 512]) for s in range(S)]
        p_look = [pb(f"rk_p_look{m}", [TE, 512]) for m in range(4)]
        p_misc = pb("rk_p_misc", [P, 512])

        row_in = [sem(f"row_in{s}") for s in range(S)]
        key_in = sem("key_in")
        const_a = sem("const_a")
        const_ready = sem("const_ready")
        zeros_ready = sem("zeros_ready")
        step = sem("step")
        keys_split = sem("keys_split")
        keys_turned = sem("keys_turned")
        hist_zero = sem("hist_zero")
        hots_ready = sem("hots_ready")
        run_ready = sem("run_ready")
        looked_up = sem("looked_up")
        look_read = sem("look_read")
        hist_added = sem("hist_added")
        counted = sem("counted")
        totals_ready = sem("totals_ready")
        carry_ready = sem("carry_ready")
        tab_ready = sem("tab_ready")
        stored = sem("stored")
        block = ctx.enter_context(nc.Block())
        keys = (dst, src)

        def groups(eng, body):
            over_groups(eng, NT // G, 2, 2, body)

        @block.sync
        def _(sp):
            for s in range(S):
                sp.dma_start(key40[:, s, :], keys[s].rearrange("(t p) -> t p", p=TE)).then_inc(key_in, 16)
            for s in range(S):
                sp.dma_start(key_row[s][:, :], keys[s].rearrange("(a e) -> a e", a=1).to_broadcast([P, E])) \
                    .then_inc(row_in[s], 16)
            sp.wait_ge(zeros_ready, 1)
            rows = zero_table.rearrange("(p r) d -> p (r d)", p=80)
            NR = zero_table.shape[0] // 80 // NZ
            for r in range(NR):
                sp.dma_start(rows[:, r * NZ * D:(r + 1) * NZ * D], zeros[:, :]).then_inc(stored, 16)
            sp.wait_ge(tab_ready, 1)
            sp.dma_start(table.rearrange("(h l) c -> h (l c)", l=LO),
                         tab[:, :, :].rearrange("h l c -> h (l c)")).then_inc(stored, 16)
            sp.wait_ge(stored, 16 * (NR + 1))

        @block.gpsimd
        def _(pool):
            pool.memset(zeros[:, :], 0.0).then_inc(zeros_ready, 1)
            pool.memset(K["src_col"][:, NT:], 0)
            pool.memset(K["dst_col"][:, NT:], 0)
            pool.iota(iota_hi[:, :], [[1, NH]], base=0, channel_multiplier=0,
                      allow_small_or_imprecise_dtypes=True).then_inc(const_ready, 1)
            pool.iota(iota_lo[:, :], [[1, LO]], base=0, channel_multiplier=0,
                      allow_small_or_imprecise_dtypes=True).then_inc(const_ready, 1)
            pool.memset(before[:, :], 1.0).then_inc(const_a, 1)
            pool.memset(above[:, :], 1.0).then_inc(const_a, 1)
            pool.memset(ones[:, :], 1.0).then_inc(const_ready, 1)
            pool.memset(zero_b[:, :], 0.0).then_inc(const_ready, 1)
            pool.wait_ge(const_a, 2)
            pool.affine_select(out=before[:, :], in_=before[:, :], compare_op=ALU.is_gt, fill=0.0,
                               base=0, pattern=[[-1, TE]], channel_multiplier=1).then_inc(const_ready, 1)
            pool.affine_select(out=above[:, :], in_=above[:, :], compare_op=ALU.is_gt, fill=0.0,
                               base=0, pattern=[[1, NH]], channel_multiplier=-1).then_inc(const_ready, 1)

        @block.vector
        def _(dve):
            dve.wait_ge(key_in, 16 * S)
            dve.tensor_scalar(part40[:, 0, :, :], key40[:, :, :], 8, None, ALU.logical_shift_right)
            dve.tensor_scalar(part40[:, 1, :, :], key40[:, :, :], LO - 1, None, ALU.bitwise_and).then_inc(step, 1)
            dve.tensor_copy(key_f[:, 0, :, :], key40[:, :, :])
            dve.wait_ge(step, 1)
            dve.tensor_copy(key_f[:, 1:3, :, :].rearrange("t a s e -> t (a s e)"),
                            part40[:, :, :, :].rearrange("t a s e -> t (a s e)")).then_inc(keys_split, 1)
            dve.wait_ge(keys_turned, 1)
            dve.tensor_copy(key_col[:, :, :, :].rearrange("p a s t -> p (a s t)"),
                            p_misc[0:TE, 0:3 * S * NT]).then_inc(step, 1)
            dve.tensor_copy(K["dst_col"][:, 0:NT], p_misc[0:TE, 0:NT])
            dve.tensor_copy(K["src_col"][:, 0:NT], p_misc[0:TE, NT:2 * NT])
            for s in range(S):
                dve.wait_ge(row_in[s], 16)
                dve.tensor_scalar(hi_row[s][:, :], key_row[s][0:NH, :], 8, None,
                                  ALU.logical_shift_right).then_inc(step, 1)
            dve.wait_ge(step, 4)
            dve.wait_ge(const_ready, 6)
            dve.sem_inc(look_read, 4)
            dve.sem_inc(counted, 2)
            dve.sem_inc(hist_added, 2 * M)

            def one_hot(t, m):
                b = t.slot(2)
                s, tile = m % S, t.g * G + m // S
                if m == 0:
                    dve.wait_ge(counted, t.g + 1)
                dve.wait_ge(hist_added, t.g * M + m + 1)
                dve.tensor_scalar(hot_hi[:, b, m, :], iota_hi[0:TE, :], key_col[:, 1, s, bass.ds(tile, 1)], None,
                                  ALU.is_equal)
                dve.tensor_scalar(hot_lo[:, b, m, :], iota_lo[0:TE, :], key_col[:, 2, s, bass.ds(tile, 1)], None,
                                  ALU.is_equal)
                dve.tensor_scalar(hot_hi_t[:, b, m, :], hi_row[s][:, bass.ds(tile * TE, TE)],
                                  K["iota_p"][0:NH, 0:1], None, ALU.is_equal).then_inc(hots_ready, 1)
                dve.scalar_tensor_tensor(out=junk_t[:, b, m, :], in0=key_row[s][0:TE, bass.ds(tile * TE, TE)],
                                         scalar=key_col[:, 0, s, bass.ds(tile, 1)], in1=before[:, :],
                                         op0=ALU.is_equal, op1=ALU.mult, accum_out=in_tile[:, b, m:m + 1])

            def count(t):
                b = t.slot(2)
                for m in range(M):
                    if t.ahead(1).exists():
                        one_hot(t.ahead(1), m)
                    dve.wait_ge(looked_up, t.g * M + m + 1)
                    ins = dve.scalar_tensor_tensor(out=junk_r[:, b, m, :], in0=p_look[m % 4][:, 0:LO], scalar=1.0,
                                                   in1=hot_lo[:, b, m, :], op0=ALU.mult, op1=ALU.mult,
                                                   accum_out=in_run[:, b, m:m + 1])
                    ins.then_inc(look_read, 1)
                dve.wait_ge(look_read, t.g * M + M + 4)
                dve.tensor_tensor(K["ord"][:, bass.ds(t.g * G, G), :].rearrange("p t s -> p (t s)"), in_tile[:, b, :],
                                  in_run[:, b, :], ALU.add).then_inc(counted, 1)

            for m in range(M):
                one_hot(Step(0, 0, 2, NT // G), m)
            groups(dve, count)
            dve.wait_ge(hist_added, S * NT + 2 * M)
            for s in range(S):
                dve.tensor_copy(hist[:, s, :], p_hist[s][:, 0:LO]).then_inc(step, 1)
            dve.wait_ge(step, 6)
            for s in range(S):
                dve.tensor_tensor_scan(incl[:, s, :], ones[:, :], hist[:, s, :], 0.0, ALU.mult, ALU.add) \
                   .then_inc(step, 1)
            dve.wait_ge(step, 8)
            dve.tensor_copy(total[:, :], incl[:, :, LO - 1]).then_inc(totals_ready, 1)
            dve.wait_ge(carry_ready, 1)
            dve.tensor_copy(carry[:, :], p_misc[0:NH, 0:S]).then_inc(step, 1)
            dve.wait_ge(step, 9)
            for s in range(S):
                dve.tensor_scalar(tab[:, :, 2 * s + 1], incl[:, s, :], carry[:, s:s + 1], None, ALU.add) \
                   .then_inc(step, 1)
            dve.wait_ge(step, 11)
            dve.tensor_tensor(tab[:, :, 0], tab[:, :, 1], hist[:, 0, :], ALU.subtract)
            dve.tensor_tensor(tab[:, :, 2], tab[:, :, 3], hist[:, 1, :], ALU.subtract).then_inc(tab_ready, 1)

        @block.scalar
        def _(act):
            act.wait_ge(hist_zero, 1)

            def copies(t):
                for m in range(M):
                    act.wait_ge(hist_added, t.g * M + m + 2 * M - 1)
                    act.copy(run[:, m % 4, :], p_hist[m % S][:, 0:LO]).then_inc(run_ready, 1)

            groups(act, copies)

        @block.tensor
        def _(pe):
            pe.wait_ge(keys_split, 1)
            for a in range(3):
                for s in range(S):
                    c = (a * S + s) * NT
                    mm = pe.transpose(p_misc[0:TE, c:c + NT], key_f[:, a, s, :], K["ident"][0:NT, 0:NT])
            mm.then_inc(keys_turned, 1)
            pe.wait_ge(const_ready, 6)
            for s in range(S):
                mm = pe.matmul(p_hist[s][:, 0:LO], zero_b[:, 0:NH], zero_b[:, :], start=True, stop=False,
                               skip_group_check=True)
            mm.then_inc(hist_zero, 1)

            def look_and_add(t):
                b = t.slot(2)
                for m in range(M):
                    pe.wait_ge(hots_ready, t.g * M + m + 1)
                    pe.wait_ge(run_ready, t.g * M + m + 1)
                    pe.wait_ge(look_read, t.g * M + m + 1)
                    pe.matmul(p_look[m % 4][:, 0:LO], hot_hi_t[:, b, m, :], run[:, m % 4, :], start=True, stop=True) \
                      .then_inc(looked_up, 1)
                    pe.matmul(p_hist[m % S][:, 0:LO], hot_hi[:, b, m, :], hot_lo[:, b, m, :], start=False, stop=False,
                              skip_group_check=True).then_inc(hist_added, 1)

            groups(pe, look_and_add)
            pe.wait_ge(totals_ready, 1)
            pe.matmul(p_misc[0:NH, 0:S], above[:, :], total[:, :], start=True, stop=True).then_inc(carry_ready, 1)


def rows_of(dram, g, n, p):
    return dram[bass.ds(g * (n * p), n * p), :].rearrange("(j p) d -> p j d", p=p)


def open_slot(pool, K, sem, count):
    K["token_n"] += 1
    n = K["token_n"]
    pool.dma_start(K["token"][0:1, n, :], K["ident"][0:1, 0:4]).then_inc(sem, count)


class Norm:

    def __init__(self, nc, ctx, name, sem, rows, n, eps):
        def sb(what, shape):
            return ctx.enter_context(nc.sbuf_tensor(f"{name}_{what}", shape, F32))

        self.rows, self.n, self.eps = rows, n, eps
        self.stats = sb("stats", [rows, 2, n, 6])
        self.mean_var = sb("mean_var", [rows, 2, n, 2])
        self.std = sb("std", [rows, 2, n])
        self.rstd = sb("rstd", [rows, 2, n])
        self.shift = sb("shift", [rows, 2, n])
        self.stats_done = sem("stats_done")
        self.passed = sem("stats_passed")
        self.var_ready = sem("var_ready")
        self.std_ready = sem("std_ready")
        self.rstd_done = sem("rstd_done")
        self.shift_ready = sem("shift_ready")

    def statistics(self, dve, g, b, x):
        for j in range(self.n):
            ins = dve.bn_stats(self.stats[:, b, j, :], x[:, j, :])
        ins.then_inc(self.stats_done, 1)
        dve.wait_ge(self.stats_done, g + 1)
        dve.sem_inc(self.passed, 1)
        for j in range(self.n):
            ins = dve.bn_aggr(self.mean_var[:, b, j, :], self.stats[:, b, j, :])
        ins.then_inc(self.var_ready, 1)

    def root(self, act, g, b):
        act.wait_ge(self.var_ready, g + 1)
        act.activation(self.std[:, b, :], self.mean_var[:, b, :, 1], ACT.Sqrt, bias=self.eps[0:self.rows, 0:1],
                       scale=1.0).then_inc(self.std_ready, 1)

    def scales(self, dve, g, b):
        dve.wait_ge(self.std_ready, g + 1)
        dve.reciprocal(self.rstd[:, b, :], self.std[:, b, :]).then_inc(self.rstd_done, 1)
        dve.wait_ge(self.rstd_done, g + 1)
        dve.scalar_tensor_tensor(out=self.shift[:, b, :], in0=self.mean_var[:, b, :, 0], scalar=-1.0,
                                 in1=self.rstd[:, b, :], op0=ALU.mult, op1=ALU.mult).then_inc(self.shift_ready, 1)

    def rows_out(self, act, g, b, h, x):
        act.wait_ge(self.shift_ready, g + 1)
        for j in range(self.n):
            ins = act.activation(h[:, j, :], x[:, j, :], ACT.Relu, bias=self.shift[:, b, j:j + 1],
                                 scale=self.rstd[:, b, j:j + 1])
        return ins


class Records:

    def __init__(self, nc, ctx, sem, K, A, table, rec_d, rec_c):
        def sb(name, shape, dt=F32):
            return ctx.enter_context(nc.sbuf_tensor(f"rc_{name}", shape, dt))

        self.K, self.A, self.table, self.rec_d, self.rec_c = K, A, table, rec_d, rec_c
        self.N = A["x"].shape[0]
        self.NT = A["src"].shape[0] // TE
        self.NREL = A["L1_gnn_alpha"].shape[0]
        self.RANK_D = RD + 2 * RC
        self.W = self.RANK_D + 4
        self.NP = self.NT // GP
        NT = self.NT
        self.idx = sb("idx", [TE, 2, 2, GP], I32)
        self.got = sb("got", [TE, 2, 2, GP, 4])
        self.tab = sb("tab", [TE, 2, NT, 4])
        self.node = sb("node", [TE, 2, NT])
        self.rec = sb("rec", [TE, NT, self.W])
        self.part = sb("part", [TE, 12, NT])
        self.a2_40 = sb("a2_40", [NT, TE, 2])
        self.a3_40 = sb("a3_40", [NT, TE, 3])
        self.type_i = sb("type_i", [NT, TE], I32)
        self.type_40 = sb("type_40", [NT, TE])
        self.type_c = sb("type_c", [TE, NT])
        self.alpha = sb("alpha", [TE, self.NREL])
        self.pick = sb("pick", [TE, 2, NT])
        self.d_out = sb("d_out", [TE, 2, GP, RD])
        self.d_idx = sb("d_idx", [TE, 2, GP], I32)
        self.c_out = sb("c_out", [TE, 2, 2, RC])
        self.c_idx = sb("c_idx", [TE, 2, 2], I32)
        self.small_in = sem("small_in")
        self.types_ready = sem("types_ready")
        self.cols_ready = sem("cols_ready")
        self.rec_cleared = sem("rec_cleared")
        self.idx_ready = sem("idx_ready")
        self.got_in = [sem(f"got_in{b}") for b in range(2)]
        self.got_read = sem("got_read")
        self.step = sem("step")
        self.steps = 0
        self.placed = sem("placed")
        self.d_ready = sem("d_ready")
        self.d_put = [sem(f"d_put{b}") for b in range(2)]
        self.c_ready = sem("c_ready")
        self.c_put = [sem(f"c_put{b}") for b in range(2)]
        self.passed = sem("passed")

    def rc(self, c):
        return self.rec[:, :, c]

    def then(self, dve, ins):
        ins.then_inc(self.step, 1)
        self.steps += 1
        dve.wait_ge(self.step, self.steps)

    def load(self, sp):
        A = self.A
        sp.dma_start(self.a2_40[:, :, :].rearrange("t e c -> t (e c)"),
                     A["edge_attr_2"].rearrange("(t e) c -> t (e c)", e=TE)).then_inc(self.small_in, 16)
        sp.dma_start(self.a3_40[:, :, :].rearrange("t e c -> t (e c)"),
                     A["edge_attr_3"].rearrange("(t e) c -> t (e c)", e=TE)).then_inc(self.small_in, 16)
        sp.dma_start(self.type_i[:, :], A["edge_type_11"].rearrange("(t e) -> t e", e=TE)).then_inc(self.small_in, 16)
        sp.dma_start(self.alpha[:, :], A["L1_gnn_alpha"].rearrange("r a -> a r").to_broadcast([TE, self.NREL])) \
            .then_inc(self.small_in, 16)

    def turn_columns(self, pe, bank):
        NT, ident = self.NT, self.K["ident"]
        pe.wait_ge(self.types_ready, 1)
        for c in range(2):
            pe.transpose(bank[:, c * NT:(c + 1) * NT], self.a2_40[:, :, c], ident[0:NT, 0:NT])
        for c in range(3):
            pe.transpose(bank[:, (2 + c) * NT:(3 + c) * NT], self.a3_40[:, :, c], ident[0:NT, 0:NT])
        pe.transpose(bank[:, 5 * NT:6 * NT], self.type_40[:, :], ident[0:NT, 0:NT]).then_inc(self.cols_ready, 1)

    def clear(self, pool):
        for b in range(2):
            open_slot(pool, self.K, self.d_put[b], 16 * GP)
        pool.memset(self.rec[:, :, :], 0.0).then_inc(self.rec_cleared, 1)
        pool.wait_ge(self.rec_cleared, 1)
        pool.memset(self.rec[:, :, D_ONE], 1.0)
        pool.iota(self.rec[:, :, D_EDGE], [[TE, self.NT]], base=0, channel_multiplier=1,
                  allow_small_or_imprecise_dtypes=True).then_inc(self.rec_cleared, 1)
        pool.sem_inc(self.got_read, 2)

    def columns(self, dve, bank):
        NT = self.NT
        dve.wait_ge(self.small_in, 64)
        dve.tensor_copy(self.type_40[:, :], self.type_i[:, :]).then_inc(self.types_ready, 1)
        dve.wait_ge(self.cols_ready, 1)
        dve.wait_ge(self.rec_cleared, 2)
        for c in range(2):
            dve.tensor_copy(self.rc(D_A2 + c), bank[:, c * NT:(c + 1) * NT])
        for c in range(3):
            dve.tensor_copy(self.rc(D_A3 + c), bank[:, (2 + c) * NT:(3 + c) * NT])
        self.then(dve, dve.tensor_copy(self.type_c[:, :], bank[:, 5 * NT:6 * NT]))

    def weights(self, dve):
        pick = self.pick
        self.then(dve, dve.tensor_scalar(pick[:, 0, :], self.type_c[:, :], 0.0, self.alpha[:, 0:1], ALU.is_equal,
                                         ALU.mult))
        for r in range(1, self.NREL):
            self.then(dve, dve.tensor_scalar(pick[:, 1, :], self.type_c[:, :], float(r), self.alpha[:, r:r + 1],
                                             ALU.is_equal, ALU.mult))
            self.then(dve, dve.tensor_tensor(pick[:, 0, :], pick[:, 0, :], pick[:, 1, :], ALU.add))

    def index(self, pool, q):
        b = q.slot(2)
        pool.tensor_copy(self.idx[:, b, 0, :], self.K["dst_col"][:, bass.ds(q.g * GP, GP)])
        pool.tensor_copy(self.idx[:, b, 1, :], self.K["src_col"][:, bass.ds(q.g * GP, GP)]) \
            .then_inc(self.idx_ready, 1)

    def look_up(self, pool, q):
        b = q.slot(2)
        pool.wait_ge(self.idx_ready, q.g + 1)
        pool.wait_ge(self.got_read, q.g + 1)
        pool.sem_inc(self.passed, 1)
        for s in range(2):
            for j in range(GP):
                pool.indirect_dma_start(self.got[:, b, s, j, :], None, self.table[:, :],
                                        IOA(self.idx[:, b, s, j:j + 1], 0), bounds_check=self.N - 1,
                                        oob_is_err=False).then_inc(self.got_in[b], 16)

    def keep(self, pool, q):
        b = q.slot(2)
        pool.wait_ge(self.got_in[b], q.round(2) * (32 * GP))
        for s in range(2):
            ins = pool.tensor_copy(self.tab[:, s, bass.ds(q.g * GP, GP), :].rearrange("p t c -> p (t c)"),
                                   self.got[:, b, s, :, :].rearrange("p t c -> p (t c)"))
        ins.then_inc(self.got_read, 1)

    def places(self, dve):
        tab, part, rc, node, pick, K, RANK_D = self.tab, self.part, self.rc, self.node, self.pick, self.K, self.RANK_D
        RANK_CD, RANK_CS = RANK_D + 1, RANK_D + 2

        def then(ins):
            self.then(dve, ins)

        dve.wait_ge(self.got_read, self.NP + 2)
        dve.tensor_copy(node[:, 0, :], K["dst_col"][:, 0:self.NT])
        dve.tensor_copy(node[:, 1, :], K["src_col"][:, 0:self.NT])
        dst_below, dst_upto, src_below, src_upto = (tab[:, 0, :, c] for c in range(4))
        s_dst_below, s_dst_upto, s_src_below, s_src_upto = (tab[:, 1, :, c] for c in range(4))
        CD, CS = RD, RD + RC
        then(dve.tensor_tensor(rc(RANK_D), dst_below, K["ord"][:, :, 0], ALU.add))
        dve.tensor_tensor(rc(RANK_CD), rc(RANK_D), src_below, ALU.add)
        then(dve.tensor_tensor(part[:, 0, :], s_src_below, K["ord"][:, :, 1], ALU.add))
        dve.tensor_tensor(rc(RANK_CS), part[:, 0, :], s_dst_upto, ALU.add)
        dve.tensor_tensor(part[:, 1, :], dst_upto, src_upto, ALU.add)
        dve.tensor_tensor(part[:, 2, :], s_dst_upto, s_src_upto, ALU.add)
        then(dve.tensor_tensor(part[:, 3, :], s_dst_below, s_src_below, ALU.add))
        dve.tensor_scalar(rc(D_SAME), K["ord"][:, :, 0], 0.0, None, ALU.is_gt)
        dve.tensor_scalar(rc(CD + C_SAME), K["ord"][:, :, 0], 0.0, None, ALU.is_gt)
        dve.tensor_tensor(rc(CS + C_SAME), rc(RANK_CS), part[:, 3, :], ALU.is_gt)
        dve.tensor_tensor(part[:, 4, :], dst_upto, rc(RANK_D), ALU.subtract)
        dve.tensor_tensor(part[:, 5, :], part[:, 1, :], rc(RANK_CD), ALU.subtract)
        then(dve.tensor_tensor(part[:, 6, :], part[:, 2, :], rc(RANK_CS), ALU.subtract))
        for c in range(3):
            ins = dve.tensor_scalar(part[:, 7 + c, :], part[:, 4 + c, :], 1.5, float(SKIP), ALU.is_gt, ALU.mult)
        then(ins)
        dve.tensor_tensor(rc(D_PUT), part[:, 7, :], node[:, 0, :], ALU.add)
        dve.tensor_tensor(rc(CD + C_PUT), part[:, 8, :], node[:, 0, :], ALU.add)
        dve.tensor_tensor(rc(CS + C_PUT), part[:, 9, :], node[:, 1, :], ALU.add)
        dve.tensor_copy(rc(D_SRC), node[:, 1, :])
        dve.tensor_copy(rc(D_DST), node[:, 0, :])
        dve.tensor_copy(rc(CD + C_PEER), node[:, 1, :])
        dve.tensor_copy(rc(CS + C_PEER), node[:, 0, :])
        dve.tensor_copy(rc(CD + C_W), pick[:, 0, :])
        dve.tensor_copy(rc(CS + C_W), pick[:, 0, :]).then_inc(self.placed, 1)

    def put_by_dst(self, pool, q):
        b = q.slot(2)
        pool.wait_ge(self.d_put[b], q.round(2) * (16 * GP))
        pool.tensor_copy(self.d_out[:, b, :, :], self.rec[:, bass.ds(q.g * GP, GP), 0:RD])
        pool.tensor_copy(self.d_idx[:, b, :], self.rec[:, bass.ds(q.g * GP, GP), self.RANK_D]) \
            .then_inc(self.d_ready, 1)
        pool.wait_ge(self.d_ready, q.g + 1)
        pool.sem_inc(self.passed, 1)
        for j in range(GP):
            pool.indirect_dma_start(self.rec_d[:, :], IOA(self.d_idx[:, b, j:j + 1], 0), self.d_out[:, b, j, :], None,
                                    bounds_check=self.rec_d.shape[0] - 1, oob_is_err=False) \
                .then_inc(self.d_put[b], 16)

    def end_by_dst(self, pool):
        for b in range(2):
            pool.wait_ge(self.d_put[b], 16 * GP * (1 + (self.NP + 1 - b) // 2))

    def start_by_node(self, pool):
        for b in range(2):
            open_slot(pool, self.K, self.c_put[b], 32)

    def put_by_node(self, pool, t):
        b = t.slot(2)
        pool.wait_ge(self.c_put[b], t.round(2) * 32)
        pool.tensor_copy(self.c_out[:, b, :, :].rearrange("p s c -> p (s c)"),
                         self.rec[:, bass.ds(t.g, 1), RD:RD + 2 * RC].rearrange("p t c -> p (t c)"))
        pool.tensor_copy(self.c_idx[:, b, :],
                         self.rec[:, bass.ds(t.g, 1), self.RANK_D + 1:self.RANK_D + 3].rearrange("p t c -> p (t c)")) \
            .then_inc(self.c_ready, 1)
        pool.wait_ge(self.c_ready, t.g + 1)
        pool.sem_inc(self.passed, 1)
        for s in range(2):
            pool.indirect_dma_start(self.rec_c[:, :], IOA(self.c_idx[:, b, s:s + 1], 0), self.c_out[:, b, s, :], None,
                                    bounds_check=self.rec_c.shape[0] - 1, oob_is_err=False) \
                .then_inc(self.c_put[b], 16)

    def end_by_node(self, pool):
        for b in range(2):
            pool.wait_ge(self.c_put[b], 32 * (1 + self.NT // 2))


def edge_messages(nc, K, A, R, msg):
    N = A["x"].shape[0]
    E = A["src"].shape[0]
    NG = E // GE
    with ExitStack() as ctx:
        def sb(name, shape, dt=F32):
            return ctx.enter_context(nc.sbuf_tensor(name, shape, dt))

        def pb(name, shape, dt=F32):
            return ctx.enter_context(nc.psum_tensor(name, shape, dt))

        sem = signals(nc, K, "em")
        w1 = sb("em_w1", [P, DC, HID])
        w2 = sb("em_w2", [P, HC, D])
        b1 = sb("em_b1", [P, HC])
        b2 = sb("em_b2", [TE, D])
        ef = sb("em_ef", [TE, 2, G, D])
        x = sb("em_x", [TE, 2, G, D])
        h = sb("em_h", [TE, 2, G, D])
        m = sb("em_m", [TE, 2, G, D])
        idx = sb("em_idx", [TE, 2, G], I32)
        ef_t = sb("em_ef_t", [P, 2, DC, GE])
        hid = sb("em_hid", [P, 2, HC, GE])
        p_t = [pb(f"em_p_t{c}", [P, 512]) for c in range(DC)]
        p_h = [pb(f"em_p_h{c}", [P, 512]) for c in range(HC)]
        p_m = [pb(f"em_p_m{c}", [TE, 2, D]) for c in range(2)]
        norm = Norm(nc, ctx, "em", sem, TE, G, K["eps"])

        w_in = sem("w_in")
        ef_in = [sem(f"ef_in{b}") for b in range(2)]
        x_in = [sem(f"x_in{b}") for b in range(2)]
        m_out = [sem(f"m_out{b}") for b in range(2)]
        idx_ready = sem("idx_ready")
        h_ready = sem("h_ready")
        ef_turned = sem("ef_turned")
        ef_t_ready = sem("ef_t_ready")
        hid_mm = sem("hid_mm")
        hid_ready = sem("hid_ready")
        m_mm = sem("m_mm")
        m_added = sem("m_added")
        m_ready = sem("m_ready")
        h_shifted = sem("h_shifted")
        passed = sem("passed")
        block = ctx.enter_context(nc.Block())
        PLACES = NG - 4

        def groups(eng, body):
            over_groups(eng, NG, 2, 4, body)

        @block.sync
        def _(sp):
            R.load(sp)
            sp.sem_inc(ef_turned, 2)

            def load(t):
                b = t.slot(2)
                sp.wait_ge(ef_turned, t.g + 1)
                sp.dma_start(ef[:, b, :, :], rows_of(A["edge_attr_256"], t.g, G, TE)).then_inc(ef_in[b], 16)

            over_groups(sp, NG, 2, 0, load)

        @block.gpsimd
        def _(pool):
            R.clear(pool)
            pool.sem_inc(h_ready, 2)

            def fetch(t):
                b = t.slot(2)
                pool.wait_ge(idx_ready, t.g + 1)
                pool.wait_ge(h_ready, t.g + 1)
                pool.sem_inc(passed, 1)
                for j in range(G):
                    pool.indirect_dma_start(x[:, b, j, :], None, A["x"], IOA(idx[:, b, j:j + 1], 0),
                                            bounds_check=N - 1, oob_is_err=False).then_inc(x_in[b], 16)

            def look_and_fetch(q):
                fetch(q.ahead(2))
                R.look_up(pool, q.ahead(1))
                R.keep(pool, q)
                R.index(pool, q.ahead(2))

            for b in range(2):
                fetch(Step(0, b, 2, NG))
                R.index(pool, Step(0, b, 2, R.NP))
            R.look_up(pool, Step(0, 0, 2, R.NP))
            over_groups(pool, R.NP - 1, 2, 0, look_and_fetch)
            R.keep(pool, Step((R.NP - 1) // 2, (R.NP - 1) % 2, 2, R.NP))
            for g in range(R.NP + 1, NG):
                fetch(Step(g // 2, g % 2, 2, NG))
            pool.wait_ge(R.placed, 1)
            over_groups(pool, R.NP, 2, 1, lambda q: R.put_by_dst(pool, q))
            R.end_by_dst(pool)

        @block.vector
        def _(dve):
            for b in range(2):
                dve.tensor_copy(idx[:, b, :], K["src_col"][:, b * G:(b + 1) * G]).then_inc(idx_ready, 1)
                dve.sem_inc(m_out[b], 16)
            R.columns(dve, p_m[0][:, :, :].rearrange("p a d -> p (a d)"))
            dve.sem_inc(m_added, 2)
            R.weights(dve)
            dve.wait_ge(w_in, 64)

            def first_half(t):
                dve.wait_ge(ef_turned, t.g + 3)
                dve.tensor_copy(ef_t[:, t.slot(2), 0, :], p_t[0][:, 0:GE]).then_inc(ef_t_ready, 1)

            def body(t):
                if isinstance(t.g, int) and t.g == PLACES:
                    R.places(dve)
                b = t.slot(2)
                dve.wait_ge(x_in[b], t.round(2) * (16 * G))
                norm.statistics(dve, t.g, b, x[:, b, :, :])
                dve.tensor_copy(idx[:, b, :], K["src_col"][:, bass.ds(t.g * G + 2 * G, G)]).then_inc(idx_ready, 1)
                norm.scales(dve, t.g, b)
                if t.ahead(1).exists():
                    first_half(t.ahead(1))
                dve.wait_ge(h_ready, t.g + 3)
                dve.wait_ge(m_out[b], t.round(2) * 16)
                dve.tensor_tensor(m[:, b, :, :], h[:, b, :, :], b2[:, :].unsqueeze(1).to_broadcast([TE, G, D]),
                                  ALU.add).then_inc(h_shifted, 1)
                dve.wait_ge(h_shifted, t.g + 1)
                for c in range(2):
                    dve.wait_ge(m_mm, t.g * 2 + c + 1)
                    dve.tensor_tensor(m[:, b, 2 * c:2 * c + 2, :], m[:, b, 2 * c:2 * c + 2, :], p_m[c][:, :, :],
                                      ALU.add).then_inc(m_added, 1)

            first_half(Step(0, 0, 2, NG))
            groups(dve, body)

        @block.scalar
        def _(act):
            act.dma_start(w1[:, :, :], A["L0_gnn_We1"].rearrange("(k p) n -> p k n", p=P)).then_inc(w_in, 16)
            act.dma_start(w2[:, :, :], A["L0_gnn_We2"].rearrange("(k p) n -> p k n", p=P)).then_inc(w_in, 16)
            with nc.allow_non_contiguous_dma(reason="512 biases"):
                act.dma_start(b1[:, :], A["L0_gnn_be1"].rearrange("(k p) -> p k", p=P)).then_inc(w_in, 16)
            act.dma_start(b2[:, :], broadcast_row(A["L0_gnn_be2"], TE)).then_inc(w_in, 16)
            act.wait_ge(w_in, 64)

            def second_half(t):
                act.wait_ge(ef_turned, t.g + 3)
                act.copy(ef_t[:, t.slot(2), 1, :], p_t[1][:, 0:GE]).then_inc(ef_t_ready, 1)

            def hidden(t, k):
                act.wait_ge(hid_mm, t.g * HC + k + 1)
                act.activation(hid[:, t.slot(2), k, :], p_h[k][:, 0:GE], ACT.Relu, bias=b1[:, k:k + 1]) \
                   .then_inc(hid_ready, 1)

            def body(t):
                b = t.slot(2)
                norm.root(act, t.g, b)
                hidden(t, 0)
                norm.rows_out(act, t.g, b, h[:, b, :, :], x[:, b, :, :]).then_inc(h_ready, 1)
                for k in range(1, HC):
                    hidden(t, k)
                if t.ahead(1).exists():
                    second_half(t.ahead(1))
                act.wait_ge(m_added, t.g * 2 + 4)
                act.activation(m[:, b, :, :], m[:, b, :, :], ACT.Relu).then_inc(m_ready, 1)
                act.wait_ge(m_ready, t.g + 1)
                act.dma_start(rows_of(msg, t.g, G, TE), m[:, b, :, :]).then_inc(m_out[b], 16)

            second_half(Step(0, 0, 2, NG))
            groups(act, body)
            for b in range(2):
                act.wait_ge(m_out[b], 16 * (NG // 2 + 1))

        @block.tensor
        def _(pe):
            R.turn_columns(pe, p_m[0][:, :, :].rearrange("p a d -> p (a d)"))
            pe.wait_ge(w_in, 64)
            pe.sem_inc(ef_t_ready, 2)
            pe.sem_inc(hid_ready, HC)

            def turn(t):
                b = t.slot(2)
                pe.wait_ge(ef_in[b], t.round(2) * 16)
                pe.wait_ge(ef_t_ready, t.g * 2 + 2)
                for c in range(DC):
                    for j in range(G):
                        mm = pe.transpose(p_t[c][:, j * TE:(j + 1) * TE], ef[:, b, j, c * P:(c + 1) * P],
                                          K["ident"][0:TE, 0:TE])
                mm.then_inc(ef_turned, 1)

            def body(t):
                b = t.slot(2)
                pe.wait_ge(ef_t_ready, t.g * 2 + 4)
                for k in range(HC):
                    pe.wait_ge(hid_ready, t.g * HC + k + 1)
                    for c in range(DC):
                        mm = pe.matmul(p_h[k][:, 0:GE], w1[:, c, k * P:(k + 1) * P], ef_t[:, b, c, :],
                                       start=(c == 0), stop=(c == DC - 1))
                    mm.then_inc(hid_mm, 1)
                if t.ahead(1).exists():
                    turn(t.ahead(1))
                pe.wait_ge(hid_ready, t.g * HC + 2 * HC)
                for c in range(2):
                    pe.wait_ge(m_added, t.g * 2 + c + 1)
                    for jj in range(2):
                        j = 2 * c + jj
                        for k in range(HC):
                            mm = pe.matmul(p_m[c][:, jj, :], hid[:, b, k, j * TE:(j + 1) * TE], w2[:, k, :],
                                           start=(k == 0), stop=(k == HC - 1))
                    mm.then_inc(m_mm, 1)

            turn(Step(0, 0, 2, NG))
            groups(pe, body)


def aggregate_messages(nc, K, msg, rec_d, agg0):
    N = agg0.shape[0]
    E = msg.shape[0]
    NG = E // GE
    same = K["same"]
    with ExitStack() as ctx:
        def sb(name, shape, dt=F32):
            return ctx.enter_context(nc.sbuf_tensor(name, shape, dt))

        def pb(name, shape, dt=F32):
            return ctx.enter_context(nc.psum_tensor(name, shape, dt))

        sem = signals(nc, K, "ag")
        rec = sb("ag_rec", [TE, 2, G, RD])
        keep = sb("ag_keep", [TE, 2, G])
        idx = sb("ag_idx", [TE, 2, G], I32)
        put_idx = sb("ag_put_idx", [TE, 2, G], I32)
        m = sb("ag_m", [TE, 2, G, D])
        run = sb("ag_run", [P, 2, DC, GE])
        rows = sb("ag_rows", [TE, 2, G, D])
        p_s = pb("ag_p_s", [P, 512])
        p_t = [[pb(f"ag_p_t{b}{c}", [P, 512]) for c in range(DC)] for b in range(2)]
        p_r = [pb(f"ag_p_r{c}", [TE, 2, D]) for c in range(2)]

        rec_in = [sem(f"rec_in{b}") for b in range(2)]
        m_in = [sem(f"m_in{b}") for b in range(2)]
        put = [sem(f"put{b}") for b in range(2)]
        idx_ready = sem("idx_ready")
        put_idx_ready = sem("put_idx_ready")
        same_mm = sem("same_mm")
        same_ready = sem("same_ready")
        m_turned = sem("m_turned")
        run_ready = sem("run_ready")
        run_turned = sem("run_turned")
        rows_ready = sem("rows_ready")
        passed = sem("passed")
        block = ctx.enter_context(nc.Block())

        def groups(eng, body):
            over_groups(eng, NG, 2, 4, body)

        @block.sync
        def _(sp):
            sp.sem_inc(same_mm, 2)

            def load(t):
                b = t.slot(2)
                sp.wait_ge(same_mm, t.g + 1)
                sp.dma_start(rec[:, b, :, :], rows_of(rec_d, t.g, G, TE)).then_inc(rec_in[b], 16)

            groups(sp, load)

        @block.gpsimd
        def _(pool):
            for b in range(2):
                open_slot(pool, K, put[b], 16 * G)

            def fetch(t):
                b = t.slot(2)
                pool.wait_ge(idx_ready, t.g + 1)
                pool.wait_ge(m_turned, t.g + 1)
                pool.sem_inc(passed, 1)
                for j in range(G):
                    pool.indirect_dma_start(m[:, b, j, :], None, msg[:, :], IOA(idx[:, b, j:j + 1], 0),
                                            bounds_check=E - 1, oob_is_err=False).then_inc(m_in[b], 16)

            def body(t):
                if t.ahead(2).exists():
                    fetch(t.ahead(2))
                b = t.slot(2)
                pool.wait_ge(rows_ready, t.g * 2 + 4)
                pool.sem_inc(passed, 1)
                for j in range(G):
                    pool.indirect_dma_start(agg0[:, :], IOA(put_idx[:, b, j:j + 1], 0), rows[:, b, j, :], None,
                                            bounds_check=N - 1, oob_is_err=False).then_inc(put[b], 16)

            pool.sem_inc(m_turned, 2)
            fetch(Step(0, 0, 2, NG))
            fetch(Step(0, 1, 2, NG))
            groups(pool, body)
            for b in range(2):
                pool.wait_ge(put[b], 16 * G * (NG // 2 + 1))

        @block.vector
        def _(dve):
            dve.memset(run[:, 1, :, GE - 1], 0.0).then_inc(run_ready, 4)

            def take(t):
                b = t.slot(2)
                dve.wait_ge(rec_in[b], t.round(2) * 16)
                dve.wait_ge(put_idx_ready, t.g + 1)
                dve.tensor_copy(keep[:, b, :], rec[:, b, :, D_PUT])
                dve.tensor_copy(idx[:, b, :], rec[:, b, :, D_EDGE]).then_inc(idx_ready, 1)

            def body(t):
                b = t.slot(2)
                dve.wait_ge(put[b], t.round(2) * (16 * G))
                dve.wait_ge(idx_ready, t.g + 1)
                dve.tensor_copy(put_idx[:, b, :], keep[:, b, :]).then_inc(put_idx_ready, 1)
                dve.wait_ge(m_turned, t.g + 3)
                if t.ahead(2).exists():
                    take(t.ahead(2))
                dve.wait_ge(same_ready, t.g + 2)
                dve.wait_ge(run_ready, t.g * 2 + 4)
                for c in range(DC):
                    dve.tensor_tensor_scan(run[:, b, c, :], same[:, bass.ds(t.g * GE, GE)], p_t[b][c][:, 0:GE],
                                           run[:, 1 - b, c, GE - 1:GE], ALU.mult, ALU.add) \
                       .then_inc(run_ready, 1)

            dve.sem_inc(put_idx_ready, 2)
            take(Step(0, 0, 2, NG))
            take(Step(0, 1, 2, NG))
            groups(dve, body)

        @block.scalar
        def _(act):
            def mask(t):
                act.wait_ge(same_mm, t.g + 3)
                act.copy(same[:, bass.ds(t.g * GE, GE)], p_s[:, 0:GE]).then_inc(same_ready, 1)

            def body(t):
                b = t.slot(2)
                if t.ahead(1).exists():
                    mask(t.ahead(1))
                act.wait_ge(put[b], t.round(2) * (16 * G))
                for c in range(2):
                    act.wait_ge(run_turned, t.g * 2 + c + 1)
                    act.copy(rows[:, b, 2 * c:2 * c + 2, :], p_r[c][:, :, :]).then_inc(rows_ready, 1)

            mask(Step(0, 0, 2, NG))
            groups(act, body)

        @block.tensor
        def _(pe):
            def turn(t):
                b = t.slot(2)
                pe.wait_ge(rec_in[b], t.round(2) * 16)
                pe.wait_ge(idx_ready, t.g + 1)
                pe.wait_ge(same_ready, t.g + 1)
                for j in range(G):
                    mm = pe.matmul(p_s[:, j * TE:(j + 1) * TE],
                                   rec[:, b, j, D_SAME:D_SAME + 1].to_broadcast([TE, P]),
                                   K["ident"][0:TE, 0:TE], start=True, stop=True)
                mm.then_inc(same_mm, 1)
                pe.wait_ge(m_in[b], t.round(2) * (16 * G))
                pe.wait_ge(run_ready, t.g * 2 + 2)
                for c in range(DC):
                    for j in range(G):
                        mm = pe.transpose(p_t[b][c][:, j * TE:(j + 1) * TE], m[:, b, j, c * P:(c + 1) * P],
                                          K["ident"][0:TE, 0:TE])
                mm.then_inc(m_turned, 1)

            def body(t):
                b = t.slot(2)
                if t.ahead(1).exists():
                    turn(t.ahead(1))
                pe.wait_ge(run_ready, t.g * 2 + 6)
                for c in range(2):
                    pe.wait_ge(rows_ready, t.g * 2 + c + 1)
                    for jj in range(2):
                        j = 2 * c + jj
                        for k in range(DC):
                            mm = pe.transpose(p_r[c][:, jj, k * P:(k + 1) * P],
                                              run[:, b, k, j * TE:(j + 1) * TE], K["ident"][:, :])
                    mm.then_inc(run_turned, 1)

            pe.sem_inc(same_ready, 1)
            pe.sem_inc(rows_ready, 2)
            turn(Step(0, 0, 2, NG))
            groups(pe, body)


def broadcast_row(vector, rows):
    return vector.rearrange("(a d) -> a d", a=1).to_broadcast([rows, vector.shape[0]])


def node_network(nc, K, A, R, agg0, x1_dram, out):
    N = A["x"].shape[0]
    ROWS = G * P
    NG = -(-N // ROWS)
    REST = N - (NG - 1) * ROWS
    XB = 4
    UN = 4
    assert NG % UN == 0 and XB == UN and NG == R.NT and 0 < REST <= P
    with ExitStack() as ctx:
        def sb(name, shape, dt=F32):
            return ctx.enter_context(nc.sbuf_tensor(name, shape, dt))

        def pb(name, shape, dt=F32):
            return ctx.enter_context(nc.psum_tensor(name, shape, dt))

        sem = signals(nc, K, "nn")
        w1 = sb("nn_w1", [P, DC, HID])
        w2 = sb("nn_w2", [P, HC, D])
        b1 = sb("nn_b1", [P, HC])
        b2 = sb("nn_b2", [P, D])
        late = sb("nn_late", [P, 2, D])
        late_sum = sb("nn_late_sum", [P, D])
        gain = sb("nn_gain", [P, 1])
        x = sb("nn_x", [P, XB, G, D])
        agg = sb("nn_agg", [P, XB, G, D])
        h = sb("nn_h", [P, 2, G, D])
        x1 = sb("nn_x1", [P, 2, G, D])
        x3 = sb("nn_x3", [P, 2, G, D])
        h_t = sb("nn_h_t", [P, 2, DC, ROWS])
        hid = sb("nn_hid", [P, 2, HC, ROWS])
        p_t = [pb(f"nn_p_t{c}", [P, ROWS]) for c in range(DC)]
        p_h = [pb(f"nn_p_h{c}", [P, ROWS]) for c in range(HC)]
        p_o = [pb(f"nn_p_o{c}", [P, 2, D]) for c in range(2)]
        norm = Norm(nc, ctx, "nn", sem, P, G, K["eps"])

        w_in = sem("w_in")
        x_in = [sem(f"x_in{r}") for r in range(XB)]
        x1_out = [sem(f"x1_out{b}") for b in range(2)]
        x3_out = [sem(f"x3_out{b}") for b in range(2)]
        late_ready = sem("late_ready")
        h_ready = sem("h_ready")
        x_shifted = sem("x_shifted")
        mixed = sem("mixed")
        turned = sem("turned")
        h_t_ready = sem("h_t_ready")
        hid_mm = sem("hid_mm")
        hid_ready = sem("hid_ready")
        o_mm = sem("o_mm")
        x1_ready = sem("x1_ready")
        x3_ready = sem("x3_ready")
        block = ctx.enter_context(nc.Block())

        def is_last(t):
            return isinstance(t.g, int) and t.g == NG - 1

        def in_dram(dram, t):
            if is_last(t):
                return dram[N - REST:N, :]
            return dram[bass.ds(t.g * ROWS, ROWS), :].rearrange("(p j) d -> p j d", j=G)

        def on_chip(buf, slot, t):
            return buf[0:REST, slot, 0, :] if is_last(t) else buf[:, slot, :, :]

        def groups(eng, body):
            over_groups(eng, NG, UN, UN, body)

        start = [Step(0, k, UN, NG) for k in range(XB)]

        @block.sync
        def _(sp):
            def load(t):
                sp.dma_start(on_chip(x, t.r, t), in_dram(A["x"], t)).then_inc(x_in[t.r], 16)
                sp.dma_start(on_chip(agg, t.r, t), in_dram(agg0, t)).then_inc(x_in[t.r], 16)

            load(start[0])
            sp.dma_start(w1[:, :, :], A["L0_gnn_Wn1"].rearrange("(k p) n -> p k n", p=P)).then_inc(w_in, 16)
            sp.dma_start(w2[:, :, :], A["L0_gnn_Wn2"].rearrange("(k p) n -> p k n", p=P)).then_inc(w_in, 16)
            with nc.allow_non_contiguous_dma(reason="512 biases"):
                sp.dma_start(b1[:, :], A["L0_gnn_bn1"].rearrange("(k p) -> p k", p=P)).then_inc(w_in, 16)
            sp.dma_start(b2[:, :], broadcast_row(A["L0_gnn_bn2"], P)).then_inc(w_in, 16)
            sp.dma_start(late[:, 0, :], broadcast_row(A["L1_gnn_bias"], P)).then_inc(w_in, 16)
            sp.dma_start(late[:, 1, :], broadcast_row(A["L2_gnn_bias"], P)).then_inc(w_in, 16)
            sp.dma_start(gain[:, :], broadcast_row(A["L0_gnn_eps"], P)).then_inc(w_in, 16)
            for b in range(2):
                sp.sem_inc(x1_out[b], 16)
                sp.sem_inc(x3_out[b], 16)

            def body(t):
                b = t.slot(2)
                sp.wait_ge(x1_ready, t.g * 2 + 4)
                sp.dma_start(in_dram(x1_dram, t), on_chip(x1, b, t)).then_inc(x1_out[b], 16)
                if t.ahead(XB).exists():
                    load(t.ahead(XB))
                sp.wait_ge(x3_ready, t.g + 3)
                sp.dma_start(in_dram(out, t), on_chip(x3, b, t)).then_inc(x3_out[b], 16)

            for t in start[1:]:
                load(t)
            over_groups(sp, NG, UN, 2 * UN, body)
            for b in range(2):
                sp.wait_ge(x1_out[b], 16 * (NG // 2 + 1))
                sp.wait_ge(x3_out[b], 16 * (NG // 2 + 1))

        @block.gpsimd
        def _(pool):
            pool.sem_inc(x3_ready, 2)
            R.start_by_node(pool)
            pool.wait_ge(late_ready, 2)

            def body(t):
                b = t.slot(2)
                pool.wait_ge(h_ready, t.g + 1)
                pool.tensor_tensor(x[:, t.r, :, :], x[:, t.r, :, :],
                                   b2[:, :].unsqueeze(1).to_broadcast([P, G, D]), ALU.add).then_inc(x_shifted, 1)
                R.put_by_node(pool, t)
                pool.wait_ge(x1_ready, t.g * 2 + 4)
                pool.wait_ge(x3_out[b], t.round(2) * 16)
                pool.tensor_tensor(x3[:, b, :, :], x1[:, b, :, :],
                                   late_sum[:, :].unsqueeze(1).to_broadcast([P, G, D]), ALU.add) \
                    .then_inc(x3_ready, 1)

            groups(pool, body)
            R.end_by_node(pool)

        @block.vector
        def _(dve):
            def statistics(t):
                dve.wait_ge(x_in[t.r], t.round(UN) * 32)
                norm.statistics(dve, t.g, t.slot(2), x[:, t.r, :, :])

            def mix(t):
                dve.wait_ge(h_ready, t.g + 1)
                dve.scalar_tensor_tensor(out=agg[:, t.r, :, :].rearrange("p j d -> p (j d)"),
                                         in0=h[:, t.slot(2), :, :].rearrange("p j d -> p (j d)"),
                                         scalar=gain[:, 0:1],
                                         in1=agg[:, t.r, :, :].rearrange("p j d -> p (j d)"),
                                         op0=ALU.mult, op1=ALU.add).then_inc(mixed, 1)

            def first_half(t):
                dve.wait_ge(turned, t.g + 1)
                dve.tensor_copy(h_t[:, t.slot(2), 0, :], p_t[0][:, :]).then_inc(h_t_ready, 1)

            def body(t):
                b = t.slot(2)
                if t.ahead(2).exists():
                    statistics(t.ahead(2))
                    norm.scales(dve, t.ahead(2).g, b)
                if t.ahead(1).exists():
                    first_half(t.ahead(1))
                if t.ahead(2).exists():
                    mix(t.ahead(2))
                dve.wait_ge(x_shifted, t.g + 1)
                dve.wait_ge(x1_out[b], t.round(2) * 16)
                dve.wait_ge(x3_ready, t.g + 1)
                for c in range(2):
                    dve.wait_ge(o_mm, t.g * 2 + c + 1)
                    dve.tensor_tensor(x1[:, b, 2 * c:2 * c + 2, :], x[:, t.r, 2 * c:2 * c + 2, :], p_o[c][:, :, :],
                                      ALU.add).then_inc(x1_ready, 1)

            for t in start[0:2]:
                statistics(t)
                norm.scales(dve, t.g, t.slot(2))
                if t.g == 0:
                    dve.wait_ge(w_in, 16 * 7)
                    dve.tensor_tensor(late_sum[:, :], late[:, 0, :], late[:, 1, :], ALU.add).then_inc(late_ready, 1)
                    dve.tensor_scalar(gain[:, :], gain[:, :], 1.0, None, ALU.add).then_inc(late_ready, 1)
                    dve.wait_ge(late_ready, 2)
                mix(t)
                if t.g == 0:
                    first_half(t)
            groups(dve, body)

        @block.scalar
        def _(act):
            def hidden(t, k):
                act.wait_ge(hid_mm, t.g * HC + k + 1)
                act.activation(hid[:, t.slot(2), k, :], p_h[k][:, :], ACT.Relu, bias=b1[:, k:k + 1]) \
                   .then_inc(hid_ready, 1)

            def rows(t):
                norm.rows_out(act, t.g, t.slot(2), h[:, t.slot(2), :, :], x[:, t.r, :, :]).then_inc(h_ready, 1)

            def second_half(t):
                act.wait_ge(turned, t.g + 1)
                act.copy(h_t[:, t.slot(2), 1, :], p_t[1][:, :]).then_inc(h_t_ready, 1)

            def body(t):
                if t.ahead(2).exists():
                    act.wait_ge(mixed, t.g + 1)
                    norm.root(act, t.ahead(2).g, t.slot(2))
                hidden(t, 0)
                if t.ahead(2).exists():
                    rows(t.ahead(2))
                for k in range(1, HC):
                    hidden(t, k)
                if t.ahead(1).exists():
                    second_half(t.ahead(1))

            for t in start[0:2]:
                norm.root(act, t.g, t.slot(2))
                rows(t)
                if t.g == 0:
                    second_half(t)
            act.wait_ge(w_in, 16 * 7)
            groups(act, body)

        @block.tensor
        def _(pe):
            pe.sem_inc(hid_ready, HC)
            pe.sem_inc(h_t_ready, 2)
            pe.sem_inc(x1_ready, 2)

            def turn(t):
                pe.wait_ge(mixed, t.g + 1)
                pe.wait_ge(h_t_ready, t.g * 2 + 2)
                for c in range(DC):
                    for j in range(1 if is_last(t) else G):
                        p = REST if is_last(t) else P
                        mm = pe.transpose(p_t[c][:, j * P:j * P + p], agg[0:p, t.r, j, c * P:(c + 1) * P],
                                          K["ident"][0:p, 0:p])
                mm.then_inc(turned, 1)

            def body(t):
                b = t.slot(2)
                pe.wait_ge(h_t_ready, t.g * 2 + 4)
                for k in range(HC):
                    pe.wait_ge(hid_ready, t.g * HC + k + 1)
                    for c in range(DC):
                        n = REST if is_last(t) else ROWS
                        mm = pe.matmul(p_h[k][:, 0:n], w1[:, c, k * P:(k + 1) * P], h_t[:, b, c, 0:n],
                                       start=(c == 0), stop=(c == DC - 1))
                    mm.then_inc(hid_mm, 1)
                if t.ahead(1).exists():
                    turn(t.ahead(1))
                pe.wait_ge(hid_ready, t.g * HC + 2 * HC)
                if is_last(t):
                    pe.wait_ge(x1_ready, t.g * 2 + 2)
                    for k in range(HC):
                        mm = pe.matmul(p_o[0][0:REST, 0, :], hid[:, b, k, 0:REST], w2[:, k, :],
                                       start=(k == 0), stop=(k == HC - 1))
                    mm.then_inc(o_mm, 2)
                    return
                for c in range(2):
                    pe.wait_ge(x1_ready, t.g * 2 + c + 1)
                    for jj in range(2):
                        j = 2 * c + jj
                        for k in range(HC):
                            mm = pe.matmul(p_o[c][:, jj, :], hid[:, b, k, j * P:(j + 1) * P], w2[:, k, :],
                                           start=(k == 0), stop=(k == HC - 1))
                    mm.then_inc(o_mm, 1)

            turn(start[0])
            pe.wait_ge(w_in, 16 * 7)
            groups(pe, body)


def relation_layer(nc, K, A, V, rec_c, rec_d, x1_dram, out):
    N = out.shape[0]
    NG = rec_c.shape[0] // GE
    with ExitStack() as ctx:
        def sb(name, shape, dt=F32):
            return ctx.enter_context(nc.sbuf_tensor(name, shape, dt))

        def pb(name, shape, dt=F32):
            return ctx.enter_context(nc.psum_tensor(name, shape, dt))

        sem = signals(nc, K, "rl")
        w = sb("rl_w", [P, DC, D])
        rec = sb("rl_rec", [TE, 2, G, RC])
        keep = sb("rl_keep", [TE, 4, G, RC])
        idx = sb("rl_idx", [TE, 2, G], I32)
        put_idx = sb("rl_put_idx", [TE, 4, G], I32)
        x = sb("rl_x", [TE, 2, G, D])
        h = sb("rl_h", [TE, 2, G, D])
        same = sb("rl_same", [P, 2, GE])
        run = sb("rl_run", [P, 2, DC, GE])
        rows = sb("rl_rows", [TE, 2, G, D])
        p_s = pb("rl_p_s", [P, 512])
        p_t = [[pb(f"rl_p_t{b}{c}", [P, 512]) for c in range(DC)] for b in range(2)]
        p_o = [pb(f"rl_p_o{c}", [TE, 2, D]) for c in range(2)]
        norm = Norm(nc, ctx, "rl", sem, TE, G, K["eps"])

        w_in = sem("w_in")
        rec_d_in = sem("rec_d_in")
        rec_in = [sem(f"rec_in{b}") for b in range(2)]
        x_in = [sem(f"x_in{b}") for b in range(2)]
        put = [sem(f"put{b}") for b in range(4)]
        idx_ready = sem("idx_ready")
        h_ready = sem("h_ready")
        weighted = sem("weighted")
        same_mm = sem("same_mm")
        same_ready = sem("same_ready")
        turned = sem("turned")
        run_ready = sem("run_ready")
        o_mm = sem("o_mm")
        rows_ready = sem("rows_ready")
        passed = sem("passed")
        block = ctx.enter_context(nc.Block())

        def groups(eng, body):
            over_groups(eng, NG, 4, 4, body)

        first = [Step(0, r, 4, NG) for r in range(4)]

        @block.sync
        def _(sp):
            sp.sem_inc(idx_ready, 2)

            def load(t):
                b = t.slot(2)
                sp.wait_ge(idx_ready, t.g + 1)
                sp.dma_start(rec[:, b, :, :], rows_of(rec_c, t.g, G, TE)).then_inc(rec_in[b], 16)

            groups(sp, load)

        @block.gpsimd
        def _(pool):
            for k in range(4):
                open_slot(pool, K, put[k], 16 * G)

            def fetch(t):
                b = t.slot(2)
                pool.wait_ge(idx_ready, t.g + 3)
                pool.sem_inc(passed, 1)
                for j in range(G):
                    pool.indirect_dma_start(x[:, b, j, :], None, x1_dram[:, :], IOA(idx[:, b, j:j + 1], 0),
                                            bounds_check=N - 1, oob_is_err=False).then_inc(x_in[b], 16)

            def body(t):
                pool.wait_ge(rows_ready, t.g * 2 + 4)
                pool.sem_inc(passed, 1)
                for j in range(G):
                    pool.indirect_dma_start(out[:, :], IOA(put_idx[:, t.slot(4), j:j + 1], 0),
                                            rows[:, t.slot(2), j, :], None, bounds_check=N - 1, oob_is_err=False,
                                            compute_op=ALU.add).then_inc(put[t.slot(4)], 16)
                if t.ahead(4).exists():
                    fetch(t.ahead(4))

            for t in first:
                fetch(t)
            groups(pool, body)
            for k in range(4):
                pool.wait_ge(put[k], 16 * G * (NG // 4 + 1))

        @block.vector
        def _(dve):
            def take(t):
                b = t.slot(2)
                dve.wait_ge(rec_in[b], t.round(2) * 16)
                dve.wait_ge(same_mm, t.g + 1)
                dve.tensor_copy(keep[:, t.slot(4), :, :], rec[:, b, :, :])
                dve.tensor_copy(idx[:, b, :], rec[:, b, :, C_PEER]).then_inc(idx_ready, 1)

            def statistics(t):
                b = t.slot(2)
                dve.wait_ge(x_in[b], t.round(2) * (16 * G))
                norm.statistics(dve, t.g, b, x[:, b, :, :])
                norm.scales(dve, t.g, b)

            def weigh(t):
                b, k = t.slot(2), t.slot(4)
                dve.wait_ge(idx_ready, t.g + 3)
                dve.wait_ge(put[k], t.round(4) * (16 * G))
                dve.tensor_copy(put_idx[:, k, :], keep[:, k, :, C_PUT])
                dve.wait_ge(h_ready, t.g + 1)
                for j in range(G):
                    ins = dve.tensor_scalar(h[:, b, j, :], h[:, b, j, :], keep[:, k, j, C_W:C_W + 1], None, ALU.mult)
                ins.then_inc(weighted, 1)
                if t.ahead(2).exists():
                    take(t.ahead(2))

            def body(t):
                b = t.slot(2)
                dve.wait_ge(same_ready, t.g + 2)
                dve.wait_ge(turned, t.g + 1)
                dve.wait_ge(run_ready, t.g * 2 + 4)
                for c in range(DC):
                    dve.tensor_tensor_scan(run[:, b, c, :], same[:, b, :], p_t[b][c][:, 0:GE],
                                           run[:, 1 - b, c, GE - 1:GE], ALU.mult, ALU.add).then_inc(run_ready, 1)
                if t.ahead(2).exists():
                    statistics(t.ahead(2))
                    weigh(t.ahead(2))

            dve.memset(run[:, 1, :, GE - 1], 0.0).then_inc(run_ready, 4)
            dve.sem_inc(same_mm, 4)
            take(first[0])
            take(first[1])
            for t in first[0:2]:
                statistics(t)
                weigh(t)
            groups(dve, body)

        @block.scalar
        def _(act):
            def prepare(t):
                b = t.slot(2)
                norm.root(act, t.g, b)
                norm.rows_out(act, t.g, b, h[:, b, :, :], x[:, b, :, :]).then_inc(h_ready, 1)

            def mask(t):
                act.wait_ge(same_mm, t.g + 5)
                act.copy(same[:, t.slot(2), :], p_s[:, 0:GE]).then_inc(same_ready, 1)

            def body(t):
                if t.ahead(1).exists():
                    mask(t.ahead(1))
                if t.ahead(2).exists():
                    prepare(t.ahead(2))
                b = t.slot(2)
                before = t.ahead(-2)
                act.wait_ge(put[before.slot(4)], (before.round(4) + 1) * (16 * G))
                for c in range(2):
                    act.wait_ge(o_mm, t.g * 2 + c + 1)
                    act.copy(rows[:, b, 2 * c:2 * c + 2, :], p_o[c][:, :, :]).then_inc(rows_ready, 1)

            act.dma_start(w[:, :, :], A["L1_gnn_weight"].rearrange("(k p) n -> p k n", p=P)).then_inc(w_in, 16)
            act.dma_start(V["rec"][:, :, :], rec_d.rearrange("(t p) c -> p t c", p=TE)).then_inc(rec_d_in, 16)
            prepare(first[0])
            mask(first[0])
            prepare(first[1])
            groups(act, body)
            act.wait_ge(rec_d_in, 16)

        @block.tensor
        def _(pe):
            def turn(t):
                b, k = t.slot(2), t.slot(4)
                pe.wait_ge(idx_ready, t.g + 3)
                pe.wait_ge(same_ready, t.g + 1)
                for j in range(G):
                    mm = pe.matmul(p_s[:, j * TE:(j + 1) * TE],
                                   keep[:, k, j, C_SAME:C_SAME + 1].to_broadcast([TE, P]),
                                   K["ident"][0:TE, 0:TE], start=True, stop=True)
                mm.then_inc(same_mm, 1)
                pe.wait_ge(weighted, t.g + 1)
                pe.wait_ge(run_ready, t.g * 2 + 2)
                for c in range(DC):
                    for j in range(G):
                        mm = pe.transpose(p_t[b][c][:, j * TE:(j + 1) * TE], h[:, b, j, c * P:(c + 1) * P],
                                          K["ident"][0:TE, 0:TE])
                mm.then_inc(turned, 1)

            def body(t):
                b = t.slot(2)
                if t.ahead(1).exists():
                    turn(t.ahead(1))
                pe.wait_ge(run_ready, t.g * 2 + 6)
                for c in range(2):
                    pe.wait_ge(rows_ready, t.g * 2 + c + 1)
                    for jj in range(2):
                        j = 2 * c + jj
                        for k in range(DC):
                            mm = pe.matmul(p_o[c][:, jj, :], run[:, b, k, j * TE:(j + 1) * TE], w[:, k, :],
                                           start=(k == 0), stop=(k == DC - 1))
                    mm.then_inc(o_mm, 1)

            pe.wait_ge(w_in, 16)
            pe.sem_inc(same_ready, 1)
            pe.sem_inc(rows_ready, 2)
            turn(first[0])
            groups(pe, body)


def attention_scores(nc, K, A, V, out):
    NG = V["edges"] // GE
    NHEAD, DH = A["L2_gnn_a_src"].shape
    WS = D + NHEAD
    with ExitStack() as ctx:
        def sb(name, shape, dt=F32):
            return ctx.enter_context(nc.sbuf_tensor(name, shape, dt))

        def pb(name, shape, dt=F32):
            return ctx.enter_context(nc.psum_tensor(name, shape, dt))

        sem = signals(nc, K, "as")
        w = sb("as_w", [P, DC, D])
        w_t = sb("as_w_t", [P, DC, WS])
        a_col = sb("as_a_col", [P, DC])
        a_blocks = sb("as_a_blocks", [P, DC, NHEAD])
        a_dst = sb("as_a_dst", [TE, D])
        w_edge = sb("as_w_edge", [4, D])
        bias = sb("as_bias", [TE, D])
        rec = V["rec"]
        attr = sb("as_attr", [TE, 2, G, 4])
        idx = sb("as_idx", [TE, 2, 2, G], I32)
        x = sb("as_x", [TE, 2, 2 * G, D])
        h = sb("as_h", [TE, 2 * G, D])
        h_t = sb("as_h_t", [P, 2, 2 * DC, GE])
        attr_t = sb("as_attr_t", [4, 2, GE])
        enc = sb("as_enc", [TE, 2, D])
        score = sb("as_score", [TE, 2, G, NHEAD])
        score_l = sb("as_score_l", [TE, 2, G, NHEAD])
        p_a = pb("as_p_a", [4, 512])
        p_s = pb("as_p_s", [NHEAD, 512])
        p_t = [pb(f"as_p_t{c}", [P, 512]) for c in range(DC)]
        p_src = [pb(f"as_p_src{c}", [TE, 512]) for c in range(2)]
        p_dst = [pb(f"as_p_dst{c}", [TE, 2, D]) for c in range(2)]
        norm = Norm(nc, ctx, "as", sem, TE, 2 * G, K["eps"])

        w_in = sem("w_in")
        setup = sem("setup")
        w_turned = sem("w_turned")
        w_ready = sem("w_ready")
        x_in = [sem(f"x_in{b}") for b in range(2)]
        x_ready = sem("x_ready")
        idx_ready = sem("idx_ready")
        h_ready = sem("h_ready")
        attr_ready = sem("attr_ready")
        attr_turned = sem("attr_turned")
        attr_t_ready = sem("attr_t_ready")
        turned = sem("turned")
        h_t_ready = sem("h_t_ready")
        src_mm = sem("src_mm")
        dst_mm = sem("dst_mm")
        src_kept = sem("src_kept")
        enc_shifted = sem("enc_shifted")
        enc_scaled = sem("enc_scaled")
        enc_summed = sem("enc_summed")
        score_summed = sem("score_summed")
        score_ready = sem("score_ready")
        score_turned = sem("score_turned")
        score_kept = sem("score_kept")
        passed = sem("passed")
        block = ctx.enter_context(nc.Block())

        def groups(eng, body):
            over_groups(eng, NG, 2, 4, body)

        first = [Step(0, b, 2, NG) for b in range(4)]

        @block.sync
        def _(sp):
            sp.dma_start(w[:, :, :], A["L2_gnn_W"].rearrange("(k p) n -> p k n", p=P)).then_inc(w_in, 16)
            with nc.allow_non_contiguous_dma(reason="a few small weights"):
                sp.dma_start(a_col[:, :], A["L2_gnn_a_src"].rearrange("h d -> (h d)").rearrange("(k p) -> p k", p=P)) \
                    .then_inc(w_in, 16)
                sp.dma_start(w_edge[0:3, :], A["L2_gnn_edge_W"].rearrange("n c -> c n")).then_inc(w_in, 16)
            sp.dma_start(w_edge[3:4, :], broadcast_row(A["L2_gnn_edge_b"], 1)).then_inc(w_in, 16)
            sp.dma_start(a_dst[:, :], broadcast_row(A["L2_gnn_a_dst"].rearrange("h d -> (h d)"), TE)).then_inc(w_in, 16)
            sp.dma_start(bias[:, :], broadcast_row(A["L2_gnn_bias"], TE)).then_inc(w_in, 16)

        @block.gpsimd
        def _(pool):
            pool.memset(a_blocks[:, :, :], 1.0).then_inc(setup, 1)
            pool.wait_ge(setup, 1)
            pool.affine_select(out=a_blocks[:, :, :], in_=a_blocks[:, :, :], compare_op=ALU.is_ge, fill=0.0,
                               base=0, pattern=[[P, DC], [-DH, NHEAD]], channel_multiplier=1).then_inc(setup, 1)
            pool.wait_ge(setup, 2)
            pool.affine_select(out=a_blocks[:, :, :], in_=a_blocks[:, :, :], compare_op=ALU.is_ge, fill=0.0,
                               base=DH - 1, pattern=[[-P, DC], [DH, NHEAD]], channel_multiplier=-1).then_inc(setup, 1)

            def fetch(t):
                b = t.slot(2)
                pool.wait_ge(idx_ready, t.g + 1)
                pool.sem_inc(passed, 1)
                for j in range(G):
                    for s in range(2):
                        pool.indirect_dma_start(x[:, b, s * G + j, :], None, out[:, :],
                                                IOA(idx[:, b, s, j:j + 1], 0), bounds_check=out.shape[0] - 1,
                                                oob_is_err=False).then_inc(x_in[b], 16)

            over_groups(pool, NG, 2, 0, fetch)

        @block.vector
        def _(dve):
            def take(t):
                tiles = bass.ds(t.g * G, G)
                dve.tensor_copy(idx[:, t.slot(2), 0, :], rec[:, tiles, D_SRC])
                dve.tensor_copy(idx[:, t.slot(2), 1, :], rec[:, tiles, D_DST]).then_inc(idx_ready, 1)

            take(first[0])
            take(first[1])
            dve.memset(V["fence"][:, V["edges"]:], NEG)
            dve.tensor_scalar(V["fence"][:, 0:V["edges"]], K["same"][0:NHEAD, :], -1.0, -NEG, ALU.add, ALU.mult)
            dve.wait_ge(w_in, 96)
            dve.wait_ge(setup, 3)
            for k in range(DC):
                ins = dve.tensor_scalar(a_blocks[:, k, :], a_blocks[:, k, :], a_col[:, k:k + 1], None, ALU.mult)
            ins.then_inc(setup, 1)
            dve.wait_ge(w_turned, 1)
            for k in range(DC):
                ins = dve.tensor_copy(w_t[:, k, :], p_t[k][:, 0:WS])
            ins.then_inc(w_ready, 1)

            def receive(t):
                b = t.slot(2)
                dve.tensor_copy(attr[:, b, :, :], rec[:, bass.ds(t.g * G, G), D_A3:D_A3 + 4]).then_inc(attr_ready, 1)
                dve.wait_ge(x_in[b], t.round(2) * (32 * G))
                dve.tensor_tensor(x[:, b, :, :], x[:, b, :, :], bias[:, :].unsqueeze(1).to_broadcast([TE, 2 * G, D]),
                                  ALU.subtract).then_inc(x_ready, 1)

            def statistics(t):
                dve.wait_ge(x_ready, t.g + 1)
                norm.statistics(dve, t.g, t.slot(2), x[:, t.slot(2), :, :])
                norm.scales(dve, t.g, t.slot(2))

            def first_half(t, s):
                dve.wait_ge(turned, t.g * 2 + s + 1)
                dve.tensor_copy(h_t[:, t.slot(2), s * DC, :], p_t[0][:, 0:GE]).then_inc(h_t_ready, 1)

            def encode(t, j):
                b = t.slot(2)
                dve.wait_ge(dst_mm, t.g * G + j + 1)
                dve.scalar_tensor_tensor(out=enc[:, j % 2, :], in0=p_dst[j % 2][:, 1, :], scalar=0.0,
                                         in1=a_dst[:, :], op0=ALU.max, op1=ALU.add).then_inc(enc_shifted, 1)
                dve.wait_ge(enc_shifted, t.g * G + j + 1)
                dve.tensor_tensor(enc[:, j % 2, :], enc[:, j % 2, :], p_dst[j % 2][:, 0, :], ALU.mult) \
                   .then_inc(enc_scaled, 1)
                dve.wait_ge(enc_scaled, t.g * G + j + 3)
                dve.tensor_reduce(score[:, b, j, :], enc[:, j % 2, :].rearrange("p (h d) -> p h d", h=NHEAD),
                                  AX.X, ALU.add).then_inc(enc_summed, 1)

            def body(t):
                b = t.slot(2)
                for j in range(G):
                    encode(t, j)
                if t.ahead(1).exists():
                    dve.wait_ge(h_ready, t.g + 2)
                if t.ahead(3).exists():
                    take(t.ahead(3))
                if t.ahead(1).exists():
                    first_half(t.ahead(1), 0)
                if t.ahead(2).exists():
                    receive(t.ahead(2))
                dve.wait_ge(enc_summed, t.g * G + G)
                dve.wait_ge(src_kept, t.g * G + G + 2)
                dve.tensor_tensor(score[:, b, :, :], score[:, b, :, :],
                                  V["proj"][:, bass.ds(t.g * G, G), D:WS], ALU.add).then_inc(score_summed, 1)
                dve.wait_ge(score_summed, t.g + 1)
                dve.scalar_tensor_tensor(out=score_l[:, b, :, :], in0=score[:, b, :, :], scalar=0.2,
                                         in1=score[:, b, :, :], op0=ALU.mult, op1=ALU.max).then_inc(score_ready, 1)
                if t.ahead(1).exists():
                    first_half(t.ahead(1), 1)
                if t.ahead(2).exists():
                    statistics(t.ahead(2))

            receive(first[0])
            statistics(first[0])
            dve.wait_ge(h_ready, 1)
            take(first[2])
            first_half(first[0], 0)
            first_half(first[0], 1)
            receive(first[1])
            statistics(first[1])
            groups(dve, body)

        @block.scalar
        def _(act):
            def rows(t):
                b = t.slot(2)
                norm.rows_out(act, t.g, b, h[:, :, :], x[:, b, :, :]).then_inc(h_ready, 1)

            def attributes(t):
                act.wait_ge(attr_turned, t.g + 1)
                act.copy(attr_t[:, t.slot(2), :], p_a[:, 0:GE]).then_inc(attr_t_ready, 1)

            def second_half(t, s):
                act.wait_ge(turned, t.g * 2 + s + 1)
                act.copy(h_t[:, t.slot(2), s * DC + 1, :], p_t[1][:, 0:GE]).then_inc(h_t_ready, 1)

            def body(t):
                if t.ahead(1).exists():
                    act.wait_ge(turned, t.g * 2 + 2)
                    rows(t.ahead(1))
                    attributes(t.ahead(1))
                    second_half(t.ahead(1), 0)
                for j in range(G):
                    act.wait_ge(src_mm, t.g * G + j + 1)
                    act.copy(V["proj"][:, bass.ds(t.g * G + j, 1), :].rearrange("p t n -> p (t n)"),
                             p_src[j % 2][:, 0:WS]).then_inc(src_kept, 1)
                if t.ahead(1).exists():
                    second_half(t.ahead(1), 1)
                act.wait_ge(score_turned, t.g + 1)
                act.copy(V["score_t"][:, bass.ds(t.g * GE, GE)], p_s[:, 0:GE]).then_inc(score_kept, 1)
                if t.ahead(2).exists():
                    norm.root(act, t.ahead(2).g, t.slot(2))

            norm.root(act, 0, 0)
            rows(first[0])
            attributes(first[0])
            second_half(first[0], 0)
            second_half(first[0], 1)
            norm.root(act, 1, 1)
            groups(act, body)

        @block.tensor
        def _(pe):
            pe.wait_ge(w_in, 96)
            for k in range(DC):
                for n in range(DC):
                    pe.transpose(p_t[k][:, n * P:(n + 1) * P], w[:, n, k * P:(k + 1) * P], K["ident"][:, :])
            pe.wait_ge(setup, 4)
            for k in range(DC):
                for n in range(DC):
                    mm = pe.matmul(p_t[k][:, D:WS], w[:, n, k * P:(k + 1) * P], a_blocks[:, n, :],
                                   start=(n == 0), stop=(n == DC - 1))
            mm.then_inc(w_turned, 1)
            pe.sem_inc(attr_t_ready, 1)
            pe.sem_inc(score_kept, 1)
            pe.sem_inc(src_kept, 2)
            pe.sem_inc(enc_scaled, 2)
            pe.wait_ge(w_ready, 1)
            pe.sem_inc(h_t_ready, 2)

            def turn_attributes(t):
                b = t.slot(2)
                pe.wait_ge(attr_ready, t.g + 1)
                pe.wait_ge(attr_t_ready, t.g + 1)
                for j in range(G):
                    mm = pe.transpose(p_a[:, j * TE:(j + 1) * TE], attr[:, b, j, :], K["ident"][0:TE, 0:TE])
                mm.then_inc(attr_turned, 1)

            def turn(t, s):
                pe.wait_ge(h_ready, t.g + 1)
                pe.wait_ge(h_t_ready, t.g * 4 + s * 2 + 2)
                for c in range(DC):
                    for j in range(G):
                        mm = pe.transpose(p_t[c][:, j * TE:(j + 1) * TE], h[:, s * G + j, c * P:(c + 1) * P],
                                          K["ident"][0:TE, 0:TE])
                mm.then_inc(turned, 1)

            def body(t):
                b = t.slot(2)
                if t.ahead(1).exists():
                    turn_attributes(t.ahead(1))
                pe.wait_ge(h_t_ready, t.g * 4 + 6)
                pe.wait_ge(attr_t_ready, t.g + 2)
                for j in range(G):
                    cols = slice(j * TE, (j + 1) * TE)
                    pe.wait_ge(enc_scaled, t.g * G + j + 1)
                    for k in range(DC):
                        pe.matmul(p_dst[j % 2][:, 0, :], h_t[:, b, DC + k, cols], w_t[:, k, 0:D],
                                  start=(k == 0), stop=(k == DC - 1))
                    pe.matmul(p_dst[j % 2][:, 1, :], attr_t[:, b, cols], w_edge[:, :], start=True, stop=True) \
                        .then_inc(dst_mm, 1)
                if t.ahead(1).exists():
                    turn(t.ahead(1), 0)
                for j in range(G):
                    cols = slice(j * TE, (j + 1) * TE)
                    pe.wait_ge(src_kept, t.g * G + j + 1)
                    for k in range(DC):
                        mm = pe.matmul(p_src[j % 2][:, 0:WS], h_t[:, b, k, cols], w_t[:, k, :],
                                       start=(k == 0), stop=(k == DC - 1))
                    mm.then_inc(src_mm, 1)
                if t.ahead(1).exists():
                    turn(t.ahead(1), 1)
                pe.wait_ge(score_ready, t.g + 1)
                pe.wait_ge(score_kept, t.g + 1)
                for j in range(G):
                    mm = pe.transpose(p_s[:, j * TE:(j + 1) * TE], score_l[:, b, j, :], K["ident"][0:TE, 0:TE])
                mm.then_inc(score_turned, 1)

            turn_attributes(first[0])
            turn(first[0], 0)
            turn(first[0], 1)
            groups(pe, body)


def above_run(dve, V, upto, step):
    score, fence = V["score_t"], V["fence"]
    E = V["edges"]
    dve.tensor_tensor_scan(upto[:, :], fence[:, 0:E], score[:, :], NEG, ALU.add, ALU.max).then_inc(step, 1)
    dve.wait_ge(step, 1)
    dve.tensor_tensor_scan(upto[:, ::-1], fence[:, E:0:-1], upto[:, ::-1], NEG, ALU.add, ALU.max).then_inc(step, 1)
    dve.wait_ge(step, 2)
    return dve.tensor_tensor(score[:, :], score[:, :], upto[:, :], ALU.subtract)


def top_of_all(dve, V, NHEAD, top, step):
    dve.tensor_reduce(top[:, 0:1], V["score_t"][0:NHEAD, :], AX.X, ALU.max).then_inc(step, 1)
    dve.wait_ge(step, 1)
    return dve.tensor_scalar(top[:, 1:2], top[:, 0:1], -1.0, None, ALU.mult)


def message_scores(nc, K, A, V, x3_dram):
    NG = V["edges"] // GE
    N = x3_dram.shape[0]
    DM = A["L3_gnn_W_forward"].shape[0]
    NHEAD = A["L3_gnn_attn_forward"].shape[1]
    WS = DM + NHEAD
    with ExitStack() as ctx:
        def sb(name, shape, dt=F32):
            return ctx.enter_context(nc.sbuf_tensor(name, shape, dt))

        def pb(name, shape, dt=F32):
            return ctx.enter_context(nc.psum_tensor(name, shape, dt))

        sem = signals(nc, K, "ms")
        w = sb("ms_w", [DM, 2, D])
        attn = sb("ms_attn", [NHEAD, DM])
        attn_t = sb("ms_attn_t", [DM, NHEAD])
        w_t = sb("ms_w_t", [P, DC, 2, WS])
        rec = V["rec"]
        idx = sb("ms_idx", [TE, 2, G], I32)
        x = sb("ms_x", [TE, 2, G, D])
        h = sb("ms_h", [TE, 2, G, D])
        h_t = sb("ms_h_t", [P, 2, DC, GE])
        scaled = sb("ms_scaled", [TE, 2, 2, G, WS])
        score = sb("ms_score", [TE, 2, G, NHEAD])
        score_l = sb("ms_score_l", [TE, 2, G, NHEAD])
        p_a = pb("ms_p_a", [P, 512])
        p_t = [pb(f"ms_p_t{c}", [P, 512]) for c in range(DC)]
        p_m = [pb(f"ms_p_m{c}", [TE, 2, 2, P]) for c in range(2)]
        norm = Norm(nc, ctx, "ms", sem, TE, G, K["eps"])

        w_in = sem("w_in")
        attn_turned = sem("attn_turned")
        attn_ready = sem("attn_ready")
        w_turned = sem("w_turned")
        w_ready = sem("w_ready")
        x_in = [sem(f"x_in{b}") for b in range(2)]
        idx_ready = sem("idx_ready")
        h_ready = sem("h_ready")
        turned = sem("turned")
        h_t_ready = sem("h_t_ready")
        m_mm = sem("m_mm")
        m_scaled = sem("m_scaled")
        score_summed = sem("score_summed")
        score_ready = sem("score_ready")
        score_turned = sem("score_turned")
        score_kept = sem("score_kept")
        passed = sem("passed")
        block = ctx.enter_context(nc.Block())

        def groups(eng, body):
            over_groups(eng, NG, 2, 4, body)

        first = [Step(0, b, 2, NG) for b in range(4)]

        @block.sync
        def _(sp):
            sp.dma_start(w[:, 0, :], A["L3_gnn_W_forward"]).then_inc(w_in, 16)
            sp.dma_start(w[:, 1, :], A["L3_gnn_W_reverse"]).then_inc(w_in, 16)
            sp.dma_start(attn[:, :], A["L3_gnn_attn_forward"].rearrange("a h f -> (a h) f")).then_inc(w_in, 16)

        @block.gpsimd
        def _(pool):
            def fetch(t):
                b = t.slot(2)
                pool.wait_ge(idx_ready, t.g + 1)
                pool.sem_inc(passed, 1)
                for j in range(G):
                    pool.indirect_dma_start(x[:, b, j, :], None, x3_dram[:, :], IOA(idx[:, b, j:j + 1], 0),
                                            bounds_check=N - 1, oob_is_err=False).then_inc(x_in[b], 16)

            over_groups(pool, NG, 2, 0, fetch)

        @block.vector
        def _(dve):
            def take(t):
                dve.tensor_copy(idx[:, t.slot(2), :], rec[:, bass.ds(t.g * G, G), D_SRC]).then_inc(idx_ready, 1)

            take(first[0])
            take(first[1])
            dve.wait_ge(attn_turned, 1)
            dve.tensor_copy(attn_t[:, :], p_a[0:DM, 0:NHEAD]).then_inc(attn_ready, 1)
            dve.wait_ge(w_turned, 1)
            for k in range(DC):
                ins = dve.tensor_copy(w_t[:, k, :, :].rearrange("p s n -> p (s n)"), p_t[k][:, 0:2 * WS])
            ins.then_inc(w_ready, 1)

            def statistics(t):
                b = t.slot(2)
                dve.wait_ge(x_in[b], t.round(2) * (16 * G))
                norm.statistics(dve, t.g, b, x[:, b, :, :])

            def first_half(t):
                dve.wait_ge(turned, t.g + 1)
                dve.tensor_copy(h_t[:, t.slot(2), 0, :], p_t[0][:, 0:GE]).then_inc(h_t_ready, 1)

            def body(t):
                b = t.slot(2)
                if t.ahead(2).exists():
                    statistics(t.ahead(2))
                if t.ahead(1).exists():
                    first_half(t.ahead(1))
                if t.ahead(2).exists():
                    norm.scales(dve, t.ahead(2).g, b)
                dve.wait_ge(m_scaled, t.g * 2 + 4)
                dve.tensor_tensor(V["proj"][:, bass.ds(t.g * G, G), 0:DM], scaled[:, b, 0, :, 0:DM],
                                  scaled[:, b, 1, :, 0:DM], ALU.add)
                dve.tensor_tensor(score[:, b, :, :], scaled[:, b, 0, :, DM:WS], scaled[:, b, 1, :, DM:WS],
                                  ALU.add).then_inc(score_summed, 1)
                dve.wait_ge(score_summed, t.g + 1)
                dve.scalar_tensor_tensor(out=score_l[:, b, :, :], in0=score[:, b, :, :], scalar=0.2,
                                         in1=score[:, b, :, :], op0=ALU.mult, op1=ALU.max).then_inc(score_ready, 1)
                if t.ahead(4).exists():
                    dve.wait_ge(h_ready, t.g + 3)
                    take(t.ahead(4))

            for t in first[0:2]:
                statistics(t)
                norm.scales(dve, t.g, t.slot(2))
                dve.wait_ge(h_ready, t.g + 1)
                take(t.ahead(2))
                if t.g == 0:
                    first_half(t)
            groups(dve, body)

        @block.scalar
        def _(act):
            def rows(t):
                b = t.slot(2)
                norm.root(act, t.g, b)
                norm.rows_out(act, t.g, b, h[:, b, :, :], x[:, b, :, :]).then_inc(h_ready, 1)

            def second_half(t):
                act.wait_ge(turned, t.g + 1)
                act.copy(h_t[:, t.slot(2), 1, :], p_t[1][:, 0:GE]).then_inc(h_t_ready, 1)

            def body(t):
                b = t.slot(2)
                for c in range(2):
                    act.wait_ge(m_mm, t.g * 2 + c + 1)
                    for jj in range(2):
                        for s in range(2):
                            j = 2 * c + jj
                            ins = act.activation(scaled[:, b, s, j, :], p_m[c][:, jj, s, 0:WS], ACT.Identity, bias=0.0,
                                                 scale=rec[:, bass.ds(t.g * G + j, 1), D_A2 + s])
                    ins.then_inc(m_scaled, 1)
                if t.ahead(1).exists():
                    second_half(t.ahead(1))
                if t.ahead(2).exists():
                    act.wait_ge(turned, t.g + 1)
                    rows(t.ahead(2))
                act.wait_ge(score_turned, t.g + 1)
                act.copy(V["score_t"][0:NHEAD, bass.ds(t.g * GE, GE)], p_a[0:NHEAD, 0:GE]).then_inc(score_kept, 1)

            rows(first[0])
            second_half(first[0])
            rows(first[1])
            groups(act, body)

        @block.tensor
        def _(pe):
            pe.wait_ge(w_in, 48)
            pe.transpose(p_a[0:DM, 0:NHEAD], attn[:, :], K["ident"][0:NHEAD, 0:NHEAD]).then_inc(attn_turned, 1)
            for k in range(DC):
                for s in range(2):
                    pe.transpose(p_t[k][:, s * WS:s * WS + DM], w[:, s, k * P:(k + 1) * P], K["ident"][0:DM, 0:DM])
            pe.wait_ge(attn_ready, 1)
            for k in range(DC):
                for s in range(2):
                    mm = pe.matmul(p_t[k][:, s * WS + DM:(s + 1) * WS], w[:, s, k * P:(k + 1) * P], attn_t[:, :],
                                   start=True, stop=True)
            mm.then_inc(w_turned, 1)
            pe.wait_ge(w_ready, 1)
            pe.sem_inc(h_t_ready, 2)
            pe.sem_inc(m_scaled, 2)
            pe.sem_inc(score_kept, 1)

            def turn(t):
                b = t.slot(2)
                pe.wait_ge(h_ready, t.g + 1)
                pe.wait_ge(h_t_ready, t.g * 2 + 2)
                for c in range(DC):
                    for j in range(G):
                        mm = pe.transpose(p_t[c][:, j * TE:(j + 1) * TE], h[:, b, j, c * P:(c + 1) * P],
                                          K["ident"][0:TE, 0:TE])
                mm.then_inc(turned, 1)

            def body(t):
                b = t.slot(2)
                pe.wait_ge(h_t_ready, t.g * 2 + 4)
                for c in range(2):
                    pe.wait_ge(m_scaled, t.g * 2 + c + 1)
                    for jj in range(2):
                        j = 2 * c + jj
                        for k in range(DC):
                            mm = pe.matmul(p_m[c][:, jj, :, 0:WS], h_t[:, b, k, j * TE:(j + 1) * TE],
                                           w_t[:, k, :, :], start=(k == 0), stop=(k == DC - 1))
                    mm.then_inc(m_mm, 1)
                if t.ahead(1).exists():
                    turn(t.ahead(1))
                pe.wait_ge(score_ready, t.g + 1)
                pe.wait_ge(score_kept, t.g + 1)
                for j in range(G):
                    mm = pe.transpose(p_a[0:NHEAD, j * TE:(j + 1) * TE], score_l[:, b, j, :],
                                      K["ident"][0:TE, 0:TE])
                mm.then_inc(score_turned, 1)

            turn(first[0])
            groups(pe, body)


def attention_sums(nc, K, V, name, NHEAD, per_head, guard, out):
    N = out.shape[0]
    NG = V["edges"] // GE
    DH = D // NHEAD
    with ExitStack() as ctx:
        def sb(what, shape, dt=F32):
            return ctx.enter_context(nc.sbuf_tensor(f"{name}_{what}", shape, dt))

        def pb(what, shape, dt=F32):
            return ctx.enter_context(nc.psum_tensor(f"{name}_{what}", shape, dt))

        sem = signals(nc, K, name)
        rec = V["rec"]
        idx = sb("idx", [TE, 2, G], I32)
        upto = sb("upto", [NHEAD, V["edges"]]) if per_head else None
        top = sb("top", [NHEAD, 2])
        ex_t = sb("ex_t", [NHEAD, 2, GE])
        ex = sb("ex", [TE, 2, G, NHEAD])
        m = sb("m", [TE, 2, G, D])
        run = sb("run", [P, 2, DC, GE])
        den_t = sb("den_t", [NHEAD, 2, GE])
        den = sb("den", [TE, 2, G, NHEAD])
        rows = sb("rows", [TE, 2, G, D])
        p_e = pb("p_e", [TE, 512])
        p_d = pb("p_d", [TE, 512])
        p_t = [pb(f"p_t{c}", [P, 512]) for c in range(DC)]
        p_r = [pb(f"p_r{c}", [TE, 2, D]) for c in range(2)]

        put = [sem(f"put{b}") for b in range(2)]
        step = sem("step")
        shifted = sem("shifted")
        ex_t_ready = sem("ex_t_ready")
        pe_passed = sem("pe_passed")
        ex_turned = sem("ex_turned")
        ex_ready = sem("ex_ready")
        m_ready = sem("m_ready")
        turned = sem("turned")
        run_ready = sem("run_ready")
        den_ready = sem("den_ready")
        den_turned = sem("den_turned")
        den_read = sem("den_read")
        den_done = sem("den_done")
        rows_turned = sem("rows_turned")
        rows_scaled = sem("rows_scaled")
        passed = sem("passed")
        block = ctx.enter_context(nc.Block())

        def groups(eng, body):
            over_groups(eng, NG, 2, 2, body)

        first = [Step(0, b, 2, NG) for b in range(2)]

        @block.gpsimd
        def _(pool):
            for b in range(2):
                open_slot(pool, K, put[b], 16 * G)

            def body(t):
                b = t.slot(2)
                pool.wait_ge(rows_scaled, t.g * 2 + 4)
                pool.sem_inc(passed, 1)
                for j in range(G):
                    pool.indirect_dma_start(out[:, :], IOA(idx[:, b, j:j + 1], 0), rows[:, b, j, :], None,
                                            bounds_check=N - 1, oob_is_err=False,
                                            compute_op=ALU.add).then_inc(put[b], 16)

            groups(pool, body)
            for b in range(2):
                pool.wait_ge(put[b], 16 * G * (NG // 2 + 1))

        @block.vector
        def _(dve):
            dve.memset(den_t[:, 1, GE - 1:GE], 0.0).then_inc(den_ready, 1)
            dve.memset(run[:, 1, :, GE - 1], 0.0).then_inc(run_ready, 2)

            if per_head:
                above_run(dve, V, upto, step).then_inc(shifted, 1)
            else:
                top_of_all(dve, V, NHEAD, top, step).then_inc(shifted, 1)

            def weigh(t):
                b = t.slot(2)
                dve.wait_ge(ex_ready, t.g + 2)
                source = V["proj"][:, bass.ds(t.g * G, G), 0:D if per_head else DH]
                source = source.rearrange("p t (h d) -> p t h d", h=NHEAD) if per_head else \
                    source.unsqueeze(2).to_broadcast([TE, G, NHEAD, DH])
                dve.tensor_tensor(m[:, b, :, :].rearrange("p t (h d) -> p t h d", h=NHEAD), source,
                                  ex[:, b, :, :].unsqueeze(3).to_broadcast([TE, G, NHEAD, DH]),
                                  ALU.mult).then_inc(m_ready, 1)

            def body(t):
                b = t.slot(2)
                same = bass.ds(t.g * GE, GE)
                dve.wait_ge(ex_t_ready, t.g + 1)
                dve.wait_ge(den_ready, t.g + 1)
                dve.tensor_tensor_scan(den_t[:, b, :], K["same"][0:NHEAD, same], ex_t[:, b, :],
                                       den_t[:, 1 - b, GE - 1:GE], ALU.mult, ALU.add).then_inc(den_ready, 1)
                dve.wait_ge(turned, t.g + 1)
                dve.wait_ge(run_ready, t.g * 2 + 2)
                for c in range(DC):
                    dve.tensor_tensor_scan(run[:, b, c, :], K["same"][:, same], p_t[c][:, 0:GE],
                                           run[:, 1 - b, c, GE - 1:GE], ALU.mult, ALU.add).then_inc(run_ready, 1)
                if t.ahead(1).exists():
                    weigh(t.ahead(1))
                dve.wait_ge(put[b], t.round(2) * (16 * G))
                dve.tensor_copy(idx[:, b, :], rec[:, bass.ds(t.g * G, G), D_PUT])
                dve.wait_ge(den_turned, t.g + 1)
                dve.tensor_scalar(den[:, b, :, :].rearrange("p t h -> p (t h)"), p_d[:, 0:G * NHEAD], guard[1], None,
                                  guard[0]).then_inc(den_read, 1)
                dve.wait_ge(den_read, t.g + 2)
                dve.reciprocal(den[:, b, :, :], den[:, b, :, :]).then_inc(den_done, 1)
                dve.wait_ge(den_done, t.g + 1)
                for c in range(2):
                    dve.wait_ge(rows_turned, t.g * 2 + c + 1)
                    dve.tensor_tensor(rows[:, b, 2 * c:2 * c + 2, :].rearrange("p t (h d) -> p t h d", h=NHEAD),
                                      p_r[c][:, :, :].rearrange("p t (h d) -> p t h d", h=NHEAD),
                                      den[:, b, 2 * c:2 * c + 2, :].unsqueeze(3).to_broadcast([TE, 2, NHEAD, DH]),
                                      ALU.mult).then_inc(rows_scaled, 1)

            weigh(first[0])
            groups(dve, body)

        @block.scalar
        def _(act):
            def weights(t):
                b = t.slot(2)
                act.activation(ex_t[:, b, :], V["score_t"][0:NHEAD, bass.ds(t.g * GE, GE)], ACT.Exp,
                               bias=0.0 if per_head else top[:, 1:2], scale=1.0).then_inc(ex_t_ready, 1)
                act.wait_ge(ex_turned, t.g + 1)
                act.copy(ex[:, b, :, :].rearrange("p t h -> p (t h)"), p_e[:, 0:G * NHEAD]).then_inc(ex_ready, 1)

            def body(t):
                if t.ahead(2).exists():
                    act.wait_ge(den_ready, t.g + 2)
                    act.wait_ge(m_ready, t.g + 1)
                    weights(t.ahead(2))

            act.wait_ge(shifted, 1)
            weights(first[0])
            weights(first[1])
            groups(act, body)

        @block.tensor
        def _(pe):
            pe.sem_inc(ex_ready, 1)
            pe.sem_inc(den_read, 1)
            pe.sem_inc(rows_scaled, 2)

            def turn_weights(t):
                b = t.slot(2)
                pe.wait_ge(ex_t_ready, t.g + 1)
                pe.wait_ge(ex_ready, t.g + 1)
                pe.sem_inc(pe_passed, 1)
                for j in range(G):
                    mm = pe.transpose(p_e[:, j * NHEAD:(j + 1) * NHEAD], ex_t[:, b, j * TE:(j + 1) * TE],
                                      K["ident"][0:NHEAD, 0:NHEAD])
                mm.then_inc(ex_turned, 1)

            def turn(t):
                b = t.slot(2)
                pe.wait_ge(m_ready, t.g + 1)
                pe.wait_ge(run_ready, t.g * 2 + 2)
                for c in range(DC):
                    for j in range(G):
                        mm = pe.transpose(p_t[c][:, j * TE:(j + 1) * TE], m[:, b, j, c * P:(c + 1) * P],
                                          K["ident"][0:TE, 0:TE])
                mm.then_inc(turned, 1)

            def body(t):
                b = t.slot(2)
                pe.wait_ge(den_ready, t.g + 2)
                pe.wait_ge(den_read, t.g + 1)
                pe.sem_inc(pe_passed, 1)
                for j in range(G):
                    mm = pe.transpose(p_d[:, j * NHEAD:(j + 1) * NHEAD], den_t[:, b, j * TE:(j + 1) * TE],
                                      K["ident"][0:NHEAD, 0:NHEAD])
                mm.then_inc(den_turned, 1)
                if t.ahead(2).exists():
                    turn_weights(t.ahead(2))
                pe.wait_ge(run_ready, t.g * 2 + 4)
                for c in range(2):
                    pe.wait_ge(rows_scaled, t.g * 2 + c + 1)
                    for jj in range(2):
                        j = 2 * c + jj
                        for k in range(DC):
                            mm = pe.transpose(p_r[c][:, jj, k * P:(k + 1) * P], run[:, b, k, j * TE:(j + 1) * TE],
                                              K["ident"][:, :])
                    mm.then_inc(rows_turned, 1)
                if t.ahead(1).exists():
                    turn(t.ahead(1))

            turn_weights(first[0])
            turn_weights(first[1])
            turn(first[0])
            groups(pe, body)


def gnn(nc, A, out):
    N = A["x"].shape[0]
    E = A["src"].shape[0]
    NT = E // TE
    NH = -(-N // LO) + 1
    table = nc.dram_tensor("node_table", [NH * LO, 4], F32).ap()
    agg0 = nc.dram_tensor("agg0", [N, D], F32).ap()
    rec_d = nc.dram_tensor("rec_by_dst", [E, RD], F32).ap()
    rec_c = nc.dram_tensor("rec_by_node", [2 * E, RC], F32).ap()
    x1 = nc.dram_tensor("x1_by_node", [N, D], F32).ap()
    msg = nc.dram_tensor("messages0", [E, D], F32).ap()
    with ExitStack() as ctx:
        def sb(name, shape, dt=F32):
            return ctx.enter_context(nc.sbuf_tensor(name, shape, dt))

        K = {
            "signals": [], "token": sb("token", [1, 32, 4]), "token_n": -1,
            "ident": sb("ident", [P, P]), "iota_p": sb("iota_p", [P, 1]), "eps": sb("eps_col", [P, 1]),
            "dst_col": sb("dst_col", [TE, NT + 2 * G], I32), "src_col": sb("src_col", [TE, NT + 2 * G], I32),
            "same": sb("same_dst", [P, E], BF16),
            "ord": sb("ord", [TE, NT, 2]),
        }
        constants(nc, K)
        rank_edges(nc, K, A["dst"], A["src"], table, agg0)
        with ExitStack() as ctx_r:
            R = Records(nc, ctx_r, signals(nc, K, "rc"), K, A, table, rec_d, rec_c)
            edge_messages(nc, K, A, R, msg)
            aggregate_messages(nc, K, msg, rec_d, agg0)
            node_network(nc, K, A, R, agg0, x1, out)
        reuse_signals(nc, K)
        H2, H3 = A["L2_gnn_a_src"].shape[0], A["L3_gnn_attn_forward"].shape[1]
        V = {"edges": E, "rec": sb("rec_dst", [TE, NT, RD])}
        relation_layer(nc, K, A, V, rec_c, rec_d, x1, out)
        V["proj"] = sb("proj", [TE, NT, D + H2])
        V["score_t"] = sb("score_t", [max(H2, H3), E])
        V["fence"] = sb("fence", [H2, E + 1])
        attention_scores(nc, K, A, V, out)
        attention_sums(nc, K, V, "a2", H2, True, (ALU.max, 1e-10), out)
        message_scores(nc, K, A, V, out)
        attention_sums(nc, K, V, "a3", H3, False, (ALU.add, 1e-10), out)


_INS = ['x', 'src', 'dst', 'edge_attr_2', 'edge_attr_256', 'edge_attr_3', 'edge_type_11',
        'L0_gnn_We1', 'L0_gnn_be1', 'L0_gnn_We2', 'L0_gnn_be2', 'L0_gnn_Wn1', 'L0_gnn_bn1', 'L0_gnn_Wn2',
        'L0_gnn_bn2', 'L0_gnn_eps', 'L1_gnn_weight', 'L1_gnn_bias', 'L1_gnn_alpha', 'L2_gnn_W', 'L2_gnn_a_src',
        'L2_gnn_a_dst', 'L2_gnn_edge_W', 'L2_gnn_edge_b', 'L2_gnn_bias', 'L3_gnn_W_forward', 'L3_gnn_W_reverse',
        'L3_gnn_attn_forward']


def kernel(**inputs):
    import numpy as _np
    import concourse.bacc as _bacc
    from concourse import mybir as _mybir
    from concourse.bass_utils import run_bass_kernel_spmd as _run

    nc = _bacc.Bacc("TRN2", target_bir_lowering=False, num_devices=1)
    arrays, args = {}, {}
    for name in _INS:
        a = _np.ascontiguousarray(inputs[name])
        arrays[f"in_{name}"] = a
        args[name] = nc.dram_tensor(f"in_{name}", a.shape, _mybir.dt.from_np(a.dtype), kind="ExternalInput").ap()
    out = nc.dram_tensor("out_x", inputs["x"].shape, _mybir.dt.float32, kind="ExternalOutput").ap()
    gnn(nc, args, out)
    r = _run(nc, [arrays], core_ids=[0])
    return r.results[0]["out_x"]
```
